# Optimizing a Trainium2 kernel written in Bass

```python
import numpy as np
import jax
import jax.numpy as jnp

def _softmax(x, axis=-1):
    return jax.nn.softmax(x, axis=axis)

def _gelu(x):
    return jax.nn.gelu(x, approximate=True)

def _silu(x):
    return jax.nn.silu(x)

def _sigmoid(x):
    return jax.nn.sigmoid(x)

def _layernorm(x, axis=-1, eps=1e-05):
    m = jnp.mean(x, axis=axis, keepdims=True)
    v = jnp.var(x, axis=axis, keepdims=True)
    return (x - m) / jnp.sqrt(v + eps)

def _scatter_add(tgt, idx, src, axis=0):
    return tgt.at[idx].add(src)

def _segment_sum(src, seg, n):
    return jax.ops.segment_sum(src, seg, n)
kernel_name = 'mk_audio_tower_d1_tok_audfeat768_r4_532d23'

def setup_inputs(seed: int=0):
    np.random.seed(seed)
    _w = jnp.asarray

    def _rec_inputs():
        import jax
        import jax.numpy as jnp
        _rk = jax.random.key(seed)
        x = 7.22013e-05 + 1.00017 * jax.random.normal(jax.random.fold_in(_rk, 1), (64, 1, 16384), jnp.float32)
        return x
    x = _rec_inputs()

    def _L0_tok_setup():
        import jax, jax.numpy as jnp
        import numpy as np
        INPUT_SIZE = 16384
        PATCH = 128
        HOP = 64
        NUM_PATCHES = (INPUT_SIZE - PATCH) // HOP + 1

        def _unfold_patches(x):
            B, C, L = x.shape
            idx = jnp.arange(NUM_PATCHES)[:, None] * HOP + jnp.arange(PATCH)[None, :]
            patches = x[:, :, idx]
            patches = jnp.transpose(patches, (0, 2, 1, 3))
            return patches.reshape(B, NUM_PATCHES, C * PATCH)
        key = jax.random.key(seed)
        k1, k2, k3, k4 = jax.random.split(key, 4)
        x = jax.random.normal(k1, (128, 1, INPUT_SIZE), dtype=jnp.float32)
        W1 = jax.random.normal(k2, (192, PATCH), dtype=jnp.float32) * (1.0 / np.sqrt(PATCH))
        W2 = jax.random.normal(k3, (192, 192), dtype=jnp.float32) * (1.0 / np.sqrt(192))
        b2 = jax.random.normal(k4, (192,), dtype=jnp.float32) * 0.01
        return {'x': x, 'W1': W1, 'W2': W2, 'b2': b2}
    _L0_tok_all = _L0_tok_setup()
    _L0_tok_in = {k: v for k, v in _L0_tok_all.items() if k in ('W1', 'W2', 'b2')}
    del _L0_tok_all

    def _L0_attn_setup():
        import jax, jax.numpy as jnp
        import numpy as np
        B, N, M, D = (128, 64, 8, 192)
        key = jax.random.key(seed)
        ks = jax.random.split(key, 6)
        w_scale = D ** (-0.5)
        return {'x': jax.random.normal(ks[0], (B, N, D), dtype=jnp.float32), 'memory': jax.random.normal(ks[1], (M, D), dtype=jnp.float32) * 0.02, 'Wq': jax.random.normal(ks[2], (D, D), dtype=jnp.float32) * w_scale, 'bq': jnp.zeros((D,), dtype=jnp.float32), 'Wk': jax.random.normal(ks[3], (D, D), dtype=jnp.float32) * w_scale, 'bk': jnp.zeros((D,), dtype=jnp.float32), 'Wv': jax.random.normal(ks[4], (D, D), dtype=jnp.float32) * w_scale, 'bv': jnp.zeros((D,), dtype=jnp.float32), 'Wo': jax.random.normal(ks[5], (D, D), dtype=jnp.float32) * w_scale, 'bo': jnp.zeros((D,), dtype=jnp.float32)}
    _L0_attn_all = _L0_attn_setup()
    _L0_attn_in = {k: v for k, v in _L0_attn_all.items() if k in ('memory', 'Wq', 'bq', 'Wk', 'bk', 'Wv', 'bv', 'Wo', 'bo')}
    del _L0_attn_all

    def _L0_ffn_setup():
        import jax, jax.numpy as jnp
        import numpy as np
        NUM_EXPERTS = 8
        TOP_K = 2
        CAPACITY_FACTOR = 1.25
        MAX_GROUP_SIZE = 1024
        MIN_EXPERT_CAPACITY = 4

        def _moe_forward(x, w_router, wi, wo):
            B, T, D = x.shape
            E = NUM_EXPERTS
            num_tokens = B * T
            G = max(num_tokens // MAX_GROUP_SIZE, E)
            while num_tokens % G != 0 or G % E != 0:
                G += 1
            S = num_tokens // G
            C = max(int(TOP_K * CAPACITY_FACTOR * S / E), MIN_EXPERT_CAPACITY)
            xg = x.reshape(G, S, D)
            logits = jnp.einsum('gsd,de->gse', xg.astype(jnp.float32), w_router.astype(jnp.float32))
            probs = jax.nn.softmax(logits, axis=-1)
            gate, idx = jax.lax.top_k(probs, TOP_K)
            idx_kf = jnp.swapaxes(idx, 1, 2).reshape(G, TOP_K * S)
            mask = jax.nn.one_hot(idx_kf, E, dtype=jnp.int32)
            prio = jnp.cumsum(mask, axis=1) * mask - 1
            prio = jnp.swapaxes(prio.reshape(G, TOP_K, S, E), 1, 2)
            prio_se = prio.max(axis=2)
            gate_se = jnp.einsum('gsk,gske->gse', gate, jax.nn.one_hot(idx, E, dtype=gate.dtype))
            dispatch = jax.nn.one_hot(prio_se, C, dtype=x.dtype)
            combine = dispatch * gate_se[..., None].astype(x.dtype)
            expert_in = jnp.einsum('gsec,gsd->egcd', dispatch, xg)
            h = jax.nn.relu(jnp.einsum('egcd,edf->egcf', expert_in, wi))
            expert_out = jnp.einsum('egcf,efd->egcd', h, wo)
            out = jnp.einsum('gsec,egcd->gsd', combine, expert_out)
            return out.reshape(B, T, D)
        key = jax.random.key(seed)
        k1, k2, k3, k4 = jax.random.split(key, 4)
        B, T, D, F = (8, 256, 192, 768)
        x = jax.random.normal(k1, (B, T, D), jnp.float32)
        w_router = jax.random.normal(k2, (D, NUM_EXPERTS), jnp.float32) * D ** (-0.5)
        wi = jax.random.normal(k3, (NUM_EXPERTS, D, F), jnp.float32) * D ** (-0.5)
        wo = jax.random.normal(k4, (NUM_EXPERTS, F, D), jnp.float32) * F ** (-0.5)
        return {'x': x, 'w_router': w_router, 'wi': wi, 'wo': wo}
    _L0_ffn_all = _L0_ffn_setup()
    _L0_ffn_in = {k: v for k, v in _L0_ffn_all.items() if k in ('w_router', 'wi', 'wo')}
    del _L0_ffn_all
    return {'x': x, 'L0_tok_W1': _L0_tok_in['W1'], 'L0_tok_W2': _L0_tok_in['W2'], 'L0_tok_b2': _L0_tok_in['b2'], 'L0_attn_memory': _L0_attn_in['memory'], 'L0_attn_Wq': _L0_attn_in['Wq'], 'L0_attn_bq': _L0_attn_in['bq'], 'L0_attn_Wk': _L0_attn_in['Wk'], 'L0_attn_bk': _L0_attn_in['bk'], 'L0_attn_Wv': _L0_attn_in['Wv'], 'L0_attn_bv': _L0_attn_in['bv'], 'L0_attn_Wo': _L0_attn_in['Wo'], 'L0_attn_bo': _L0_attn_in['bo'], 'L0_ffn_w_router': _L0_ffn_in['w_router'], 'L0_ffn_wi': _L0_ffn_in['wi'], 'L0_ffn_wo': _L0_ffn_in['wo']}

def reference(x, L0_tok_W1, L0_tok_W2, L0_tok_b2, L0_attn_memory, L0_attn_Wq, L0_attn_bq, L0_attn_Wk, L0_attn_bk, L0_attn_Wv, L0_attn_bv, L0_attn_Wo, L0_attn_bo, L0_ffn_w_router, L0_ffn_wi, L0_ffn_wo):
    import jax
    import jax.numpy as jnp

    def _L0_tok_ref(x, W1, W2, b2):
        import jax, jax.numpy as jnp
        import numpy as np
        INPUT_SIZE = 16384
        PATCH = 128
        HOP = 64
        NUM_PATCHES = (INPUT_SIZE - PATCH) // HOP + 1

        def _unfold_patches(x):
            B, C, L = x.shape
            idx = jnp.arange(NUM_PATCHES)[:, None] * HOP + jnp.arange(PATCH)[None, :]
            patches = x[:, :, idx]
            patches = jnp.transpose(patches, (0, 2, 1, 3))
            return patches.reshape(B, NUM_PATCHES, C * PATCH)
        patches = _unfold_patches(x)
        h = jnp.einsum('bpd,kd->bpk', patches, W1)
        out = jnp.einsum('bpk,ek->bpe', h, W2) + b2
        return out

    def _L0_attn_ref(x, memory, Wq, bq, Wk, bk, Wv, bv, Wo, bo):
        import jax, jax.numpy as jnp
        import numpy as np
        B, N, M, D = (128, 64, 8, 192)
        b, n, d = x.shape
        m = memory.shape[0]
        t = n + m
        scaling = d ** (-0.5)
        cat = jnp.concatenate([x, jnp.broadcast_to(memory[None], (b, m, d))], axis=1)
        q = cat @ Wq + bq
        k = cat @ Wk + bk
        v = cat @ Wv + bv
        att = jax.nn.softmax(jnp.einsum('bqd,bkd->bqk', q, k) * scaling, axis=-1)
        row_mask = (jnp.arange(t) < n).astype(att.dtype)[None, :, None]
        att = att * row_mask
        head_out = jnp.einsum('bqk,bkd->bqd', att, v)
        attended = head_out @ Wo + bo
        return attended[:, :n, :]

    def _L0_ffn_ref(x, w_router, wi, wo):
        import jax, jax.numpy as jnp
        import numpy as np
        NUM_EXPERTS = 8
        TOP_K = 2
        CAPACITY_FACTOR = 1.25
        MAX_GROUP_SIZE = 1024
        MIN_EXPERT_CAPACITY = 4

        def _moe_forward(x, w_router, wi, wo):
            B, T, D = x.shape
            E = NUM_EXPERTS
            num_tokens = B * T
            G = max(num_tokens // MAX_GROUP_SIZE, E)
            while num_tokens % G != 0 or G % E != 0:
                G += 1
            S = num_tokens // G
            C = max(int(TOP_K * CAPACITY_FACTOR * S / E), MIN_EXPERT_CAPACITY)
            xg = x.reshape(G, S, D)
            logits = jnp.einsum('gsd,de->gse', xg.astype(jnp.float32), w_router.astype(jnp.float32))
            probs = jax.nn.softmax(logits, axis=-1)
            gate, idx = jax.lax.top_k(probs, TOP_K)
            idx_kf = jnp.swapaxes(idx, 1, 2).reshape(G, TOP_K * S)
            mask = jax.nn.one_hot(idx_kf, E, dtype=jnp.int32)
            prio = jnp.cumsum(mask, axis=1) * mask - 1
            prio = jnp.swapaxes(prio.reshape(G, TOP_K, S, E), 1, 2)
            prio_se = prio.max(axis=2)
            gate_se = jnp.einsum('gsk,gske->gse', gate, jax.nn.one_hot(idx, E, dtype=gate.dtype))
            dispatch = jax.nn.one_hot(prio_se, C, dtype=x.dtype)
            combine = dispatch * gate_se[..., None].astype(x.dtype)
            expert_in = jnp.einsum('gsec,gsd->egcd', dispatch, xg)
            h = jax.nn.relu(jnp.einsum('egcd,edf->egcf', expert_in, wi))
            expert_out = jnp.einsum('egcf,efd->egcd', h, wo)
            out = jnp.einsum('gsec,egcd->gsd', combine, expert_out)
            return out.reshape(B, T, D)
        return _moe_forward(x, w_router, wi, wo)
    h = _L0_tok_ref(x, L0_tok_W1, L0_tok_W2, L0_tok_b2)
    h = h + _L0_attn_ref(_layernorm(h, axis=-1), L0_attn_memory, L0_attn_Wq, L0_attn_bq, L0_attn_Wk, L0_attn_bk, L0_attn_Wv, L0_attn_bv, L0_attn_Wo, L0_attn_bo)
    h = h + _L0_ffn_ref(_layernorm(h, axis=-1), L0_ffn_w_router, L0_ffn_wi, L0_ffn_wo)
    return h

_drawn_inputs = setup_inputs


def setup_inputs(seed=0):
    import zlib

    import numpy as np

    out = dict(_drawn_inputs(seed))
    spreads = {'L0_attn_bq': (0.0, 0.1),
     'L0_attn_bk': (0.0, 2.0),
     'L0_attn_bv': (0.0, 0.1),
     'L0_attn_bo': (0.0, 0.1)}
    factors = {'L0_attn_memory': 64.0}
    for name, (base, spread) in spreads.items():
        noise = np.random.default_rng([zlib.crc32(name.encode()), seed]).standard_normal(out[name].shape)
        drawn = base * np.exp(spread * noise) if base else spread * noise
        out[name] = jnp.asarray(drawn.astype(out[name].dtype))
    for name, factor in factors.items():
        out[name] = (out[name] * factor).astype(out[name].dtype)
    return out
```

```python
from contextlib import ExitStack

import concourse.bass as bass
from concourse import mybir

F32 = mybir.dt.float32
F32R = mybir.dt.float32r
BF16 = mybir.dt.bfloat16
I32 = mybir.dt.int32
U32 = mybir.dt.uint32
ALU = mybir.AluOpType
ACT = mybir.ActivationFunctionType
AX = mybir.AxisListType

B, L = 64, 16384
PATCH, HOP = 128, 64
NP = (L - PATCH) // HOP + 1
D = 192
DH = D // 2
MEM = 8
NK = NP + MEM
KW = NK + 1
E, F = 8, 768
G = 16
SPG = B // G
S = SPG * NP
C = int(2 * 1.25 * S / E)
TPG = 2 * SPG
J = 3
CP = C // J
CPP = 112
SLOTS = CPP * J
ROWS = E * SLOTS
FT = F // 128
SCALE = float(D) ** -0.5
EPS = 1e-5
FAR = float(1 << 20)
LAGS = 4


def audio_tower(nc, x, W1, W2, b2, memory, Wq, bq, Wk, bk, Wv, bv, Wo, bo, Wr, wi, wo, out):
    h2_dram = nc.dram_tensor("h2_scratch", (B, 2, 128, D), F32, kind="Internal").ap()
    xs_dram = nc.dram_tensor("slots_in", (2 * ROWS, D), F32, kind="Internal").ap()
    ys_dram = nc.dram_tensor("slots_out", (2 * ROWS, D), F32, kind="Internal").ap()
    with ExitStack() as both:
        routes = both.enter_context(nc.sbuf_tensor("routes", [128, B * 20], F32))
        ident = both.enter_context(nc.sbuf_tensor("ident", [128, 128], F32))
        with ExitStack() as ctx:
            attention(nc, ctx, x, W1, W2, b2, memory, Wq, bq, Wk, bk, Wv, bv, Wo, bo, Wr,
                      routes, ident, h2_dram, xs_dram, ys_dram)
        with ExitStack() as ctx:
            experts(nc, ctx, wi, wo, routes, ident, h2_dram, xs_dram, ys_dram, out)


def wait(eng, sem, value):
    if isinstance(value, int) and value <= 0:
        return
    eng.wait_ge(sem, value)


def settle(eng, passed):
    eng.sem_inc(passed, 1)


def attention(nc, ctx, x, W1, W2, b2, memory, Wq, bq, Wk, bk, Wv, bv, Wo, bo, Wr,
              routes, ident, h2_dram, xs_dram, ys_dram):
    def sb(name, shape, dt=F32):
        return ctx.enter_context(nc.sbuf_tensor(name, shape, dt))

    def psum(name, shape):
        return ctx.enter_context(nc.psum_tensor(name, shape, F32))

    def sem(name):
        return ctx.enter_context(nc.semaphore(name))

    w1_sb = sb("w1_sb", [DH, 2, PATCH])
    w2_sb = sb("w2_sb", [DH, 2, D])
    wqkv_sb = [sb(f"w{n}_sb", [DH, 2, D]) for n in "qkv"]
    wo_sb = sb("wo_sb", [DH, 2, D])
    w2T = sb("w2T", [DH, 2, D])
    wqkvT = [sb(f"w{n}T", [DH, 2, D + 1]) for n in "qkv"]
    bias_sb = sb("bias_sb", [DH, 3, 2])
    bo_sb = sb("bo_sb", [128, D])
    b2_sb = sb("b2_sb", [128, D])
    wr_sb = sb("wr_sb", [DH, 2, E])
    memT = sb("memT", [128, 2, MEM])
    zero_sb = sb("zero_sb", [128, 2 * D])
    vo_sb = sb("vo_sb", [128, 2, D])
    w21 = [sb(f"w21_{p}", [128, D], F32R) for p in ("hi", "lo")]
    qk = [sb(f"qk_{p}", [128, 2, D + 1], F32R) for p in ("hi", "lo")]
    vo = [sb(f"vo_{p}", [128, 2, D], F32R) for p in ("hi", "lo")]
    vmem = [sb(f"vmem_{p}", [128, D], F32R) for p in ("hi", "lo")]
    half = sb("half", [128, 2])
    patches = sb("patches", [128, 2, 2, PATCH])
    patchT = [sb(f"patchT_{p}", [128, 256], F32R) for p in ("hi", "lo")]
    h = sb("h", [128, 4, 2, D])
    c = sb("c", [128, 2, D])
    cT = [sb(f"cT_{p}", [128, 2, 2, KW], F32R) for p in ("hi", "lo")]
    qT = [sb(f"qT_{p}", [128, 2, 2, 256], F32R) for p in ("hi", "lo")]
    v = [sb(f"v_{p}", [128, 2, 2, D], F32R) for p in ("hi", "lo")]
    probs = sb("probs", [128, 2, 384])
    probsT = [sb(f"probsT_{p}", [128, 3, 256], F32R) for p in ("hi", "lo")]
    h2 = sb("h2", [128, 2, 2, D])
    c2 = sb("c2", [128, 2, D])
    c2T = sb("c2T", [DH, 2, 256])
    stats = sb("stats", [128, 2, 2, 6])
    mv = sb("mv", [128, 2, 2, 2])
    vare = sb("vare", [128, 2, 2])
    rstd = sb("rstd", [128, 2, 2])
    peak = sb("peak", [128, 2])
    npeak = sb("npeak", [128, 2])
    total = sb("total", [128, 2, 2])
    rtotal = sb("rtotal", [128, 2])
    ps_h = psum("ps_h", [128, 512])
    ps_q = psum("ps_q", [128, 2, 256])
    ps_c = psum("ps_c", [128, 2, 256])
    ps_v = psum("ps_v", [128, 512])
    ps_s = psum("ps_s", [128, 2, 512])
    ps_p = psum("ps_p", [128, 4, 256])
    ps_x = ps_h[:, 0:256]
    ps_lg = ps_c[:, 0, 0:2 * E]
    ps_o = ps_p[:].rearrange("p k n -> p (k n)")[:, 0:2 * D].rearrange("p (k d) -> p k d", k=2)
    loads = sem("setup_loads")
    zeroed = sem("slots_zeroed")
    pool_set = sem("pool_set")
    weights_tr = sem("weights_transposed")
    weights_cp = sem("weights_copied")
    folded = sem("weights_folded")
    split_hi = sem("folded_split_hi")
    split_lo = sem("folded_split_lo")
    mem_set = sem("memory_keys_set")
    vmem_mm = sem("memory_values_made")
    x_loaded = [sem(f"x_loaded_{i}") for i in range(2)]
    patch_tr = sem("patch_transposed")
    patch_hi = sem("patchT_hi_ready")
    patch_lo = sem("patchT_lo_ready")
    h_mm = sem("tokens_made")
    h_ready = sem("tokens_ready")
    st1 = sem("stats1_ready")
    mv1 = sem("mean_var1_ready")
    ve1 = sem("var_eps1_ready")
    rs1 = sem("rstd1_ready")
    c_ready = sem("c_ready")
    c_tr = sem("c_transposed")
    cT_hi = sem("cT_hi_ready")
    cT_lo = sem("cT_lo_ready")
    q_mm = sem("q_made")
    q_hi = sem("q_hi_ready")
    q_lo = sem("q_lo_ready")
    v_mm = sem("v_made")
    v_hi = sem("v_hi_ready")
    v_lo = sem("v_lo_ready")
    s_mm = sem("scores_made")
    peak_ready = sem("peak_ready")
    npeak_ready = sem("npeak_ready")
    exp_done = sem("exp_done")
    p_tr = sem("probs_transposed")
    pT_hi = sem("probsT_hi_ready")
    pT_lo = sem("probsT_lo_ready")
    pv_mm = sem("attended_made")
    rt_ready = sem("rtotal_ready")
    h2_ready = sem("h2_ready")
    h2_stored = [sem(f"h2_stored_{i}") for i in range(2)]
    st2 = sem("stats2_ready")
    mv2 = sem("mean_var2_ready")
    ve2 = sem("var_eps2_ready")
    rs2 = sem("rstd2_ready")
    c2_ready = sem("c2_ready")
    c2_tr = sem("c2_transposed")
    c2T_ready = sem("c2T_ready")
    lg_mm = sem("logits_made")
    lg_kept = sem("logits_kept")
    dve_passed = sem("vector_waits_passed")
    sp_passed = sem("sync_waits_passed")
    pool_passed = sem("gpsimd_waits_passed")
    NLOADS = 15
    block = ctx.enter_context(nc.Block())

    def rows(w):
        return w.rearrange("(t p) d -> p t d", t=2)

    def all_iterations(eng, body):
        for j in range(4):
            body(0, j, lambda lag: j >= lag)
        for j in range(4):
            body(1, j, lambda lag: True)
        with eng.Fori(2, B // 4) as g:
            for j in range(4):
                body(g, j, lambda lag: True)
        for j in range(LAGS):
            body(B // 4, j, lambda lag: j < lag)

    def turns(g, j, lag):
        return g * 2 + ((j - lag) // 2 + 1)

    @block.sync
    def _(sp):
        sp.dma_start(w1_sb[:], rows(W1)).then_inc(loads, 16)
        sp.dma_start(w2_sb[:], rows(W2)).then_inc(loads, 16)
        for w, d in zip(wqkv_sb, (Wq, Wk, Wv)):
            sp.dma_start(w[:], rows(d)).then_inc(loads, 16)
        sp.dma_start(wo_sb[:], rows(Wo)).then_inc(loads, 16)
        sp.dma_start(wr_sb[:], rows(Wr)).then_inc(loads, 16)
        with nc.allow_non_contiguous_dma(reason="small vectors, once"):
            for i, b in enumerate((bq, bk, bv)):
                sp.dma_start(bias_sb[:, i, :], b.rearrange("(t p) -> p t", t=2)).then_inc(loads, 16)
            for t in range(2):
                sp.dma_start(memT[0:DH, t, :], memory[:, t * DH:(t + 1) * DH].rearrange("m p -> p m")).then_inc(loads, 16)
        sp.dma_start(bo_sb[DH:DH + 1, :], bo.rearrange("(a d) -> a d", a=1)).then_inc(loads, 16)
        sp.dma_start(b2_sb[:], b2.rearrange("(a d) -> a d", a=1).to_broadcast([128, D])).then_inc(loads, 16)
        sp.wait_ge(pool_set, 2)
        for slots in (xs_dram, ys_dram):
            flat = slots.rearrange("(n p r) d -> n p (r d)", p=128, r=2)
            for n in range(2 * ROWS // 256):
                sp.dma_start(flat[n], zero_sb[:]).then_inc(zeroed, 16)

        def body(g, j, live):
            t = g * 4 + j
            if live(0):
                if not (isinstance(t, int) and t < 2):
                    sp.wait_ge(patch_tr, t - 1)
                for k in range(2):
                    n = 127 if k and isinstance(t, int) and t == B - 1 else 128
                    src = windows(x, t, k * 128, n)
                    settle(sp, sp_passed)
                    sp.dma_start(patches[0:n, j % 2, k, :], src).then_inc(x_loaded[j % 2], 16)
            if live(3):
                sp.wait_ge(h2_ready, t - 2)
                settle(sp, sp_passed)
                sp.dma_start(h2_dram[t - 3].rearrange("k p d -> p k d"), h2[:, (j + 1) % 2, :, :]) \
                    .then_inc(h2_stored[(j + 1) % 2], 16)

        for j in range(4):
            body(0, j, lambda lag: j >= lag)
        for j in range(4):
            body(1, j, lambda lag: True)
        with sp.Fori(2, B // 4 - 1) as g:
            for j in range(4):
                body(g, j, lambda lag: True)
        for j in range(4):
            body(B // 4 - 1, j, lambda lag: True)
        for j in range(LAGS):
            body(B // 4, j, lambda lag: j < lag)
        sp.wait_ge(h2_stored[0], 16 * (B // 2))
        sp.wait_ge(h2_stored[1], 16 * (B // 2))
        sp.wait_ge(zeroed, 2 * 16 * (2 * ROWS // 256))

    @block.gpsimd
    def _(pool):
        pool.memset(ident[:], 0.0).then_inc(pool_set, 1)
        pool.memset(zero_sb[:], 0.0).then_inc(pool_set, 1)
        pool.wait_ge(pool_set, 1)
        pool.affine_select(out=ident[:], in_=ident[:], compare_op=ALU.not_equal, fill=1.0, base=0,
                           pattern=[[-1, 128]], channel_multiplier=1).then_inc(pool_set, 1)
        pool.memset(half[:], -0.5).then_inc(pool_set, 1)
        pool.memset(probs[:], 0.0).then_inc(pool_set, 1)
        pool.wait_ge(pool_set, 5)
        pool.memset(memT[DH:DH + 1, :, :], 1.0).then_inc(pool_set, 1)
        pool.wait_ge(pool_set, 6)

        def norm(n, which, mv_ready, ve_ready, rs_ready):
            pool.wait_ge(mv_ready, n + 1)
            settle(pool, pool_passed)
            pool.tensor_scalar(vare[:, which, :], mv[:, which, :, 1], EPS, None, ALU.add).then_inc(ve_ready, 1)
            pool.wait_ge(ve_ready, n + 1)
            pool.tensor_tensor(rstd[:, which, :], vare[:, which, :], half[:], ALU.pow).then_inc(rs_ready, 1)
            pool.wait_ge(rs_ready, n + 1)

        def body(g, j, live):
            t = g * 4 + j
            if live(3):
                n = t - 3
                norm(n, 1, mv2, ve2, rs2)
                wait(pool, c2_tr, n)
                settle(pool, pool_passed)
                for k in range(2):
                    ins = pool.tensor_scalar(c2[:, k, :], h2[:, (j + 1) % 2, k, :], mv[:, 1, k, 0:1],
                                             rstd[:, 1, k:k + 1], ALU.subtract, ALU.mult)
                ins.then_inc(c2_ready, 1)
            if live(0):
                n = t
                norm(n, 0, mv1, ve1, rs1)
                wait(pool, c_tr, n)
                settle(pool, pool_passed)
                for k in range(2):
                    ins = pool.tensor_scalar(c[:, k, :], h[:, j, k, :], mv[:, 0, k, 0:1],
                                             rstd[:, 0, k:k + 1], ALU.subtract, ALU.mult)
                ins.then_inc(c_ready, 1)

        all_iterations(pool, body)

    @block.scalar
    def _(act):
        act.wait_ge(weights_tr, 2)
        act.activation(w2T[:], ps_h[0:DH, 0:2 * D].rearrange("p (t d) -> p t d", t=2), ACT.Copy).then_inc(weights_cp, 1)
        act.activation(wqkvT[0][:, :, 0:D], ps_v[0:DH, 0:2 * D].rearrange("p (t d) -> p t d", t=2),
                       ACT.Copy).then_inc(weights_cp, 1)
        act.wait_ge(folded, 3)
        act.activation(w21[0][:], ps_q[:, 0, 0:D], ACT.Copy).then_inc(split_hi, 1)
        for k in range(2):
            n = DH + k
            act.activation(qk[0][0:n, k, 0:D + 1], ps_s[0:n, k, 0:D + 1], ACT.Copy).then_inc(split_hi, 1)
        act.wait_ge(split_lo, 4)
        act.activation(vo[0][0:DH, 0, :], vo_sb[0:DH, 0, :], ACT.Copy).then_inc(split_hi, 1)
        act.activation(vo[0][0:DH + 1, 1, :], vo_sb[0:DH + 1, 1, :], ACT.Copy).then_inc(split_hi, 1)
        act.wait_ge(vmem_mm, 1)
        act.activation(vmem[0][0:MEM - 1, :], ps_h[0:MEM - 1, 0:D], ACT.Copy).then_inc(split_hi, 1)
        act.wait_ge(mem_set, 1)

        def body(g, j, live):
            t = g * 4 + j
            if live(3):
                n = t - 3
                act.wait_ge(p_tr, n + 1)
                wait(act, pv_mm, n)
                act.activation(probsT[0][:], ps_p[:, 0:3, :], ACT.Copy).then_inc(pT_hi, 1)
            if live(0):
                n = t
                act.wait_ge(patch_tr, n + 1)
                wait(act, h_mm, n)
                act.activation(patchT[0][:], ps_x, ACT.Copy).then_inc(patch_hi, 1)
            if live(1):
                n = t - 1
                r = (j - 1) % 2
                act.wait_ge(c_tr, n + 1)
                wait(act, s_mm, n - 1)
                act.activation(cT[0][0:DH, r, :, 0:NP], ps_c[0:DH, :, 0:NP], ACT.Copy).then_inc(cT_hi, 1)
            if live(2):
                n = t - 2
                act.wait_ge(npeak_ready, n + 1)
                wait(act, p_tr, n)
                wait(act, rt_ready, n - 1)
                for k in range(2):
                    ins = act.activation(probs[:, k, 0:NK], ps_s[:, k, 0:NK], ACT.Exp, bias=npeak[:, k:k + 1],
                                         scale=SCALE, accum_out=total[:, j % 2, k:k + 1])
                ins.then_inc(exp_done, 1)
            if live(1):
                n = t - 1
                r = (j - 1) % 2
                act.wait_ge(q_mm, n + 1)
                wait(act, s_mm, n - 1)
                act.activation(qT[0][0:DH + 1, r, :, :], ps_q[0:DH + 1, :, :], ACT.Copy).then_inc(q_hi, 1)
                act.wait_ge(v_mm, n + 1)
                wait(act, pv_mm, n - 1)
                act.activation(v[0][:, r, :, :], ps_v[:, 0:2 * D].rearrange("p (t d) -> p t d", t=2),
                               ACT.Copy).then_inc(v_hi, 1)
            if live(4):
                n = t - 4
                act.wait_ge(c2_tr, n + 1)
                wait(act, lg_mm, n)
                act.activation(c2T[:], ps_c[0:DH, :, :], ACT.Copy).then_inc(c2T_ready, 1)

        all_iterations(act, body)

    @block.vector
    def _(dve):
        dve.wait_ge(weights_tr, 4)
        for i in range(1, 3):
            src = ps_q if i == 1 else ps_c
            for k in range(2):
                ins = dve.tensor_copy(wqkvT[i][:, k, 0:D], src[0:DH, k, 0:D])
        dve.wait_ge(loads, 16 * (NLOADS - 1))
        for i in range(3):
            ins = dve.tensor_copy(wqkvT[i][:, :, D], bias_sb[:, i, :])
        ins.then_inc(weights_cp, 1)
        for k in range(2):
            for r in range(2):
                dve.memset(cT[k][0:DH, r, :, NP:KW].bitcast(F32), 0.0)
                dve.memset(cT[k][DH:DH + 1, r, :, :].bitcast(F32), 1.0 - k)
            ins = dve.memset(vmem[k][:].bitcast(F32), 0.0)
        ins.then_inc(split_lo, 1)
        dve.wait_ge(split_lo, 1)
        dve.wait_ge(pool_set, 6)
        for r in range(2):
            ins = dve.tensor_copy(cT[0][0:DH, r, :, NP:NK], memT[0:DH, :, :])
        ins.then_inc(split_lo, 1)
        dve.wait_ge(split_lo, 2)
        for r in range(2):
            dve.tensor_tensor(cT[1][0:DH, r, :, NP:NK], memT[0:DH, :, :],
                              cT[0][0:DH, r, :, NP:NK].bitcast(F32), ALU.subtract)
        dve.wait_ge(folded, 4)
        dve.tensor_copy(vo_sb[0:DH, 0, :], ps_h[0:DH, 0:D])
        dve.tensor_copy(vo_sb[0:DH + 1, 1, :], ps_v[0:DH + 1, 0:D]).then_inc(split_lo, 1)
        dve.wait_ge(split_lo, 3)
        dve.tensor_tensor(vo_sb[DH:DH + 1, 1, :], vo_sb[DH:DH + 1, 1, :], bo_sb[DH:DH + 1, :],
                          ALU.add).then_inc(split_lo, 1)
        dve.wait_ge(split_hi, 3)
        dve.tensor_tensor(w21[1][:], ps_q[:, 0, 0:D], w21[0][:].bitcast(F32), ALU.subtract)
        for k in range(2):
            n = DH + k
            dve.tensor_tensor(qk[1][0:n, k, 0:D + 1], ps_s[0:n, k, 0:D + 1],
                              qk[0][0:n, k, 0:D + 1].bitcast(F32), ALU.subtract)
        dve.wait_ge(split_hi, 5)
        for k in range(2):
            n = DH + k
            ins = dve.tensor_tensor(vo[1][0:n, k, :], vo_sb[0:n, k, :], vo[0][0:n, k, :].bitcast(F32), ALU.subtract)
        dve.wait_ge(split_hi, 6)
        ins = dve.tensor_tensor(vmem[1][0:MEM - 1, :], ps_h[0:MEM - 1, 0:D],
                                vmem[0][0:MEM - 1, :].bitcast(F32), ALU.subtract)
        ins.then_inc(mem_set, 1)

        def mean_variance(n, src, which, st_ready, mv_ready):
            for k in range(2):
                ins = dve.bn_stats(stats[:, which, k, :], src[:, k, :])
            ins.then_inc(st_ready, 1)
            dve.wait_ge(st_ready, n + 1)
            settle(dve, dve_passed)
            for k in range(2):
                ins = dve.bn_aggr(mv[:, which, k, :], stats[:, which, k, :])
            ins.then_inc(mv_ready, 1)

        def low(dst, src, hi, hi_ready, lo_ready, n):
            dve.wait_ge(hi_ready, n + 1)
            dve.tensor_tensor(dst, src, hi.bitcast(F32), ALU.subtract).then_inc(lo_ready, 1)

        def body(g, j, live):
            t = g * 4 + j
            if live(3):
                low(probsT[1][:], ps_p[:, 0:3, :], probsT[0][:], pT_hi, pT_lo, t - 3)
            if live(0):
                low(patchT[1][:], ps_x, patchT[0][:], patch_hi, patch_lo, t)
            if live(1):
                r = (j - 1) % 2
                low(cT[1][0:DH, r, :, 0:NP], ps_c[0:DH, :, 0:NP], cT[0][0:DH, r, :, 0:NP], cT_hi, cT_lo, t - 1)
            if live(2):
                n = t - 2
                dve.wait_ge(s_mm, n + 1)
                dve.tensor_reduce(peak[:], ps_s[:, :, 0:NK], AX.X, ALU.max).then_inc(peak_ready, 1)
                dve.wait_ge(peak_ready, n + 1)
                wait(dve, exp_done, n)
                dve.tensor_scalar(npeak[:], peak[:], -SCALE, None, ALU.mult).then_inc(npeak_ready, 1)
            if live(3):
                n = t - 3
                r = (j - 3) % 2
                dve.wait_ge(exp_done, n + 1)
                dve.reciprocal(rtotal[:], total[:, r, :]).then_inc(rt_ready, 1)
                dve.wait_ge(rt_ready, n + 1)
                dve.wait_ge(pv_mm, n + 1)
                if not (isinstance(t, int) and n < 2):
                    dve.wait_ge(h2_stored[r], (turns(g, j, 3) - 1) * 16)
                wait(dve, c2_ready, n)
                for k in range(2):
                    ins = dve.scalar_tensor_tensor(h2[:, r, k, :], ps_o[:, k, :], rtotal[:, k:k + 1],
                                                   h[:, (j - 3) % 4, k, :], ALU.mult, ALU.add)
                ins.then_inc(h2_ready, 1)
                dve.wait_ge(h2_ready, n + 1)
                mean_variance(n, h2[:, r], 1, st2, mv2)
            if live(0):
                n = t
                dve.wait_ge(h_mm, n + 1)
                wait(dve, c_ready, n)
                dve.tensor_tensor(h[:, j, :, :], ps_h[:, 0:2 * D].rearrange("p (t d) -> p t d", t=2),
                                  b2_sb[:].rearrange("p (a d) -> p a d", a=1).to_broadcast([128, 2, D]),
                                  ALU.add).then_inc(h_ready, 1)
                dve.wait_ge(h_ready, n + 1)
                mean_variance(n, h[:, j], 0, st1, mv1)
            if live(1):
                r = (j - 1) % 2
                low(qT[1][0:DH + 1, r, :, :], ps_q[0:DH + 1, :, :], qT[0][0:DH + 1, r, :, :], q_hi, q_lo, t - 1)
                low(v[1][:, r, :, :], ps_v[:, 0:2 * D].rearrange("p (t d) -> p t d", t=2), v[0][:, r, :, :],
                    v_hi, v_lo, t - 1)
            if live(3):
                n = t - 3
                dve.wait_ge(rs2, n + 1)
                kept = routes[:, bass.ds(n * 20, 20)].rearrange("p (k r) -> p k r", k=2)
                dve.tensor_copy(kept[:, :, E], mv[:, 1, :, 0])
                dve.tensor_copy(kept[:, :, E + 1], rstd[:, 1, :])
            if live(4):
                n = t - 4
                dve.wait_ge(lg_mm, n + 1)
                kept = routes[:, bass.ds(n * 20, 20)].rearrange("p (k r) -> p k r", k=2)
                dve.tensor_copy(kept[:, :, 0:E], ps_lg.rearrange("p (k e) -> p k e", k=2)).then_inc(lg_kept, 1)

        all_iterations(dve, body)

    @block.tensor
    def _(pe):
        pe.wait_ge(loads, 16 * (NLOADS - 1))
        pe.wait_ge(pool_set, 6)
        for w, bank in ((w2_sb, ps_h), (wqkv_sb[0], ps_v), (wqkv_sb[1], ps_q), (wqkv_sb[2], ps_c)):
            for k in range(2):
                for i in range(2):
                    dst = bank[0:DH, k * D + i * DH:k * D + (i + 1) * DH] if bank in (ps_h, ps_v) \
                        else bank[0:DH, k, i * DH:(i + 1) * DH]
                    ins = pe.transpose(dst, w[:, i, k * DH:(k + 1) * DH], ident[0:DH, 0:DH])
            ins.then_inc(weights_tr, 1)
        pe.wait_ge(weights_cp, 3)
        for k in range(2):
            ins = pe.matmul(ps_q[:, 0, 0:D], w1_sb[:, k, :], w2T[:, k, :], start=(k == 0), stop=(k == 1))
        ins.then_inc(folded, 1)
        for i in range(2):
            n = DH + i
            for k in range(2):
                ins = pe.matmul(ps_s[0:n, i, 0:D + 1], wqkvT[0][:, k, i * DH:i * DH + n], wqkvT[1][:, k, :],
                                start=(k == 0), stop=(k == 1))
            ins.then_inc(folded, 1)
        for i in range(2):
            n = DH + i
            for k in range(2):
                ins = pe.matmul((ps_v if i else ps_h)[0:n, 0:D], wqkvT[2][:, k, i * DH:i * DH + n], wo_sb[:, k, :],
                                start=(k == 0), stop=(k == 1))
        ins.then_inc(folded, 1)
        pe.wait_ge(split_lo, 4)
        for k in range(2):
            n = DH + k
            ins = pe.matmul(ps_h[0:MEM - 1, 0:D], memT[0:n, k, 1:MEM], vo_sb[0:n, k, :], start=(k == 0), stop=(k == 1))
        ins.then_inc(vmem_mm, 1)
        pe.wait_ge(mem_set, 1)
        pe.wait_ge(split_hi, 6)

        PASSES = ((0, 0), (0, 1), (1, 0))

        def product(dst, terms):
            n = 0
            for stationary, moving in terms:
                for a, b in PASSES:
                    ins = pe.matmul(dst, stationary[a], moving[b], start=(n == 0), stop=(n == 3 * len(terms) - 1))
                    n += 1
            return ins

        def pair(two, *index):
            return [part[index] for part in two]

        def body(g, j, live):
            t = g * 4 + j
            if live(3):
                n = t - 3
                pe.wait_ge(exp_done, n + 1)
                wait(pe, h2_ready, n)
                for i in range(3):
                    for k in range(2):
                        ins = pe.transpose(ps_p[:, i, k * 128:(k + 1) * 128], probs[:, k, i * 128:(i + 1) * 128], ident[:])
                ins.then_inc(p_tr, 1)
            if live(0):
                n = t
                pe.wait_ge(x_loaded[j % 2], turns(g, j, 0) * 32)
                wait(pe, h_ready, n)
                for k in range(2):
                    ins = pe.transpose(ps_x[:, k * 128:(k + 1) * 128], patches[:, j % 2, k, :], ident[:])
                ins.then_inc(patch_tr, 1)
            if live(1):
                n = t - 1
                pe.wait_ge(c_ready, n + 1)
                wait(pe, lg_kept, n - 3)
                for i in range(2):
                    for k in range(2):
                        ins = pe.transpose(ps_c[0:DH, i, k * 128:(k + 1) * 128], c[:, k, i * DH:(i + 1) * DH], ident[:])
                ins.then_inc(c_tr, 1)
            if live(2):
                n = t - 2
                r = j % 2
                pe.wait_ge(q_lo, n + 1)
                wait(pe, exp_done, n)
                for k in range(2):
                    ins = product(ps_s[:, k, 0:KW],
                                  [(pair(qT, slice(0, DH + i), r, i, slice(k * 128, (k + 1) * 128)),
                                    pair(cT, slice(0, DH + i), r, i, slice(0, KW))) for i in range(2)])
                ins.then_inc(s_mm, 1)
            if live(3):
                n = t - 3
                r = (j - 3) % 2
                pe.wait_ge(pT_lo, n + 1)
                pe.wait_ge(v_lo, n + 1)
                for k in range(2):
                    q = slice(k * 128, (k + 1) * 128)
                    ins = product(ps_o[:, k, :],
                                  [(pair(probsT, slice(0, 128), i, q), pair(v, slice(0, 128), r, i, slice(0, D)))
                                   for i in range(2)]
                                  + [(pair(probsT, slice(0, 128), 2, q), pair(vmem, slice(0, 128), slice(0, D)))])
                ins.then_inc(pv_mm, 1)
            if live(0):
                n = t
                pe.wait_ge(patch_lo, n + 1)
                for k in range(2):
                    ins = product(ps_h[:, k * D:(k + 1) * D],
                                  [(pair(patchT, slice(0, 128), slice(k * 128, (k + 1) * 128)),
                                    pair(w21, slice(0, 128), slice(0, D)))])
                ins.then_inc(h_mm, 1)
            if live(1):
                n = t - 1
                r = (j - 1) % 2
                pe.wait_ge(cT_lo, n + 1)
                wait(pe, q_lo, n)
                for o in range(2):
                    m = DH + 1
                    ins = product(ps_q[0:m, o, :],
                                  [(pair(qk, slice(0, DH + i), i, slice(o * DH, o * DH + m)),
                                    pair(cT, slice(0, DH + i), r, i, slice(0, 256))) for i in range(2)])
                ins.then_inc(q_mm, 1)
            if live(4):
                n = t - 4
                pe.wait_ge(c2_ready, n + 1)
                if live(1):
                    pe.wait_ge(cT_lo, t)
                else:
                    pe.wait_ge(lg_kept, n)
                for i in range(2):
                    for k in range(2):
                        ins = pe.transpose(ps_c[0:DH, i, k * 128:(k + 1) * 128], c2[:, k, i * DH:(i + 1) * DH], ident[:])
                ins.then_inc(c2_tr, 1)
            if live(1):
                n = t - 1
                r = (j - 1) % 2
                wait(pe, v_lo, n)
                for k in range(2):
                    ins = product(ps_v[:, k * D:(k + 1) * D],
                                  [(pair(cT, slice(0, DH + i), r, i, slice(k * 128, (k + 1) * 128)),
                                    pair(vo, slice(0, DH + i), i, slice(0, D))) for i in range(2)])
                ins.then_inc(v_mm, 1)
            if live(4):
                n = t - 4
                pe.wait_ge(c2T_ready, n + 1)
                for k in range(2):
                    for i in range(2):
                        ins = pe.matmul(ps_lg[:, k * E:(k + 1) * E], c2T[:, i, k * 128:(k + 1) * 128], wr_sb[:, i, :],
                                        start=(i == 0), stop=(i == 1))
                ins.then_inc(lg_mm, 1)

        all_iterations(pe, body)


def windows(x, s, first, count):
    return bass.AP(x.tensor, s * L + first * HOP, [[HOP, count], [1, PATCH]])


def experts(nc, ctx, wi, wo, routes, ident, h2_dram, xs_dram, ys_dram, out):
    def sb(name, shape, dt=F32):
        return ctx.enter_context(nc.sbuf_tensor(name, shape, dt))

    def psum(name, shape):
        return ctx.enter_context(nc.psum_tensor(name, shape, F32))

    def sem(name):
        return ctx.enter_context(nc.semaphore(name))

    PARTS = ("hi", "lo")
    wi_main = [sb(f"wi_main_{p}", [128, E, F], F32R) for p in PARTS]
    wi_rest = [sb(f"wi_rest_{p}", [128, E // 2, F], F32R) for p in PARTS]
    wo_sb = [sb(f"wo_{p}", [128, E, FT, D], F32R) for p in PARTS]
    xrow = sb("xrow", [CPP, 2, J, D])
    xmain = [sb(f"xmain_{p}", [128, C], F32R) for p in PARTS]
    xrest = [[sb(f"xrest_{p}_{o}", [128, C], F32R) for p in PARTS] for o in range(2)]
    hid = [sb(f"hid_{p}", [128, FT, C], F32R) for p in PARTS]
    yrow = sb("yrow", [CPP, 2, J, D])
    send = sb("send", [128, TPG, D])
    rt = sb("rt", [128, TPG, E + 2])
    expo = sb("expo", [128, TPG, E])
    tokmax = sb("tokmax", [128, TPG])
    toksum = sb("toksum", [128, TPG])
    top = sb("top", [128, TPG, 8])
    topi = sb("topi", [128, TPG, 8], U32)
    chosen = sb("chosen", [128, 2, TPG])
    gate = sb("gate", [128, 2, TPG])
    mask = sb("mask", [128, 2, TPG, E], BF16)
    scan = [sb(f"scan_{i}", [128, 24, E]) for i in range(2)]
    pos = sb("pos", [128, 16, E])
    sel = sb("sel", [128, 16])
    ok = sb("ok", [128, 16])
    slot = sb("slot", [128, 16])
    miss = sb("miss", [128, 16])
    send_idx = sb("send_idx", [128, 16], I32)
    ret_new = sb("ret_new", [128, 2, 16], I32)
    ret_mid = sb("ret_mid", [128, 2, 16], I32)
    ret_use = sb("ret_use", [128, 2, 16], I32)
    ring = sb("ring", [128, 1])
    before = sb("before", [128, 128], BF16)
    ones = sb("ones", [128, 128], BF16)
    which = sb("which", [128, TPG, E])
    whichi = sb("whichi", [128, TPG * E], I32)
    far = sb("far", [128, 2, TPG])
    area = sb("area", [128, 16 * D])
    raw_main = area[:, 0:F]
    raw_rest = area[:, F:2 * F]
    raw_wo = area[:, 2 * F:2 * F + FT * D].rearrange("p (f d) -> p f d", f=FT)
    back = area[:, 0:TPG * D].rearrange("p (t d) -> p t d", t=TPG)
    got = area[:, TPG * D:16 * D].rearrange("p (r k d) -> p r k d", r=4, k=2)
    ps_x = psum("ps_xT", [128, 2, 512])
    ps_h = psum("ps_hid", [128, 3, 512])
    ps_y = psum("ps_y", [128, 2, 512])
    ps_r = psum("ps_route", [128, 2, 256])
    consts = sem("consts_set")
    w_in = sem("raw_weights_in")
    w_hi = sem("weights_hi_ready")
    w_lo = sem("weights_lo_ready")
    x_in = [sem(f"xrow_in_{i}") for i in range(2)]
    x_tr = sem("x_transposed")
    x_hi = sem("xT_hi_ready")
    x_lo = sem("xT_lo_ready")
    h_mm = sem("hidden_made")
    h_hi = sem("hidden_hi_ready")
    h_lo = sem("hidden_lo_ready")
    y_mm = sem("y_made")
    y_act = sem("y_third_copied")
    y_dve = sem("y_first_two_copied")
    y_out = [sem(f"y_stored_{i}") for i in range(2)]
    send_in = sem("send_in")
    route = sem("route_steps")
    exp_done = sem("route_exp_done")
    mask_ready = sem("mask_ready")
    count_mm = sem("counts_made")
    send_ready = sem("send_ready")
    idx_ready = sem("indices_ready")
    sent = sem("sent")
    use_ready = sem("return_indices_ready")
    fetched = [sem(f"fetched_{i}") for i in range(4)]
    back_in = sem("back_in")
    comb_half = sem("first_expert_added")
    comb = sem("second_expert_added")
    out_done = sem("out_stored")
    ret_moved = sem("return_indices_moved")
    dve_passed = sem("vector_passed")
    sp_passed = sem("sync_passed")
    pool_passed = sem("gpsimd_passed")
    STEPS = 22
    block = ctx.enter_context(nc.Block())

    def all_groups(eng, body):
        body(0, False, True, True)
        body(1, True, True, True)
        with eng.Fori(2, G - 1) as g:
            body(g, True, True, True)
        body(G - 1, True, True, False)
        body(G, True, False, False)

    @block.sync
    def _(sp):
        def load_x(g, e):
            if e < 2:
                sp.wait_ge(sent, (g + 1) * 256)
            if not (isinstance(g, int) and g == 0 and e < 2):
                sp.wait_ge(x_tr, g * E + (e - 1))
            first = (g % 2) * ROWS + e * SLOTS
            settle(sp, sp_passed)
            sp.dma_start(xrow[:, e % 2, :, :].rearrange("p j d -> p (j d)"),
                         xs_dram[bass.ds(first, SLOTS), :].rearrange("(p j) d -> p (j d)", j=J)) \
                .then_inc(x_in[e % 2], 16)

        def load_weights(e):
            if e:
                sp.wait_ge(w_lo, e)
            m = 64 * (e % 2)
            sp.dma_start(raw_main, wi[e, m:m + 128, :]).then_inc(w_in, 16)
            if e % 2 == 0:
                sp.dma_start(raw_rest[64:128, :], wi[e, 128:192, :]).then_inc(w_in, 16)
                sp.dma_start(raw_rest[0:64, :], wi[e + 1, 0:64, :]).then_inc(w_in, 16)
            sp.dma_start(raw_wo, wo[e].rearrange("(f p) d -> p f d", p=128)).then_inc(w_in, 16)

        def load_send(g):
            if not (isinstance(g, int) and g == 0):
                sp.wait_ge(sent, g * 256)
            settle(sp, sp_passed)
            sp.dma_start(send[:], h2_dram[bass.ds(g * SPG, SPG)].rearrange("s k p d -> p (s k) d")) \
                .then_inc(send_in, 16)

        load_weights(0)
        load_send(0)
        load_x(0, 0)
        load_x(0, 1)

        def body(g, prev, cur, nxt):
            if nxt:
                load_send(g + 1)
            if prev:
                if isinstance(g, int):
                    wait(sp, w_lo, E)
                else:
                    sp.wait_ge(w_lo, E)
                wait(sp, out_done, (g - 1) * (16 * 3 * SPG))
                settle(sp, sp_passed)
                sp.dma_start(back, h2_dram[bass.ds((g - 1) * SPG, SPG)].rearrange("s k p d -> p (s k) d")) \
                    .then_inc(back_in, 16)
            for e in range(E):
                if cur:
                    if isinstance(g, int) and g == 0 and e + 1 < E:
                        load_weights(e + 1)
                    if e + 2 < E:
                        load_x(g, e + 2)
                    elif nxt:
                        load_x(g + 1, e + 2 - E)
                    sp.wait_ge(y_act, g * E + (e + 1))
                    settle(sp, sp_passed)
                    sp.wait_ge(y_dve, g * E + (e + 1))
                    settle(sp, sp_passed)
                    if not (isinstance(g, int) and g < 2):
                        sp.wait_ge(comb, (g - 1) * TPG)
                    first = (g % 2) * ROWS + e * SLOTS
                    settle(sp, sp_passed)
                    sp.dma_start(ys_dram[bass.ds(first, SLOTS), :].rearrange("(p j) d -> p (j d)", j=J),
                                 yrow[:, e % 2, :, :].rearrange("p j d -> p (j d)")).then_inc(y_out[e % 2], 16)
                if prev and e in STORES:
                    for s in STORES[e]:
                        sp.wait_ge(comb, (g - 1) * TPG + (2 * s + 2))
                        settle(sp, sp_passed)
                        b = (g - 1) * SPG + s
                        sp.dma_start(out[bass.ds(b, 1), 0:128, :].rearrange("b p d -> p (b d)"), back[:, 2 * s, :]) \
                            .then_inc(out_done, 16)
                        for lo, hi in ((0, 112), (112, 127)):
                            sp.dma_start(out[bass.ds(b, 1), 128 + lo:128 + hi, :].rearrange("b p d -> p (b d)"),
                                         back[lo:hi, 2 * s + 1, :]).then_inc(out_done, 16)

        all_groups(sp, body)
        sp.wait_ge(out_done, G * 16 * 3 * SPG)

    @block.gpsimd
    def _(pool):
        n = [0]

        def mark(ins):
            n[0] += 1
            ins.then_inc(consts, 1)

        mark(pool.memset(before[:], 1.0))
        mark(pool.memset(ones[:], 1.0))
        mark(pool.memset(far[:], FAR))
        mark(pool.iota(whichi[:], pattern=[[0, TPG], [1, E]], base=0, channel_multiplier=0))
        for o in range(2):
            for part in xrest[o]:
                pool.wait_ge(consts, n[0])
                mark(pool.memset(part[64 * o:64 * o + 64, :].bitcast(F32), 0.0))
        pool.wait_ge(consts, n[0])
        mark(pool.memset(yrow[:], 0.0))
        pool.wait_ge(consts, n[0])
        mark(pool.memset(ring[:], float(ROWS)))
        for s in scan:
            mark(pool.memset(s[:, 0:9, :], 0.0))
        pool.wait_ge(consts, n[0])
        mark(pool.affine_select(out=before[:], in_=before[:], compare_op=ALU.is_gt, fill=0.0, base=0,
                                pattern=[[1, 128]], channel_multiplier=-1))
        oddfar = far[:].rearrange("p k (s o) -> p k s o", o=2)[:, :, :, 1]
        mark(pool.affine_select(out=oddfar, in_=oddfar, compare_op=ALU.is_gt, fill=2 * FAR, base=127,
                                pattern=[[0, 2], [0, SPG]], channel_multiplier=-1))
        mark(pool.tensor_copy(which[:].rearrange("p t e -> p (t e)"), whichi[:]))
        pool.wait_ge(consts, n[0])
        oddwhich = which[:].rearrange("p (s o) e -> p s o e", o=2)[:, :, 1, :]
        mark(pool.affine_select(out=oddwhich, in_=oddwhich, compare_op=ALU.is_gt, fill=100.0, base=127,
                                pattern=[[0, SPG], [0, E]], channel_multiplier=-1))
        assert n[0] == NCONSTS

        def low_weights(e):
            pool.wait_ge(w_hi, e + 1)
            pool.tensor_tensor(wi_main[1][:, e, :], raw_main, wi_main[0][:, e, :].bitcast(F32), ALU.subtract)
            if e % 2 == 0:
                pool.tensor_tensor(wi_rest[1][:, e // 2, :], raw_rest, wi_rest[0][:, e // 2, :].bitcast(F32),
                                   ALU.subtract)
            pool.tensor_tensor(wo_sb[1][:, e, :, :], raw_wo, wo_sb[0][:, e, :, :].bitcast(F32),
                               ALU.subtract).then_inc(w_lo, 1)

        def dispatch(g):
            pool.wait_ge(idx_ready, g + 1)
            pool.wait_ge(send_ready, g + 1)
            if not (isinstance(g, int) and g < 2):
                for i in range(2):
                    pool.wait_ge(x_in[i], (g - 1) * (16 * E // 2))
            settle(pool, pool_passed)
            for t in range(TPG):
                for k in range(2):
                    i = k * TPG + t
                    pool.indirect_dma_start(xs_dram, bass.IndirectOffsetOnAxis(ap=send_idx[:, i:i + 1], axis=0),
                                            send[:, t, :], None, bounds_check=2 * ROWS - 1, oob_is_err=False) \
                        .then_inc(sent, 16)

        def fetch(g, t):
            if t == 0:
                pool.wait_ge(use_ready, g + 1)
                for i in range(2):
                    pool.wait_ge(y_out[i], (g + 1) * (16 * E // 2))
                pool.wait_ge(w_lo, E)
            if t >= 4 or not (isinstance(g, int) and g == 0):
                pool.wait_ge(comb, g * TPG + (t - 3))
            settle(pool, pool_passed)
            for k in range(2):
                i = k * TPG + t
                pool.indirect_dma_start(got[:, t % 4, k, :], None, ys_dram,
                                        bass.IndirectOffsetOnAxis(ap=ret_use[:, 0, i:i + 1], axis=0),
                                        bounds_check=2 * ROWS - 1, oob_is_err=False).then_inc(fetched[t % 4], 16)

        low_weights(0)
        dispatch(0)

        def body(g, prev, cur, nxt):
            if prev:
                for t in range(4):
                    fetch(g - 1, t)
            if isinstance(g, int) and g == 0:
                for e in range(1, 4):
                    low_weights(e)
            if nxt:
                dispatch(g + 1)
            if isinstance(g, int) and g == 0:
                for e in range(4, E):
                    low_weights(e)
            if prev:
                for t in range(4, 8):
                    fetch(g - 1, t)

        all_groups(pool, body)

    @block.scalar
    def _(act):
        def high_weights(e):
            act.wait_ge(w_in, 16 * (2 * (e + 1) + 2 * (e // 2 + 1)))
            act.activation(wi_main[0][:, e, :], raw_main, ACT.Copy)
            if e % 2 == 0:
                act.activation(wi_rest[0][:, e // 2, :], raw_rest, ACT.Copy)
            act.activation(wo_sb[0][:, e, :, :], raw_wo, ACT.Copy).then_inc(w_hi, 1)

        def high_x(g, e):
            act.wait_ge(x_tr, g * E + (e + 1))
            main, rest, p = (0, 1, 64) if e % 2 == 0 else (1, 0, 0)
            act.activation(xmain[0][:], ps_x[:, main, 0:C], ACT.Copy)
            act.activation(xrest[e % 2][0][p:p + 64, :], ps_x[p:p + 64, rest, 0:C], ACT.Copy).then_inc(x_hi, 1)

        def exponentials(g):
            act.wait_ge(route, g * STEPS + 3)
            act.activation(expo[:], expo[:], ACT.Exp).then_inc(exp_done, 1)

        high_weights(0)
        exponentials(0)
        act.wait_ge(consts, NCONSTS)
        high_x(0, 0)

        def body(g, prev, cur, nxt):
            for e in range(E):
                if cur:
                    wait(act, y_mm, g * (2 * E) + 2 * e)
                    for f in range(FT):
                        act.wait_ge(h_mm, g * (FT * E) + (FT * e + f + 1))
                        act.activation(hid[0][:, f, :], ps_h[:, f % 3, 0:C], ACT.Relu).then_inc(h_hi, 1)
                    if isinstance(g, int) and g == 0 and e + 1 < E:
                        high_weights(e + 1)
                    if e + 1 < E:
                        high_x(g, e + 1)
                    elif nxt:
                        high_x(g + 1, 0)
                    act.wait_ge(y_mm, g * (2 * E) + (2 * e + 2))
                    if not (isinstance(g, int) and g == 0 and e < 2):
                        act.wait_ge(y_out[e % 2], g * (16 * E // 2) + 16 * (e // 2))
                    act.activation(yrow[0:CP, e % 2, 2, :], ps_y[0:CP, 1, 0:D], ACT.Copy).then_inc(y_act, 1)
                if nxt and e == 0:
                    exponentials(g + 1)

        all_groups(act, body)

    @block.vector
    def _(dve):
        def low_x(g, e):
            dve.wait_ge(x_hi, g * E + (e + 1))
            main, rest, p = (0, 1, 64) if e % 2 == 0 else (1, 0, 0)
            dve.tensor_tensor(xmain[1][:], ps_x[:, main, 0:C], xmain[0][:].bitcast(F32), ALU.subtract)
            dve.tensor_tensor(xrest[e % 2][1][p:p + 64, :], ps_x[p:p + 64, rest, 0:C],
                              xrest[e % 2][0][p:p + 64, :].bitcast(F32), ALU.subtract).then_inc(x_lo, 1)

        def spread(ap, n):
            return ap.unsqueeze(len(ap.shape)).to_broadcast(list(ap.shape) + [n])

        def step(g, i, ins, go_on=False):
            ins.then_inc(route, 1)
            if not go_on:
                dve.wait_ge(route, g * STEPS + i)
                if i == 6:
                    settle(dve, dve_passed)

        def route_logits(g):
            step(g, 1, dve.tensor_copy(rt[:].rearrange("p t r -> p (t r)"), routes[:, bass.ds(g * 80, 80)]))
            step(g, 2, dve.tensor_reduce(tokmax[:], rt[:, :, 0:E], AX.X, ALU.max))
            step(g, 3, dve.tensor_tensor(expo[:], rt[:, :, 0:E], spread(tokmax[:], E), ALU.subtract), True)

        def normed(g, tiles):
            dve.wait_ge(route, g * STEPS + 1)
            dve.wait_ge(send_in, (g + 1) * 16)
            for t in tiles:
                ins = dve.tensor_scalar(send[:, t, :], send[:, t, :], rt[:, t, E:E + 1], rt[:, t, E + 1:E + 2],
                                        ALU.subtract, ALU.mult)
            return ins

        def route_choice(g):
            dve.wait_ge(exp_done, g + 1)
            step(g, 4, dve.tensor_reduce(toksum[:], expo[:], AX.X, ALU.add))
            step(g, 5, dve.reciprocal(toksum[:], toksum[:]), True)
            for t in range(TPG):
                ins = dve.max(top[:, t, :], expo[:, t, :])
            step(g, 6, ins)
            for t in range(TPG):
                ins = dve.max_index(topi[:, t, :], top[:, t, :], expo[:, t, :])
            step(g, 7, ins)
            for k in range(2):
                dve.tensor_tensor(gate[:, k, :], top[:, :, k], toksum[:], ALU.mult)
            step(g, 8, dve.tensor_copy(chosen[:].rearrange("p k t -> p t k"), topi[:, :, 0:2]))
            for k in range(2):
                ins = dve.tensor_tensor(mask[:, k, :, :], which[:], spread(chosen[:, k, :], E), ALU.is_equal)
            ins.then_inc(mask_ready, 1)

        def route_slots(g):
            dve.wait_ge(count_mm, g + 1)
            tot = ps_r[:, 1, 0:128].rearrange("p (b e) -> p b e", e=E)
            step(g, 9, dve.tensor_copy(scan[0][:, 9:24, :], tot[:, 0:15, :]))
            for i, d in enumerate((1, 2, 4, 8)):
                src, dst = scan[i % 2], scan[1 - i % 2]
                step(g, 10 + i, dve.tensor_tensor(dst[:, 8:24, :], src[:, 8:24, :], src[:, 8 - d:24 - d, :], ALU.add))
            step(g, 14, dve.tensor_tensor(pos[:], ps_r[:, 0, 0:128].rearrange("p (b e) -> p b e", e=E),
                                          scan[0][:, 8:24, :], ALU.add))
            m = mask[:].rearrange("p k t e -> p (k t) e")
            step(g, 15, dve.tensor_tensor(pos[:], pos[:], m, ALU.mult))
            step(g, 16, dve.tensor_reduce(sel[:], pos[:], AX.X, ALU.add))
            step(g, 17, dve.tensor_scalar(ok[:], sel[:], float(C), None, ALU.is_lt), True)
            step(g, 18, dve.scalar_tensor_tensor(slot[:], chosen[:].rearrange("p k t -> p (k t)"), float(SLOTS),
                                                 sel[:], ALU.mult, ALU.add), True)
            step(g, 19, dve.tensor_scalar(ring[:], ring[:], -1.0, float(ROWS), ALU.mult, ALU.add))
            step(g, 20, dve.tensor_tensor(slot[:], slot[:], ok[:], ALU.mult), True)
            step(g, 21, dve.scalar_tensor_tensor(miss[:], ok[:], -FAR, far[:].rearrange("p k t -> p (k t)"),
                                                 ALU.mult, ALU.add))
            if not (isinstance(g, int) and g == 0):
                dve.wait_ge(sent, g * 256)
            dve.tensor_scalar(ret_new[:, 0, :], slot[:], ring[:, 0:1], None, ALU.add)
            dve.tensor_tensor(ret_new[:, 1, :].bitcast(F32), gate[:].rearrange("p k t -> p (k t)"), ok[:],
                              ALU.mult).then_inc(route, 1)
            dve.scalar_tensor_tensor(send_idx[:], slot[:], ring[:, 0:1], miss[:], ALU.add, ALU.add) \
                .then_inc(idx_ready, 1)

        def add_expert(g, t):
            if t == 0:
                dve.wait_ge(back_in, (g + 1) * 16)
                dve.wait_ge(use_ready, g + 1)
            dve.wait_ge(fetched[t % 4], g * 64 + (32 * (t // 4) + 32))
            for k, done in ((0, comb_half), (1, comb)):
                i = k * TPG + t
                dve.scalar_tensor_tensor(back[:, t, :], got[:, t % 4, k, :], ret_use[:, 1, i:i + 1].bitcast(F32),
                                         back[:, t, :], ALU.mult, ALU.add).then_inc(done, 1)
                dve.wait_ge(done, g * TPG + (t + 1))

        dve.wait_ge(consts, NCONSTS)
        route_logits(0)
        normed(0, range(TPG)).then_inc(send_ready, 1)
        route_choice(0)
        route_slots(0)
        low_x(0, 0)

        def body(g, prev, cur, nxt):
            if prev:
                dve.tensor_copy(ret_use[:], ret_mid[:]).then_inc(use_ready, 1)
                dve.wait_ge(use_ready, g)
            if cur:
                dve.wait_ge(route, (g + 1) * STEPS)
                dve.tensor_copy(ret_mid[:], ret_new[:]).then_inc(ret_moved, 1)
                dve.wait_ge(ret_moved, g + 1)
            for e in range(E):
                if cur:
                    for f in range(FT):
                        dve.wait_ge(h_hi, g * (FT * E) + (FT * e + f + 1))
                        dve.scalar_tensor_tensor(hid[1][:, f, :], ps_h[:, f % 3, 0:C], 0.0,
                                                 hid[0][:, f, :].bitcast(F32), ALU.max, ALU.subtract).then_inc(h_lo, 1)
                    if e + 1 < E:
                        low_x(g, e + 1)
                    elif nxt:
                        low_x(g + 1, 0)
                    dve.wait_ge(y_mm, g * (2 * E) + (2 * e + 1))
                    if not (isinstance(g, int) and g == 0 and e < 2):
                        dve.wait_ge(y_out[e % 2], g * (16 * E // 2) + 16 * (e // 2))
                    dve.tensor_copy(yrow[0:CP, e % 2, 0:2, :].rearrange("p j d -> p (j d)"),
                                    ps_y[0:CP, 0, 0:2 * D]).then_inc(y_dve, 1)
                if nxt:
                    if e == 0:
                        route_logits(g + 1)
                        normed(g + 1, range(0, 4))
                    if e == 1:
                        route_choice(g + 1)
                        normed(g + 1, range(4, 8)).then_inc(send_ready, 1)
                    if e == 2:
                        route_slots(g + 1)
                if prev:
                    for t in ADDS[e]:
                        add_expert(g - 1, t)

        all_groups(dve, body)

    @block.tensor
    def _(pe):
        pe.wait_ge(consts, NCONSTS)
        PASSES = ((0, 0), (0, 1), (1, 0))

        def transpose_x(g, e):
            pe.wait_ge(x_in[e % 2], g * (16 * E // 2) + 16 * (e // 2 + 1))
            if not (isinstance(g, int) and g == 0 and e == 0):
                pe.wait_ge(x_lo, g * E + e)
            for part, first in ((0, 0), (1, 64)):
                for j in range(J):
                    ins = pe.transpose(ps_x[:, part, j * CP:(j + 1) * CP], xrow[0:CP, e % 2, j, first:first + 128],
                                       ident[0:CP, 0:CP])
            ins.then_inc(x_tr, 1)

        def count(g):
            pe.wait_ge(mask_ready, g + 1)
            m = mask[:].rearrange("p k t e -> p (k t e)")
            pe.matmul(ps_r[:, 0, 0:128], before[:], m, start=True, stop=True)
            pe.matmul(ps_r[:, 1, 0:128], ones[:], m, start=True, stop=True).then_inc(count_mm, 1)

        count(0)
        transpose_x(0, 0)

        def body(g, prev, cur, nxt):
            if not cur:
                return
            for e in range(E):
                first = isinstance(g, int) and g == 0
                pe.wait_ge(x_lo, g * E + (e + 1))
                if first:
                    pe.wait_ge(w_lo, e + 1)
                for f in range(FT):
                    if not (first and e == 0 and f < 3):
                        pe.wait_ge(h_lo, g * (FT * E) + (FT * e + f - 2))
                    n = 0
                    for w, xx in (([p[:, e, f * 128:(f + 1) * 128] for p in wi_main], xmain),
                                  ([p[:, e // 2, f * 128:(f + 1) * 128] for p in wi_rest], xrest[e % 2])):
                        for a, b in PASSES:
                            ins = pe.matmul(ps_h[:, f % 3, 0:C], w[a], xx[b][:], start=(n == 0), stop=(n == 5))
                            n += 1
                    ins.then_inc(h_mm, 1)
                if e + 1 < E:
                    transpose_x(g, e + 1)
                elif nxt:
                    transpose_x(g + 1, 0)
                if not (first and e == 0):
                    pe.wait_ge(y_act, g * E + e)
                    pe.wait_ge(y_dve, g * E + e)
                for j in range(J):
                    for f in range(FT):
                        if j == 0:
                            pe.wait_ge(h_lo, g * (FT * E) + (FT * e + f + 1))
                        for n, (a, b) in enumerate(PASSES):
                            ins = pe.matmul(ps_y[0:CP, j // 2, j % 2 * D:(j % 2 + 1) * D], hid[a][:, f, j * CP:(j + 1) * CP], wo_sb[b][:, e, f, :],
                                            start=(f == 0 and n == 0), stop=(f == FT - 1 and n == 2))
                    if j:
                        ins.then_inc(y_mm, 1)
                if nxt and e == 1:
                    count(g + 1)

        all_groups(pe, body)


NCONSTS = 16
ADDS = ((), (0,), (1,), (2,), (3,), (4,), (5,), (6, 7))
STORES = {3: (0,), 5: (1,), 7: (2, 3)}


_INS = ['x', 'L0_tok_W1', 'L0_tok_W2', 'L0_tok_b2', 'L0_attn_memory', 'L0_attn_Wq', 'L0_attn_bq', 'L0_attn_Wk',
        'L0_attn_bk', 'L0_attn_Wv', 'L0_attn_bv', 'L0_attn_Wo', 'L0_attn_bo', 'L0_ffn_w_router', 'L0_ffn_wi',
        'L0_ffn_wo']


def kernel(**inputs):
    import numpy as np
    import concourse.bacc as bacc
    from concourse.bass_utils import run_bass_kernel_spmd

    nc = bacc.Bacc("TRN2", target_bir_lowering=False, num_devices=1)
    arrays, args = {}, []
    for name in _INS:
        a = np.ascontiguousarray(inputs[name])
        arrays["in_" + name] = a
        args.append(nc.dram_tensor("in_" + name, a.shape, F32, kind="ExternalInput").ap())
    out = nc.dram_tensor("out", (B, NP, D), F32, kind="ExternalOutput").ap()
    audio_tower(nc, *args, out)
    r = run_bass_kernel_spmd(nc, [arrays], core_ids=[0])
    return r.results[0]["out"]
```

```python
from contextlib import ExitStack

import concourse.bass as bass
from concourse import mybir

F32 = mybir.dt.float32
F32R = mybir.dt.float32r
BF16 = mybir.dt.bfloat16
I32 = mybir.dt.int32
U32 = mybir.dt.uint32
ALU = mybir.AluOpType
ACT = mybir.ActivationFunctionType
AX = mybir.AxisListType

B, L = 64, 16384
PATCH, HOP = 128, 64
NP = (L - PATCH) // HOP + 1
D = 192
DH = D // 2
MEM = 8
NK = NP + MEM
KW = NK + 1
E, F = 8, 768
G = 16
SPG = B // G
S = SPG * NP
C = int(2 * 1.25 * S / E)
TPG = 2 * SPG
J = 3
CP = C // J
CPP = 112
SLOTS = CPP * J
ROWS = E * SLOTS
FT = F // 128
DW = 256
SCALE = float(D) ** -0.5
EPS = 1e-5
FAR = float(1 << 20)
LAGS = 4


def audio_tower(nc, x, W1, W2, b2, memory, Wq, bq, Wk, bk, Wv, bv, Wo, bo, Wr, wi, wo, out):
    h2_dram = nc.dram_tensor("h2_scratch", (B, 2, 128, D), F32, kind="Internal").ap()
    xs_dram = nc.dram_tensor("slots_in", (2 * ROWS, DW), F32, kind="Internal").ap()
    ys_dram = nc.dram_tensor("slots_out", (2 * ROWS, D), F32, kind="Internal").ap()
    with ExitStack() as both:
        routes = both.enter_context(nc.sbuf_tensor("routes", [128, B * 20], F32))
        ident = both.enter_context(nc.sbuf_tensor("ident", [128, 128], F32))
        with ExitStack() as ctx:
            attention(nc, ctx, x, W1, W2, b2, memory, Wq, bq, Wk, bk, Wv, bv, Wo, bo, Wr,
                      routes, ident, h2_dram, xs_dram, ys_dram)
        with ExitStack() as ctx:
            experts(nc, ctx, wi, wo, routes, ident, h2_dram, xs_dram, ys_dram, out)


def wait(eng, sem, value):
    if isinstance(value, int) and value <= 0:
        return
    eng.wait_ge(sem, value)


def settle(eng, passed):
    eng.sem_inc(passed, 1)


def attention(nc, ctx, x, W1, W2, b2, memory, Wq, bq, Wk, bk, Wv, bv, Wo, bo, Wr,
              routes, ident, h2_dram, xs_dram, ys_dram):
    def sb(name, shape, dt=F32):
        return ctx.enter_context(nc.sbuf_tensor(name, shape, dt))

    def psum(name, shape):
        return ctx.enter_context(nc.psum_tensor(name, shape, F32))

    def sem(name):
        return ctx.enter_context(nc.semaphore(name))

    w1_sb = sb("w1_sb", [DH, 2, PATCH])
    w2_sb = sb("w2_sb", [DH, 2, D])
    wqkv_sb = [sb(f"w{n}_sb", [DH, 2, D]) for n in "qkv"]
    wo_sb = sb("wo_sb", [DH, 2, D])
    w2T = sb("w2T", [DH, 2, D])
    wqkvT = [sb(f"w{n}T", [DH, 2, D + 1]) for n in "qkv"]
    bias_sb = sb("bias_sb", [DH, 3, 2])
    bo_sb = sb("bo_sb", [128, D])
    b2_sb = sb("b2_sb", [128, D])
    wr_sb = sb("wr_sb", [DH, 2, E])
    memT = sb("memT", [128, 2, MEM])
    zero_sb = sb("zero_sb", [128, 2 * DW])
    vo_sb = sb("vo_sb", [128, 2, D])
    w21 = [sb(f"w21_{p}", [128, D], F32R) for p in ("hi", "lo")]
    qk = [sb(f"qk_{p}", [128, 2, D + 1], F32R) for p in ("hi", "lo")]
    vo = [sb(f"vo_{p}", [128, 2, D], F32R) for p in ("hi", "lo")]
    vmem = sb("vmem", [128, D], F32R)
    mem3 = sb("mem3", [128, 2, 128])
    half = sb("half", [128, 2])
    patches = sb("patches", [128, 2, 2, PATCH])
    patchT = [sb(f"patchT_{p}", [128, 256], F32R) for p in ("hi", "lo")]
    h = sb("h", [128, 4, 2, D])
    c = sb("c", [128, 2, D])
    cT = [sb(f"cT_{p}", [128, 2, 2, KW], F32R) for p in ("hi", "lo")]
    qT = [sb(f"qT_{p}", [128, 2, 2, 256], F32R) for p in ("hi", "lo")]
    v = [sb(f"v_{p}", [128, 2, 2, D], F32R) for p in ("hi", "lo")]
    probs = sb("probs", [128, 2, 384])
    probsT = [sb(f"probsT_{p}", [128, n, 256], F32R) for p, n in (("hi", 3), ("lo", 2))]
    h2 = sb("h2", [128, 2, 2, D])
    c2 = sb("c2", [128, 2, D])
    c2T = sb("c2T", [DH, 2, 256])
    stats = sb("stats", [128, 2, 2, 6])
    mv = sb("mv", [128, 2, 2, 2])
    vare = sb("vare", [128, 2, 2])
    nmean = sb("nmean", [128, 2, 2])
    scales = sb("scales", [128, 2, 2, 2])
    peak = sb("peak", [128, 2])
    npeak = sb("npeak", [128, 2])
    total = sb("total", [128, 2, 2])
    rtotal = sb("rtotal", [128, 2])
    ps_h = psum("ps_h", [128, 512])
    ps_q = psum("ps_q", [128, 2, 256])
    ps_c = psum("ps_c", [128, 2, 256])
    ps_v = psum("ps_v", [128, 512])
    ps_s = psum("ps_s", [128, 2, 512])
    ps_p = psum("ps_p", [128, 4, 256])
    ps_x = ps_h[:, 0:256]
    ps_lg = ps_c[:, 0, 0:2 * E]
    ps_o = ps_p[:].rearrange("p k n -> p (k n)")[:, 0:2 * D].rearrange("p (k d) -> p k d", k=2)
    loads = sem("setup_loads")
    zeroed = sem("slots_zeroed")
    pool_set = sem("pool_set")
    weights_tr = sem("weights_transposed")
    weights_cp = sem("weights_copied")
    folded = sem("weights_folded")
    split_hi = sem("folded_split_hi")
    split_lo = sem("folded_split_lo")
    mem_set = sem("memory_keys_set")
    vmem_mm = sem("memory_values_made")
    x_loaded = [sem(f"x_loaded_{i}") for i in range(2)]
    patch_tr = sem("patch_transposed")
    patch_hi = sem("patchT_hi_ready")
    patch_lo = sem("patchT_lo_ready")
    h_mm = sem("tokens_made")
    h_ready = sem("tokens_ready")
    st1 = sem("stats1_ready")
    mv1 = sem("mean_var1_ready")
    sc1 = sem("scales1_steps")
    c_ready = sem("c_ready")
    c_tr = sem("c_transposed")
    cT_hi = sem("cT_hi_ready")
    cT_lo = sem("cT_lo_ready")
    q_mm = sem("q_made")
    q_hi = sem("q_hi_ready")
    q_lo = sem("q_lo_ready")
    v_mm = sem("v_made")
    v_hi = sem("v_hi_ready")
    v_lo = sem("v_lo_ready")
    s_mm = sem("scores_made")
    peak_ready = sem("peak_ready")
    npeak_ready = sem("npeak_ready")
    exp_done = sem("exp_done")
    mem_twice = sem("memory_probs_copied")
    p_tr = sem("probs_transposed")
    pT_hi = sem("probsT_hi_ready")
    pT_lo = sem("probsT_lo_ready")
    pv_mm = sem("attended_made")
    rt_ready = sem("rtotal_ready")
    h2_ready = sem("h2_ready")
    h2_stored = [sem(f"h2_stored_{i}") for i in range(2)]
    st2 = sem("stats2_ready")
    mv2 = sem("mean_var2_ready")
    sc2 = sem("scales2_steps")
    sc_kept = sem("scales_kept")
    c2_ready = sem("c2_ready")
    c2_tr = sem("c2_transposed")
    c2T_ready = sem("c2T_ready")
    lg_mm = sem("logits_made")
    lg_kept = sem("logits_kept")
    dve_passed = sem("vector_waits_passed")
    sp_passed = sem("sync_waits_passed")
    pool_passed = sem("gpsimd_waits_passed")
    NLOADS = 15
    block = ctx.enter_context(nc.Block())

    def rows(w):
        return w.rearrange("(t p) d -> p t d", t=2)

    def all_iterations(eng, body):
        for j in range(4):
            body(0, j, lambda lag: j >= lag)
        for j in range(4):
            body(1, j, lambda lag: True)
        with eng.Fori(2, B // 4) as g:
            for j in range(4):
                body(g, j, lambda lag: True)
        for j in range(LAGS):
            body(B // 4, j, lambda lag: j < lag)

    def turns(g, j, lag):
        return g * 2 + ((j - lag) // 2 + 1)

    @block.sync
    def _(sp):
        sp.dma_start(w1_sb[:], rows(W1)).then_inc(loads, 16)
        sp.dma_start(w2_sb[:], rows(W2)).then_inc(loads, 16)
        for w, d in zip(wqkv_sb, (Wq, Wk, Wv)):
            sp.dma_start(w[:], rows(d)).then_inc(loads, 16)
        sp.dma_start(wo_sb[:], rows(Wo)).then_inc(loads, 16)
        sp.dma_start(wr_sb[:], rows(Wr)).then_inc(loads, 16)
        with nc.allow_non_contiguous_dma(reason="small vectors, once"):
            for i, b in enumerate((bq, bk, bv)):
                sp.dma_start(bias_sb[:, i, :], b.rearrange("(t p) -> p t", t=2)).then_inc(loads, 16)
            for t in range(2):
                sp.dma_start(memT[0:DH, t, :], memory[:, t * DH:(t + 1) * DH].rearrange("m p -> p m")).then_inc(loads, 16)
        sp.dma_start(bo_sb[DH:DH + 1, :], bo.rearrange("(a d) -> a d", a=1)).then_inc(loads, 16)
        sp.dma_start(b2_sb[:], b2.rearrange("(a d) -> a d", a=1).to_broadcast([128, D])).then_inc(loads, 16)
        flats = [slots.rearrange("(n p r) d -> n p (r d)", p=128, r=2) for slots in (xs_dram, ys_dram)]
        zeroes = [flat[n] for n in range(2 * ROWS // 256) for flat in flats]
        share = -(-len(zeroes) // 8)

        def body(g, j, live):
            t = g * 4 + j
            if live(0):
                if not (isinstance(t, int) and t < 2):
                    sp.wait_ge(patch_tr, t - 1)
                for k in range(2):
                    n = 127 if k and isinstance(t, int) and t == B - 1 else 128
                    src = windows(x, t, k * 128, n)
                    settle(sp, sp_passed)
                    sp.dma_start(patches[0:n, j % 2, k, :], src).then_inc(x_loaded[j % 2], 16)
            if isinstance(t, int) and 0 < t <= 8:
                if t == 1:
                    sp.wait_ge(pool_set, 2)
                for part in zeroes[(t - 1) * share:t * share]:
                    sp.dma_start(part, zero_sb[:, 0:part.shape[1]]).then_inc(zeroed, 16)
            if live(3):
                sp.wait_ge(h2_ready, t - 2)
                settle(sp, sp_passed)
                sp.dma_start(h2_dram[t - 3].rearrange("k p d -> p k d"), h2[:, (j + 1) % 2, :, :]) \
                    .then_inc(h2_stored[(j + 1) % 2], 16)

        for j in range(4):
            body(0, j, lambda lag: j >= lag)
        for j in range(4):
            body(1, j, lambda lag: True)
        for j in range(4):
            body(2, j, lambda lag: True)
        with sp.Fori(3, B // 4 - 1) as g:
            for j in range(4):
                body(g, j, lambda lag: True)
        for j in range(4):
            body(B // 4 - 1, j, lambda lag: True)
        for j in range(LAGS):
            body(B // 4, j, lambda lag: j < lag)
        sp.wait_ge(h2_stored[0], 16 * (B // 2))
        sp.wait_ge(h2_stored[1], 16 * (B // 2))
        sp.wait_ge(zeroed, 2 * 16 * (2 * ROWS // 256))

    @block.gpsimd
    def _(pool):
        pool.memset(ident[:], 0.0).then_inc(pool_set, 1)
        pool.memset(zero_sb[:], 0.0).then_inc(pool_set, 1)
        pool.wait_ge(pool_set, 1)
        pool.affine_select(out=ident[:], in_=ident[:], compare_op=ALU.not_equal, fill=1.0, base=0,
                           pattern=[[-1, 128]], channel_multiplier=1).then_inc(pool_set, 1)
        pool.memset(half[:], -0.5).then_inc(pool_set, 1)
        pool.memset(probs[:], 0.0).then_inc(pool_set, 1)
        pool.wait_ge(pool_set, 5)
        pool.memset(memT[DH:DH + 1, :, :], 1.0).then_inc(pool_set, 1)
        pool.wait_ge(pool_set, 6)

        def norm(n, which, mv_ready, done, applied):
            pool.wait_ge(mv_ready, n + 1)
            wait(pool, applied, n)
            settle(pool, pool_passed)
            pool.tensor_scalar(vare[:, which, :], mv[:, which, :, 1], EPS, None, ALU.add)
            pool.tensor_scalar(nmean[:, which, :], mv[:, which, :, 0], -1.0, None, ALU.mult).then_inc(done, 1)
            pool.wait_ge(done, n * 3 + 1)
            pool.tensor_tensor(scales[:, which, :, 0], vare[:, which, :], half[:], ALU.pow).then_inc(done, 1)
            pool.wait_ge(done, n * 3 + 2)
            pool.tensor_tensor(scales[:, which, :, 1], nmean[:, which, :], scales[:, which, :, 0],
                               ALU.mult).then_inc(done, 1)

        def body(g, j, live):
            t = g * 4 + j
            if live(2):
                pool.wait_ge(exp_done, t - 1)
                settle(pool, pool_passed)
                for k in range(2):
                    copies = probs[:, k, 288:352].rearrange("p (i m) -> p i m", i=2)[:, :, 0:MEM - 1]
                    ins = pool.tensor_copy(copies, probs[:, k, 256:NK].unsqueeze(1).to_broadcast([128, 2, MEM - 1]))
                ins.then_inc(mem_twice, 1)
            if live(0):
                norm(t, 0, mv1, sc1, c_ready)
            if live(3):
                n = t - 3
                norm(n, 1, mv2, sc2, c2_ready)
                pool.wait_ge(sc2, n * 3 + 3)
                settle(pool, pool_passed)
                kept = routes[:, bass.ds(n * 20, 20)].rearrange("p (k r) -> p k r", k=2)
                pool.tensor_copy(kept[:, :, E:E + 2], scales[:, 1, :, :]).then_inc(sc_kept, 1)

        all_iterations(pool, body)

    @block.scalar
    def _(act):
        act.wait_ge(weights_tr, 2)
        act.activation(w2T[:], ps_h[0:DH, 0:2 * D].rearrange("p (t d) -> p t d", t=2), ACT.Copy).then_inc(weights_cp, 1)
        act.activation(wqkvT[0][:, :, 0:D], ps_v[0:DH, 0:2 * D].rearrange("p (t d) -> p t d", t=2),
                       ACT.Copy).then_inc(weights_cp, 1)
        act.wait_ge(folded, 3)
        act.activation(w21[0][:], ps_q[:, 0, 0:D], ACT.Copy).then_inc(split_hi, 1)
        for k in range(2):
            n = DH + k
            act.activation(qk[0][0:n, k, 0:D + 1], ps_s[0:n, k, 0:D + 1], ACT.Copy).then_inc(split_hi, 1)
        act.wait_ge(split_lo, 4)
        act.activation(vo[0][0:DH, 0, :], vo_sb[0:DH, 0, :], ACT.Copy).then_inc(split_hi, 1)
        act.activation(vo[0][0:DH + 1, 1, :], vo_sb[0:DH + 1, 1, :], ACT.Copy).then_inc(split_hi, 1)
        act.wait_ge(vmem_mm, 1)
        act.activation(vmem[:], ps_h[:, 0:D], ACT.Copy).then_inc(split_hi, 1)
        act.wait_ge(mem_set, 1)

        def normed(dst, src, which):
            for k in range(2):
                ins = act.activation(dst[:, k, :], src[:, k, :], ACT.Identity, bias=scales[:, which, k, 1:2],
                                     scale=scales[:, which, k, 0:1])
            return ins

        def body(g, j, live):
            t = g * 4 + j
            if live(0):
                n = t
                act.wait_ge(patch_tr, n + 1)
                wait(act, h_mm, n)
                act.activation(patchT[0][:], ps_x, ACT.Copy).then_inc(patch_hi, 1)
            if live(1):
                n = t - 1
                r = (j - 1) % 2
                act.wait_ge(c_tr, n + 1)
                wait(act, s_mm, n - 1)
                act.activation(cT[0][0:DH, r, :, 0:NP], ps_c[0:DH, :, 0:NP], ACT.Copy).then_inc(cT_hi, 1)
            if live(2):
                n = t - 2
                act.wait_ge(npeak_ready, n + 1)
                wait(act, p_tr, n)
                wait(act, rt_ready, n - 1)
                for k in range(2):
                    ins = act.activation(probs[:, k, 0:NK], ps_s[:, k, 0:NK], ACT.Exp, bias=npeak[:, k:k + 1],
                                         scale=SCALE, accum_out=total[:, j % 2, k:k + 1])
                ins.then_inc(exp_done, 1)
            if live(4):
                n = t - 4
                act.wait_ge(c2_tr, n + 1)
                wait(act, lg_mm, n)
                act.activation(c2T[:], ps_c[0:DH, :, :], ACT.Copy).then_inc(c2T_ready, 1)
            if live(1):
                n = t - 1
                act.wait_ge(q_mm, n + 1)
                wait(act, s_mm, n - 1)
                act.activation(qT[0][0:DH + 1, r, :, :], ps_q[0:DH + 1, :, :], ACT.Copy).then_inc(q_hi, 1)
            if live(2):
                n = t - 2
                act.wait_ge(p_tr, n + 1)
                wait(act, pv_mm, n)
                act.activation(probsT[0][:], ps_p[:, 0:3, :], ACT.Copy).then_inc(pT_hi, 1)
            if live(0):
                n = t
                act.wait_ge(sc1, n * 3 + 3)
                wait(act, c_tr, n)
                normed(c, h[:, j], 0).then_inc(c_ready, 1)
            if live(1):
                n = t - 1
                act.wait_ge(v_mm, n + 1)
                wait(act, pv_mm, n - 1)
                act.activation(v[0][:, r, :, :], ps_v[:, 0:2 * D].rearrange("p (t d) -> p t d", t=2),
                               ACT.Copy).then_inc(v_hi, 1)
            if live(3):
                n = t - 3
                act.wait_ge(sc2, n * 3 + 3)
                wait(act, c2_tr, n)
                normed(c2, h2[:, (j + 1) % 2], 1).then_inc(c2_ready, 1)

        all_iterations(act, body)

    @block.vector
    def _(dve):
        dve.wait_ge(weights_tr, 4)
        for i in range(1, 3):
            src = ps_q if i == 1 else ps_c
            for k in range(2):
                ins = dve.tensor_copy(wqkvT[i][:, k, 0:D], src[0:DH, k, 0:D])
        dve.wait_ge(loads, 16 * (NLOADS - 1))
        for i in range(3):
            ins = dve.tensor_copy(wqkvT[i][:, :, D], bias_sb[:, i, :])
        ins.then_inc(weights_cp, 1)
        for k in range(2):
            for r in range(2):
                dve.memset(cT[k][0:DH, r, :, NP:KW].bitcast(F32), 0.0)
                dve.memset(cT[k][DH:DH + 1, r, :, :].bitcast(F32), 1.0 - k)
        dve.memset(mem3[:], 0.0).then_inc(split_lo, 1)
        dve.wait_ge(split_lo, 1)
        dve.wait_ge(pool_set, 6)
        for i in range(3):
            dve.tensor_copy(mem3[0:DH + 1, :, 32 * i:32 * i + MEM - 1], memT[0:DH + 1, :, 1:MEM])
        for r in range(2):
            ins = dve.tensor_copy(cT[0][0:DH, r, :, NP:NK], memT[0:DH, :, :])
        ins.then_inc(split_lo, 1)
        dve.wait_ge(split_lo, 2)
        for r in range(2):
            dve.tensor_tensor(cT[1][0:DH, r, :, NP:NK], memT[0:DH, :, :],
                              cT[0][0:DH, r, :, NP:NK].bitcast(F32), ALU.subtract)
        dve.wait_ge(folded, 4)
        dve.tensor_copy(vo_sb[0:DH, 0, :], ps_h[0:DH, 0:D])
        dve.tensor_copy(vo_sb[0:DH + 1, 1, :], ps_v[0:DH + 1, 0:D]).then_inc(split_lo, 1)
        dve.wait_ge(split_lo, 3)
        dve.tensor_tensor(vo_sb[DH:DH + 1, 1, :], vo_sb[DH:DH + 1, 1, :], bo_sb[DH:DH + 1, :],
                          ALU.add).then_inc(split_lo, 1)
        dve.wait_ge(split_hi, 3)
        dve.tensor_tensor(w21[1][:], ps_q[:, 0, 0:D], w21[0][:].bitcast(F32), ALU.subtract)
        for k in range(2):
            n = DH + k
            dve.tensor_tensor(qk[1][0:n, k, 0:D + 1], ps_s[0:n, k, 0:D + 1],
                              qk[0][0:n, k, 0:D + 1].bitcast(F32), ALU.subtract)
        dve.wait_ge(split_hi, 5)
        for k in range(2):
            n = DH + k
            ins = dve.tensor_tensor(vo[1][0:n, k, :], vo_sb[0:n, k, :], vo[0][0:n, k, :].bitcast(F32), ALU.subtract)
        dve.wait_ge(split_hi, 6)
        ins = dve.tensor_tensor(vmem[64:96, :], ps_h[64:96, 0:D], vmem[64:96, :].bitcast(F32), ALU.subtract)
        ins.then_inc(mem_set, 1)

        def statistics(n, src, which, src_ready, st_ready, mv_ready):
            dve.wait_ge(src_ready, n + 1)
            wait(dve, mv_ready, n)
            for k in range(2):
                ins = dve.bn_stats(stats[:, which, k, :], src[:, k, :])
            ins.then_inc(st_ready, 1)

        def mean_variance(n, which, st_ready, scaled, mv_ready):
            dve.wait_ge(st_ready, n + 1)
            wait(dve, scaled, n * 3)
            settle(dve, dve_passed)
            for k in range(2):
                ins = dve.bn_aggr(mv[:, which, k, :], stats[:, which, k, :])
            ins.then_inc(mv_ready, 1)

        def low(dst, src, hi, hi_ready, lo_ready, n):
            dve.wait_ge(hi_ready, n + 1)
            dve.tensor_tensor(dst, src, hi.bitcast(F32), ALU.subtract).then_inc(lo_ready, 1)

        def body(g, j, live):
            t = g * 4 + j
            if live(0):
                low(patchT[1][:], ps_x, patchT[0][:], patch_hi, patch_lo, t)
            if live(1):
                r = (j - 1) % 2
                low(cT[1][0:DH, r, :, 0:NP], ps_c[0:DH, :, 0:NP], cT[0][0:DH, r, :, 0:NP], cT_hi, cT_lo, t - 1)
            if live(3):
                n = t - 3
                dve.wait_ge(rt_ready, n + 1)
                dve.wait_ge(pv_mm, n + 1)
                if not (isinstance(t, int) and n < 2):
                    dve.wait_ge(h2_stored[(j - 3) % 2], (turns(g, j, 3) - 1) * 16)
                    dve.wait_ge(c2_ready, n - 1)
                for k in range(2):
                    ins = dve.scalar_tensor_tensor(h2[:, (j - 3) % 2, k, :], ps_o[:, k, :], rtotal[:, k:k + 1],
                                                   h[:, (j - 3) % 4, k, :], ALU.mult, ALU.add)
                ins.then_inc(h2_ready, 1)
            if live(0):
                dve.wait_ge(h_mm, t + 1)
                dve.tensor_tensor(h[:, j, :, :], ps_h[:, 0:2 * D].rearrange("p (t d) -> p t d", t=2),
                                  b2_sb[:].rearrange("p (a d) -> p a d", a=1).to_broadcast([128, 2, D]),
                                  ALU.add).then_inc(h_ready, 1)
            if live(3):
                statistics(t - 3, h2[:, (j - 3) % 2], 1, h2_ready, st2, mv2)
            if live(0):
                statistics(t, h[:, j], 0, h_ready, st1, mv1)
            if live(2):
                n = t - 2
                dve.wait_ge(exp_done, n + 1)
                wait(dve, h2_ready, n)
                dve.reciprocal(rtotal[:], total[:, j % 2, :]).then_inc(rt_ready, 1)
            if live(0):
                mean_variance(t, 0, st1, sc1, mv1)
            if live(3):
                mean_variance(t - 3, 1, st2, sc2, mv2)
            if live(1):
                low(qT[1][0:DH + 1, r, :, :], ps_q[0:DH + 1, :, :], qT[0][0:DH + 1, r, :, :], q_hi, q_lo, t - 1)
            if live(4):
                n = t - 4
                dve.wait_ge(lg_mm, n + 1)
                kept = routes[:, bass.ds(n * 20, 20)].rearrange("p (k r) -> p k r", k=2)
                dve.tensor_copy(kept[:, :, 0:E], ps_lg.rearrange("p (k e) -> p k e", k=2)).then_inc(lg_kept, 1)
            if live(2):
                dve.wait_ge(pT_hi, t - 1)
                low3 = probsT[0][32:64, 2, :]
                dve.tensor_tensor(low3, ps_p[32:64, 2, :], low3.bitcast(F32), ALU.subtract)
                low(probsT[1][:], ps_p[:, 0:2, :], probsT[0][:, 0:2, :], pT_hi, pT_lo, t - 2)
            if live(1):
                n = t - 1
                low(v[1][:, r, :, :], ps_v[:, 0:2 * D].rearrange("p (t d) -> p t d", t=2), v[0][:, r, :, :],
                    v_hi, v_lo, n)
                dve.wait_ge(s_mm, n + 1)
                dve.tensor_reduce(peak[:], ps_s[:, :, 0:NK], AX.X, ALU.max).then_inc(peak_ready, 1)
                dve.wait_ge(peak_ready, n + 1)
                wait(dve, exp_done, n)
                dve.tensor_scalar(npeak[:], peak[:], -SCALE, None, ALU.mult).then_inc(npeak_ready, 1)

        all_iterations(dve, body)

    @block.tensor
    def _(pe):
        pe.wait_ge(loads, 16 * (NLOADS - 1))
        pe.wait_ge(pool_set, 6)
        for w, bank in ((w2_sb, ps_h), (wqkv_sb[0], ps_v), (wqkv_sb[1], ps_q), (wqkv_sb[2], ps_c)):
            for k in range(2):
                for i in range(2):
                    dst = bank[0:DH, k * D + i * DH:k * D + (i + 1) * DH] if bank in (ps_h, ps_v) \
                        else bank[0:DH, k, i * DH:(i + 1) * DH]
                    ins = pe.transpose(dst, w[:, i, k * DH:(k + 1) * DH], ident[0:DH, 0:DH])
            ins.then_inc(weights_tr, 1)
        pe.wait_ge(weights_cp, 3)
        for k in range(2):
            ins = pe.matmul(ps_q[:, 0, 0:D], w1_sb[:, k, :], w2T[:, k, :], start=(k == 0), stop=(k == 1))
        ins.then_inc(folded, 1)
        for i in range(2):
            n = DH + i
            for k in range(2):
                ins = pe.matmul(ps_s[0:n, i, 0:D + 1], wqkvT[0][:, k, i * DH:i * DH + n], wqkvT[1][:, k, :],
                                start=(k == 0), stop=(k == 1))
            ins.then_inc(folded, 1)
        for i in range(2):
            n = DH + i
            for k in range(2):
                ins = pe.matmul((ps_v if i else ps_h)[0:n, 0:D], wqkvT[2][:, k, i * DH:i * DH + n], wo_sb[:, k, :],
                                start=(k == 0), stop=(k == 1))
        ins.then_inc(folded, 1)
        pe.wait_ge(split_lo, 4)
        for k in range(2):
            n = DH + k
            ins = pe.matmul(ps_h[:, 0:D], mem3[0:n, k, :], vo_sb[0:n, k, :], start=(k == 0), stop=(k == 1))
        ins.then_inc(vmem_mm, 1)
        pe.wait_ge(mem_set, 1)
        pe.wait_ge(split_hi, 6)

        PASSES = ((0, 0), (0, 1), (1, 0))

        def product(dst, terms, first=True):
            n = 0
            for stationary, moving in terms:
                for a, b in PASSES:
                    ins = pe.matmul(dst, stationary[a], moving[b], start=(first and n == 0),
                                    stop=(n == 3 * len(terms) - 1))
                    n += 1
            return ins

        def pair(two, *index):
            return [part[index] for part in two]

        def body(g, j, live):
            t = g * 4 + j
            if live(0):
                n = t
                pe.wait_ge(x_loaded[j % 2], turns(g, j, 0) * 32)
                wait(pe, h_ready, n)
                for k in range(2):
                    ins = pe.transpose(ps_x[:, k * 128:(k + 1) * 128], patches[:, j % 2, k, :], ident[:])
                ins.then_inc(patch_tr, 1)
            if live(1):
                n = t - 1
                pe.wait_ge(c_ready, n + 1)
                wait(pe, lg_kept, n - 3)
                for i in range(2):
                    for k in range(2):
                        ins = pe.transpose(ps_c[0:DH, i, k * 128:(k + 1) * 128], c[:, k, i * DH:(i + 1) * DH], ident[:])
                ins.then_inc(c_tr, 1)
            if live(3):
                n = t - 3
                r = (j - 3) % 2
                pe.wait_ge(pT_lo, n + 1)
                pe.wait_ge(v_lo, n + 1)
                for k in range(2):
                    q = slice(k * 128, (k + 1) * 128)
                    pe.matmul(ps_o[:, k, :], probsT[0][:, 2, q], vmem[:], start=True, stop=False)
                    ins = product(ps_o[:, k, :],
                                  [(pair(probsT, slice(0, 128), i, q), pair(v, slice(0, 128), r, i, slice(0, D)))
                                   for i in range(2)], first=False)
                ins.then_inc(pv_mm, 1)
            if live(0):
                n = t
                pe.wait_ge(patch_lo, n + 1)
                for k in range(2):
                    ins = product(ps_h[:, k * D:(k + 1) * D],
                                  [(pair(patchT, slice(0, 128), slice(k * 128, (k + 1) * 128)),
                                    pair(w21, slice(0, 128), slice(0, D)))])
                ins.then_inc(h_mm, 1)
            if live(4):
                n = t - 4
                pe.wait_ge(c2_ready, n + 1)
                if live(1):
                    pe.wait_ge(cT_lo, t)
                else:
                    pe.wait_ge(lg_kept, n)
                for i in range(2):
                    for k in range(2):
                        ins = pe.transpose(ps_c[0:DH, i, k * 128:(k + 1) * 128], c2[:, k, i * DH:(i + 1) * DH], ident[:])
                ins.then_inc(c2_tr, 1)
            if live(1):
                n = t - 1
                r = (j - 1) % 2
                pe.wait_ge(cT_lo, n + 1)
                wait(pe, q_lo, n)
                for o in range(2):
                    m = DH + 1
                    ins = product(ps_q[0:m, o, :],
                                  [(pair(qk, slice(0, DH + i), i, slice(o * DH, o * DH + m)),
                                    pair(cT, slice(0, DH + i), r, i, slice(0, 256))) for i in range(2)])
                ins.then_inc(q_mm, 1)
            if live(4):
                n = t - 4
                pe.wait_ge(c2T_ready, n + 1)
                for k in range(2):
                    for i in range(2):
                        ins = pe.matmul(ps_lg[:, k * E:(k + 1) * E], c2T[:, i, k * 128:(k + 1) * 128], wr_sb[:, i, :],
                                        start=(i == 0), stop=(i == 1))
                ins.then_inc(lg_mm, 1)
            if live(2):
                n = t - 2
                pe.wait_ge(mem_twice, n + 1)
                wait(pe, h2_ready, n)
                for i in range(3):
                    for k in range(2):
                        ins = pe.transpose(ps_p[:, i, k * 128:(k + 1) * 128], probs[:, k, i * 128:(i + 1) * 128], ident[:])
                ins.then_inc(p_tr, 1)
            if live(1):
                n = t - 1
                r = (j - 1) % 2
                wait(pe, v_lo, n)
                for k in range(2):
                    ins = product(ps_v[:, k * D:(k + 1) * D],
                                  [(pair(cT, slice(0, DH + i), r, i, slice(k * 128, (k + 1) * 128)),
                                    pair(vo, slice(0, DH + i), i, slice(0, D))) for i in range(2)])
                ins.then_inc(v_mm, 1)
            if live(1):
                n = t - 1
                r = (j - 1) % 2
                pe.wait_ge(q_lo, n + 1)
                wait(pe, exp_done, n)
                for k in range(2):
                    ins = product(ps_s[:, k, 0:KW],
                                  [(pair(qT, slice(0, DH + i), r, i, slice(k * 128, (k + 1) * 128)),
                                    pair(cT, slice(0, DH + i), r, i, slice(0, KW))) for i in range(2)])
                ins.then_inc(s_mm, 1)

        all_iterations(pe, body)


def windows(x, s, first, count):
    return bass.AP(x.tensor, s * L + first * HOP, [[HOP, count], [1, PATCH]])


def experts(nc, ctx, wi, wo, routes, ident, h2_dram, xs_dram, ys_dram, out):
    def sb(name, shape, dt=F32):
        return ctx.enter_context(nc.sbuf_tensor(name, shape, dt))

    def psum(name, shape):
        return ctx.enter_context(nc.psum_tensor(name, shape, F32))

    def sem(name):
        return ctx.enter_context(nc.semaphore(name))

    PARTS = ("hi", "lo")
    wi_main = [sb(f"wi_main_{p}", [128, E, F], F32R) for p in PARTS]
    wi_rest = sb("wi_rest", [128, E, F], F32R)
    wo_sb = [sb(f"wo_{p}", [128, E, FT, D], F32R) for p in PARTS]
    xrow = sb("xrow", [CPP, 2, J, DW])
    xmain = [sb(f"xmain_{p}", [128, C], F32R) for p in PARTS]
    xrest = [sb(f"xrest_{p}", [128, C], F32R) for p in PARTS]
    hid = [sb(f"hid_{p}", [128, FT, C], F32R) for p in PARTS]
    yrow = sb("yrow", [CPP, 2, J, D])
    send = sb("send", [128, TPG, DW])
    rt = sb("rt", [128, TPG, E + 2])
    expo = sb("expo", [128, TPG, E])
    tokmax = sb("tokmax", [128, TPG])
    toksum = sb("toksum", [128, TPG])
    top = sb("top", [128, TPG, 8])
    topi = sb("topi", [128, TPG, 8], U32)
    chosen = sb("chosen", [128, 2, TPG])
    gate = sb("gate", [128, 2, TPG])
    mask = sb("mask", [128, 2, TPG, E], BF16)
    scan = [sb(f"scan_{i}", [128, 24, E]) for i in range(2)]
    pos = sb("pos", [128, 16, E])
    sel = sb("sel", [128, 16])
    ok = sb("ok", [128, 16])
    slot = sb("slot", [128, 16])
    miss = sb("miss", [128, 16])
    send_idx = sb("send_idx", [128, 16], I32)
    ret_new = sb("ret_new", [128, 2, 16], I32)
    ret_mid = sb("ret_mid", [128, 2, 16], I32)
    ret_use = sb("ret_use", [128, 2, 16], I32)
    ring = sb("ring", [128, 1])
    before = sb("before", [128, 128], BF16)
    ones = sb("ones", [128, 128], BF16)
    which = sb("which", [128, TPG, E])
    whichi = sb("whichi", [128, TPG * E], I32)
    far = sb("far", [128, 2, TPG])
    area = sb("area", [128, 16 * D])
    raw_main = area[:, 0:F]
    raw_rest = area[:, F:2 * F]
    raw_wo = area[:, 2 * F:2 * F + FT * D].rearrange("p (f d) -> p f d", f=FT)
    back = area[:, 0:TPG * D].rearrange("p (t d) -> p t d", t=TPG)
    got = area[:, TPG * D:16 * D].rearrange("p (r k d) -> p r k d", r=4, k=2)
    ps_x = psum("ps_xT", [128, 2, 512])
    ps_h = psum("ps_hid", [128, 3, 512])
    ps_y = psum("ps_y", [128, 2, 512])
    ps_r = psum("ps_route", [128, 2, 256])
    consts = sem("consts_set")
    w_in = sem("raw_weights_in")
    w_hi = sem("weights_hi_ready")
    w_lo = sem("weights_lo_ready")
    w_rest = sem("wi_rest_lo_ready")
    x_in = [sem(f"xrow_in_{i}") for i in range(2)]
    x_tr = sem("x_transposed")
    x_hi = sem("xT_hi_ready")
    x_lo = sem("xT_lo_ready")
    h_mm = sem("hidden_made")
    h_hi = sem("hidden_hi_ready")
    h_lo = sem("hidden_lo_ready")
    y_mm = sem("y_made")
    y_act = sem("y_third_copied")
    y_dve = sem("y_first_two_copied")
    y_out = [sem(f"y_stored_{i}") for i in range(2)]
    send_in = sem("send_in")
    route = sem("route_steps")
    exp_done = sem("route_exp_done")
    mask_ready = sem("mask_ready")
    count_mm = sem("counts_made")
    send_ready = sem("send_ready")
    idx_ready = sem("indices_ready")
    twice = sem("last_features_doubled")
    sent = sem("sent")
    use_ready = sem("return_indices_ready")
    fetched = [sem(f"fetched_{i}") for i in range(4)]
    back_in = sem("back_in")
    comb_half = sem("first_expert_added")
    comb = sem("second_expert_added")
    out_done = sem("out_stored")
    ret_moved = sem("return_indices_moved")
    dve_passed = sem("vector_passed")
    sp_passed = sem("sync_passed")
    pool_passed = sem("gpsimd_passed")
    STEPS = 22
    block = ctx.enter_context(nc.Block())

    def all_groups(eng, body):
        body(0, False, True, True)
        body(1, True, True, True)
        with eng.Fori(2, G - 1) as g:
            body(g, True, True, True)
        body(G - 1, True, True, False)
        body(G, True, False, False)

    @block.sync
    def _(sp):
        def load_x(g, e):
            if e < 2:
                sp.wait_ge(sent, (g + 1) * 256)
            if not (isinstance(g, int) and g == 0 and e < 2):
                sp.wait_ge(x_tr, g * E + (e - 1))
            first = (g % 2) * ROWS + e * SLOTS
            settle(sp, sp_passed)
            sp.dma_start(xrow[:, e % 2, :, :].rearrange("p j d -> p (j d)"),
                         xs_dram[bass.ds(first, SLOTS), :].rearrange("(p j) d -> p (j d)", j=J)) \
                .then_inc(x_in[e % 2], 16)

        def load_weights(e):
            if e:
                sp.wait_ge(w_lo, e)
                sp.wait_ge(w_rest, e)
            sp.dma_start(raw_main, wi[e, 0:128, :]).then_inc(w_in, 16)
            for half in range(2):
                sp.dma_start(raw_rest[64 * half:64 * half + 64, :], wi[e, 128:192, :]).then_inc(w_in, 16)
            sp.dma_start(raw_wo, wo[e].rearrange("(f p) d -> p f d", p=128)).then_inc(w_in, 16)

        def load_send(g):
            if not (isinstance(g, int) and g == 0):
                sp.wait_ge(sent, g * 256)
            settle(sp, sp_passed)
            sp.dma_start(send[:, :, 0:D], h2_dram[bass.ds(g * SPG, SPG)].rearrange("s k p d -> p (s k) d")) \
                .then_inc(send_in, 16)

        load_weights(0)
        load_send(0)
        load_x(0, 0)
        load_x(0, 1)

        def body(g, prev, cur, nxt):
            if nxt:
                load_send(g + 1)
            if prev:
                if isinstance(g, int):
                    wait(sp, w_lo, E)
                else:
                    sp.wait_ge(w_lo, E)
                wait(sp, out_done, (g - 1) * (16 * 3 * SPG))
                settle(sp, sp_passed)
                sp.dma_start(back, h2_dram[bass.ds((g - 1) * SPG, SPG)].rearrange("s k p d -> p (s k) d")) \
                    .then_inc(back_in, 16)
            for e in range(E):
                if cur:
                    if isinstance(g, int) and g == 0 and e + 1 < E:
                        load_weights(e + 1)
                    if e + 2 < E:
                        load_x(g, e + 2)
                    elif nxt:
                        load_x(g + 1, e + 2 - E)
                    sp.wait_ge(y_act, g * E + (e + 1))
                    settle(sp, sp_passed)
                    sp.wait_ge(y_dve, g * E + (e + 1))
                    settle(sp, sp_passed)
                    if not (isinstance(g, int) and g < 2):
                        sp.wait_ge(comb, (g - 1) * TPG)
                    first = (g % 2) * ROWS + e * SLOTS
                    settle(sp, sp_passed)
                    sp.dma_start(ys_dram[bass.ds(first, SLOTS), :].rearrange("(p j) d -> p (j d)", j=J),
                                 yrow[:, e % 2, :, :].rearrange("p j d -> p (j d)")).then_inc(y_out[e % 2], 16)
                if prev and e in STORES:
                    for s in STORES[e]:
                        sp.wait_ge(comb, (g - 1) * TPG + (2 * s + 2))
                        settle(sp, sp_passed)
                        b = (g - 1) * SPG + s
                        sp.dma_start(out[bass.ds(b, 1), 0:128, :].rearrange("b p d -> p (b d)"), back[:, 2 * s, :]) \
                            .then_inc(out_done, 16)
                        for lo, hi in ((0, 112), (112, 127)):
                            sp.dma_start(out[bass.ds(b, 1), 128 + lo:128 + hi, :].rearrange("b p d -> p (b d)"),
                                         back[lo:hi, 2 * s + 1, :]).then_inc(out_done, 16)

        all_groups(sp, body)
        sp.wait_ge(out_done, G * 16 * 3 * SPG)

    @block.gpsimd
    def _(pool):
        n = [0]

        def mark(ins):
            n[0] += 1
            ins.then_inc(consts, 1)

        mark(pool.memset(before[:], 1.0))
        mark(pool.memset(ones[:], 1.0))
        mark(pool.memset(far[:], FAR))
        mark(pool.iota(whichi[:], pattern=[[0, TPG], [1, E]], base=0, channel_multiplier=0))
        pool.wait_ge(consts, n[0])
        mark(pool.memset(yrow[:], 0.0))
        pool.wait_ge(consts, n[0])
        mark(pool.memset(ring[:], float(ROWS)))
        for s in scan:
            mark(pool.memset(s[:, 0:9, :], 0.0))
        pool.wait_ge(consts, n[0])
        mark(pool.affine_select(out=before[:], in_=before[:], compare_op=ALU.is_gt, fill=0.0, base=0,
                                pattern=[[1, 128]], channel_multiplier=-1))
        oddfar = far[:].rearrange("p k (s o) -> p k s o", o=2)[:, :, :, 1]
        mark(pool.affine_select(out=oddfar, in_=oddfar, compare_op=ALU.is_gt, fill=2 * FAR, base=127,
                                pattern=[[0, 2], [0, SPG]], channel_multiplier=-1))
        mark(pool.tensor_copy(which[:].rearrange("p t e -> p (t e)"), whichi[:]))
        pool.wait_ge(consts, n[0])
        oddwhich = which[:].rearrange("p (s o) e -> p s o e", o=2)[:, :, 1, :]
        mark(pool.affine_select(out=oddwhich, in_=oddwhich, compare_op=ALU.is_gt, fill=100.0, base=127,
                                pattern=[[0, SPG], [0, E]], channel_multiplier=-1))
        assert n[0] == NCONSTS

        def low_weights(e):
            pool.wait_ge(w_hi, e + 1)
            pool.tensor_tensor(wi_main[1][:, e, :], raw_main, wi_main[0][:, e, :].bitcast(F32), ALU.subtract)
            pool.tensor_tensor(wo_sb[1][:, e, :, :], raw_wo, wo_sb[0][:, e, :, :].bitcast(F32),
                               ALU.subtract).then_inc(w_lo, 1)

        def dispatch(g):
            pool.wait_ge(send_ready, g + 1)
            settle(pool, pool_passed)
            pool.tensor_copy(send[:, :, D:DW], send[:, :, 128:D]).then_inc(twice, 1)
            pool.wait_ge(twice, g + 1)
            pool.wait_ge(idx_ready, g + 1)
            if not (isinstance(g, int) and g < 2):
                for i in range(2):
                    pool.wait_ge(x_in[i], (g - 1) * (16 * E // 2))
            settle(pool, pool_passed)
            for t in range(TPG):
                for k in range(2):
                    i = k * TPG + t
                    pool.indirect_dma_start(xs_dram, bass.IndirectOffsetOnAxis(ap=send_idx[:, i:i + 1], axis=0),
                                            send[:, t, :], None, bounds_check=2 * ROWS - 1, oob_is_err=False) \
                        .then_inc(sent, 16)

        def fetch(g, t):
            if t == 0:
                pool.wait_ge(use_ready, g + 1)
                for i in range(2):
                    pool.wait_ge(y_out[i], (g + 1) * (16 * E // 2))
                pool.wait_ge(w_lo, E)
            if t >= 4 or not (isinstance(g, int) and g == 0):
                pool.wait_ge(comb, g * TPG + (t - 3))
            settle(pool, pool_passed)
            for k in range(2):
                i = k * TPG + t
                pool.indirect_dma_start(got[:, t % 4, k, :], None, ys_dram,
                                        bass.IndirectOffsetOnAxis(ap=ret_use[:, 0, i:i + 1], axis=0),
                                        bounds_check=2 * ROWS - 1, oob_is_err=False).then_inc(fetched[t % 4], 16)

        low_weights(0)
        dispatch(0)

        def body(g, prev, cur, nxt):
            if prev:
                for t in range(4):
                    fetch(g - 1, t)
            if isinstance(g, int) and g == 0:
                for e in range(1, 4):
                    low_weights(e)
            if nxt:
                dispatch(g + 1)
            if isinstance(g, int) and g == 0:
                for e in range(4, E):
                    low_weights(e)
            if prev:
                for t in range(4, 8):
                    fetch(g - 1, t)

        all_groups(pool, body)

    @block.scalar
    def _(act):
        def high_weights(e):
            act.wait_ge(w_in, 64 * (e + 1))
            act.activation(wi_main[0][:, e, :], raw_main, ACT.Copy)
            act.activation(wi_rest[:, e, :], raw_rest, ACT.Copy)
            act.activation(wo_sb[0][:, e, :, :], raw_wo, ACT.Copy).then_inc(w_hi, 1)

        def high_x(g, e):
            act.wait_ge(x_tr, g * E + (e + 1))
            act.activation(xmain[0][:], ps_x[:, 0, 0:C], ACT.Copy)
            act.activation(xrest[0][:], ps_x[:, 1, 0:C], ACT.Copy).then_inc(x_hi, 1)

        def exponentials(g):
            act.wait_ge(route, g * STEPS + 3)
            act.activation(expo[:], expo[:], ACT.Exp).then_inc(exp_done, 1)

        high_weights(0)
        exponentials(0)
        act.wait_ge(consts, NCONSTS)
        high_x(0, 0)

        def body(g, prev, cur, nxt):
            for e in range(E):
                if cur:
                    wait(act, y_mm, g * (2 * E) + 2 * e)
                    for f in range(FT):
                        act.wait_ge(h_mm, g * (FT * E) + (FT * e + f + 1))
                        act.activation(hid[0][:, f, :], ps_h[:, f % 3, 0:C], ACT.Relu).then_inc(h_hi, 1)
                    if isinstance(g, int) and g == 0 and e + 1 < E:
                        high_weights(e + 1)
                    if e + 1 < E:
                        high_x(g, e + 1)
                    elif nxt:
                        high_x(g + 1, 0)
                    act.wait_ge(y_mm, g * (2 * E) + (2 * e + 2))
                    if not (isinstance(g, int) and g == 0 and e < 2):
                        act.wait_ge(y_out[e % 2], g * (16 * E // 2) + 16 * (e // 2))
                    act.activation(yrow[0:CP, e % 2, 2, :], ps_y[0:CP, 1, 0:D], ACT.Copy).then_inc(y_act, 1)
                if nxt and e == 0:
                    exponentials(g + 1)

        all_groups(act, body)

    @block.vector
    def _(dve):
        def low_weights(e):
            dve.wait_ge(w_hi, e + 1)
            lower = wi_rest[64:128, e, :]
            dve.tensor_tensor(lower, raw_rest[64:128, :], lower.bitcast(F32), ALU.subtract).then_inc(w_rest, 1)

        def low_x(g, e):
            dve.wait_ge(x_hi, g * E + (e + 1))
            dve.tensor_tensor(xmain[1][:], ps_x[:, 0, 0:C], xmain[0][:].bitcast(F32), ALU.subtract)
            dve.tensor_tensor(xrest[1][:], ps_x[:, 1, 0:C], xrest[0][:].bitcast(F32), ALU.subtract).then_inc(x_lo, 1)

        def spread(ap, n):
            return ap.unsqueeze(len(ap.shape)).to_broadcast(list(ap.shape) + [n])

        def step(g, i, ins, go_on=False):
            ins.then_inc(route, 1)
            if not go_on:
                dve.wait_ge(route, g * STEPS + i)
                if i == 6:
                    settle(dve, dve_passed)

        def route_logits(g):
            step(g, 1, dve.tensor_copy(rt[:].rearrange("p t r -> p (t r)"), routes[:, bass.ds(g * 80, 80)]))
            step(g, 2, dve.tensor_reduce(tokmax[:], rt[:, :, 0:E], AX.X, ALU.max))
            step(g, 3, dve.tensor_tensor(expo[:], rt[:, :, 0:E], spread(tokmax[:], E), ALU.subtract), True)

        def normed(g, tiles):
            dve.wait_ge(route, g * STEPS + 1)
            dve.wait_ge(send_in, (g + 1) * 16)
            for t in tiles:
                ins = dve.tensor_scalar(send[:, t, 0:D], send[:, t, 0:D], rt[:, t, E:E + 1], rt[:, t, E + 1:E + 2],
                                        ALU.mult, ALU.add)
            return ins

        def route_choice(g):
            dve.wait_ge(exp_done, g + 1)
            step(g, 4, dve.tensor_reduce(toksum[:], expo[:], AX.X, ALU.add))
            step(g, 5, dve.reciprocal(toksum[:], toksum[:]), True)
            for t in range(TPG):
                ins = dve.max(top[:, t, :], expo[:, t, :])
            step(g, 6, ins)
            for t in range(TPG):
                ins = dve.max_index(topi[:, t, :], top[:, t, :], expo[:, t, :])
            step(g, 7, ins)
            for k in range(2):
                dve.tensor_tensor(gate[:, k, :], top[:, :, k], toksum[:], ALU.mult)
            step(g, 8, dve.tensor_copy(chosen[:].rearrange("p k t -> p t k"), topi[:, :, 0:2]))
            for k in range(2):
                ins = dve.tensor_tensor(mask[:, k, :, :], which[:], spread(chosen[:, k, :], E), ALU.is_equal)
            ins.then_inc(mask_ready, 1)

        def route_slots(g):
            dve.wait_ge(count_mm, g + 1)
            tot = ps_r[:, 1, 0:128].rearrange("p (b e) -> p b e", e=E)
            step(g, 9, dve.tensor_copy(scan[0][:, 9:24, :], tot[:, 0:15, :]))
            for i, d in enumerate((1, 2, 4, 8)):
                src, dst = scan[i % 2], scan[1 - i % 2]
                step(g, 10 + i, dve.tensor_tensor(dst[:, 8:24, :], src[:, 8:24, :], src[:, 8 - d:24 - d, :], ALU.add))
            step(g, 14, dve.tensor_tensor(pos[:], ps_r[:, 0, 0:128].rearrange("p (b e) -> p b e", e=E),
                                          scan[0][:, 8:24, :], ALU.add))
            m = mask[:].rearrange("p k t e -> p (k t) e")
            step(g, 15, dve.tensor_tensor(pos[:], pos[:], m, ALU.mult))
            step(g, 16, dve.tensor_reduce(sel[:], pos[:], AX.X, ALU.add))
            step(g, 17, dve.tensor_scalar(ok[:], sel[:], float(C), None, ALU.is_lt), True)
            step(g, 18, dve.scalar_tensor_tensor(slot[:], chosen[:].rearrange("p k t -> p (k t)"), float(SLOTS),
                                                 sel[:], ALU.mult, ALU.add), True)
            step(g, 19, dve.tensor_scalar(ring[:], ring[:], -1.0, float(ROWS), ALU.mult, ALU.add))
            step(g, 20, dve.tensor_tensor(slot[:], slot[:], ok[:], ALU.mult), True)
            step(g, 21, dve.scalar_tensor_tensor(miss[:], ok[:], -FAR, far[:].rearrange("p k t -> p (k t)"),
                                                 ALU.mult, ALU.add))
            if not (isinstance(g, int) and g == 0):
                dve.wait_ge(sent, g * 256)
            dve.tensor_scalar(ret_new[:, 0, :], slot[:], ring[:, 0:1], None, ALU.add)
            dve.tensor_tensor(ret_new[:, 1, :].bitcast(F32), gate[:].rearrange("p k t -> p (k t)"), ok[:],
                              ALU.mult).then_inc(route, 1)
            dve.scalar_tensor_tensor(send_idx[:], slot[:], ring[:, 0:1], miss[:], ALU.add, ALU.add) \
                .then_inc(idx_ready, 1)

        def add_expert(g, t):
            if t == 0:
                dve.wait_ge(back_in, (g + 1) * 16)
                dve.wait_ge(use_ready, g + 1)
            dve.wait_ge(fetched[t % 4], g * 64 + (32 * (t // 4) + 32))
            for k, done in ((0, comb_half), (1, comb)):
                i = k * TPG + t
                dve.scalar_tensor_tensor(back[:, t, :], got[:, t % 4, k, :], ret_use[:, 1, i:i + 1].bitcast(F32),
                                         back[:, t, :], ALU.mult, ALU.add).then_inc(done, 1)
                dve.wait_ge(done, g * TPG + (t + 1))

        dve.wait_ge(consts, NCONSTS)
        route_logits(0)
        normed(0, range(TPG)).then_inc(send_ready, 1)
        route_choice(0)
        route_slots(0)
        low_weights(0)
        low_x(0, 0)

        def body(g, prev, cur, nxt):
            if prev:
                dve.tensor_copy(ret_use[:], ret_mid[:]).then_inc(use_ready, 1)
                dve.wait_ge(use_ready, g)
            if cur:
                dve.wait_ge(route, (g + 1) * STEPS)
                dve.tensor_copy(ret_mid[:], ret_new[:]).then_inc(ret_moved, 1)
                dve.wait_ge(ret_moved, g + 1)
            for e in range(E):
                if cur:
                    for f in range(FT):
                        dve.wait_ge(h_hi, g * (FT * E) + (FT * e + f + 1))
                        dve.scalar_tensor_tensor(hid[1][:, f, :], ps_h[:, f % 3, 0:C], 0.0,
                                                 hid[0][:, f, :].bitcast(F32), ALU.max, ALU.subtract).then_inc(h_lo, 1)
                    if isinstance(g, int) and g == 0 and e + 1 < E:
                        low_weights(e + 1)
                    if e + 1 < E:
                        low_x(g, e + 1)
                    elif nxt:
                        low_x(g + 1, 0)
                if nxt:
                    if e == 0:
                        route_logits(g + 1)
                        normed(g + 1, range(0, 4))
                    if e == 1:
                        route_choice(g + 1)
                    if e == 2:
                        normed(g + 1, range(4, 8)).then_inc(send_ready, 1)
                    if e == 3:
                        route_slots(g + 1)
                if prev:
                    for t in ADDS[e]:
                        add_expert(g - 1, t)
                if cur:
                    dve.wait_ge(y_mm, g * (2 * E) + (2 * e + 1))
                    if not (isinstance(g, int) and g == 0 and e < 2):
                        dve.wait_ge(y_out[e % 2], g * (16 * E // 2) + 16 * (e // 2))
                    dve.tensor_copy(yrow[0:CP, e % 2, 0:2, :].rearrange("p j d -> p (j d)"),
                                    ps_y[0:CP, 0, 0:2 * D]).then_inc(y_dve, 1)

        all_groups(dve, body)

    @block.tensor
    def _(pe):
        pe.wait_ge(consts, NCONSTS)
        PASSES = ((0, 0), (0, 1), (1, 0))

        def transpose_x(g, e):
            pe.wait_ge(x_in[e % 2], g * (16 * E // 2) + 16 * (e // 2 + 1))
            if not (isinstance(g, int) and g == 0 and e == 0):
                pe.wait_ge(x_lo, g * E + e)
            for j in range(J):
                for part in range(2):
                    ins = pe.transpose(ps_x[:, part, j * CP:(j + 1) * CP],
                                       xrow[0:CP, e % 2, j, part * 128:(part + 1) * 128], ident[0:CP, 0:CP])
            ins.then_inc(x_tr, 1)

        def count(g):
            pe.wait_ge(mask_ready, g + 1)
            m = mask[:].rearrange("p k t e -> p (k t e)")
            pe.matmul(ps_r[:, 0, 0:128], before[:], m, start=True, stop=True)
            pe.matmul(ps_r[:, 1, 0:128], ones[:], m, start=True, stop=True).then_inc(count_mm, 1)

        count(0)
        transpose_x(0, 0)

        def body(g, prev, cur, nxt):
            if not cur:
                return
            for e in range(E):
                first = isinstance(g, int) and g == 0
                pe.wait_ge(x_lo, g * E + (e + 1))
                if first:
                    pe.wait_ge(w_lo, e + 1)
                    pe.wait_ge(w_rest, e + 1)
                for f in range(FT):
                    if not (first and e == 0 and f < 3):
                        pe.wait_ge(h_lo, g * (FT * E) + (FT * e + f - 2))
                    cols = slice(f * 128, (f + 1) * 128)
                    rest = wi_rest[:, e, cols]
                    terms = [(wi_main[a][:, e, cols], xmain[b]) for a, b in PASSES] + [(rest, part) for part in xrest]
                    for n, (w, xx) in enumerate(terms):
                        ins = pe.matmul(ps_h[:, f % 3, 0:C], w, xx[:], start=(n == 0), stop=(n == len(terms) - 1))
                    ins.then_inc(h_mm, 1)
                if e + 1 < E:
                    transpose_x(g, e + 1)
                elif nxt:
                    transpose_x(g + 1, 0)
                if nxt and e == 2:
                    count(g + 1)
                if not (first and e == 0):
                    pe.wait_ge(y_act, g * E + e)
                    pe.wait_ge(y_dve, g * E + e)
                for j in range(J):
                    for f in range(FT):
                        if j == 0:
                            pe.wait_ge(h_lo, g * (FT * E) + (FT * e + f + 1))
                        for n, (a, b) in enumerate(PASSES):
                            ins = pe.matmul(ps_y[0:CP, j // 2, j % 2 * D:(j % 2 + 1) * D], hid[a][:, f, j * CP:(j + 1) * CP], wo_sb[b][:, e, f, :],
                                            start=(f == 0 and n == 0), stop=(f == FT - 1 and n == 2))
                    if j:
                        ins.then_inc(y_mm, 1)

        all_groups(pe, body)


NCONSTS = 12
ADDS = ((), (), (0,), (1,), (2, 3), (4,), (5,), (6, 7))
STORES = {3: (0,), 5: (1,), 7: (2, 3)}


_INS = ['x', 'L0_tok_W1', 'L0_tok_W2', 'L0_tok_b2', 'L0_attn_memory', 'L0_attn_Wq', 'L0_attn_bq', 'L0_attn_Wk',
        'L0_attn_bk', 'L0_attn_Wv', 'L0_attn_bv', 'L0_attn_Wo', 'L0_attn_bo', 'L0_ffn_w_router', 'L0_ffn_wi',
        'L0_ffn_wo']


def kernel(**inputs):
    import numpy as np
    import concourse.bacc as bacc
    from concourse.bass_utils import run_bass_kernel_spmd

    nc = bacc.Bacc("TRN2", target_bir_lowering=False, num_devices=1)
    arrays, args = {}, []
    for name in _INS:
        a = np.ascontiguousarray(inputs[name])
        arrays["in_" + name] = a
        args.append(nc.dram_tensor("in_" + name, a.shape, F32, kind="ExternalInput").ap())
    out = nc.dram_tensor("out", (B, NP, D), F32, kind="ExternalOutput").ap()
    audio_tower(nc, *args, out)
    r = run_bass_kernel_spmd(nc, [arrays], core_ids=[0])
    return r.results[0]["out"]
```

```python
from contextlib import ExitStack

import concourse.bass as bass
from concourse import mybir

F32 = mybir.dt.float32
F32R = mybir.dt.float32r
BF16 = mybir.dt.bfloat16
I32 = mybir.dt.int32
U32 = mybir.dt.uint32
ALU = mybir.AluOpType
ACT = mybir.ActivationFunctionType
AX = mybir.AxisListType

B, L = 64, 16384
PATCH, HOP = 128, 64
NP = (L - PATCH) // HOP + 1
D = 192
DH = D // 2
DM, DR = 128, D - 128
BIAS = (64, 96)
DS = 97
DV = D + 2
MEM = 8
NK = NP + MEM
KW = NK + 1
E, F = 8, 768
G = 16
SPG = B // G
S = SPG * NP
C = int(2 * 1.25 * S / E)
TPG = 2 * SPG
J = 3
CP = C // J
CPP = 112
SLOTS = CPP * J
ROWS = E * SLOTS
FT = F // 128
DW = 256
SCALE = float(D) ** -0.5
EPS = 1e-5
FAR = float(1 << 20)
EARLY = 4
STEPS = 22
NCONSTS = 11
LAGS = 4


def audio_tower(nc, x, W1, W2, b2, memory, Wq, bq, Wk, bk, Wv, bv, Wo, bo, Wr, wi, wo, out):
    h2_dram = nc.dram_tensor("h2_scratch", (B, 2, 128, D), F32, kind="Internal").ap()
    xs_dram = nc.dram_tensor("slots_in", (2 * ROWS, DW), F32, kind="Internal").ap()
    ys_dram = nc.dram_tensor("slots_out", (2 * ROWS, D), F32, kind="Internal").ap()
    with ExitStack() as both:
        routes = both.enter_context(nc.sbuf_tensor("routes", [128, B * 20], F32))
        ident = both.enter_context(nc.sbuf_tensor("ident", [128, 128], F32))
        r = Router(nc, both, routes, h2_dram, xs_dram)
        w = ExpertWeights(nc, both, wi, wo)
        with ExitStack() as ctx:
            attention(nc, ctx, x, W1, W2, b2, memory, Wq, bq, Wk, bk, Wv, bv, Wo, bo, Wr,
                      ident, r, w, ys_dram)
        with ExitStack() as ctx:
            w.room(ctx, range(EARLY, E))
            experts(nc, ctx, ident, r, w, ys_dram, out)


def wait(eng, sem, value):
    if isinstance(value, int) and value <= 0:
        return
    eng.wait_ge(sem, value)


def settle(eng, passed):
    eng.sem_inc(passed, 1)


def attention(nc, ctx, x, W1, W2, b2, memory, Wq, bq, Wk, bk, Wv, bv, Wo, bo, Wr,
              ident, routing, ffn, ys_dram):
    def sb(name, shape, dt=F32):
        return ctx.enter_context(nc.sbuf_tensor(name, shape, dt))

    def psum(name, shape):
        return ctx.enter_context(nc.psum_tensor(name, shape, F32))

    def sem(name):
        return ctx.enter_context(nc.semaphore(name))

    w1_sb = sb("w1_sb", [DH, 2, PATCH])
    w2_sb = sb("w2_sb", [DH, 2, D])
    wqkv_sb = [sb(f"w{n}_sb", [DH, 2, D]) for n in "qkv"]
    wo_sb = sb("wo_sb", [DH, 2, D])
    w2T = sb("w2T", [DH, 2, D])
    wqkvT = [sb(f"w{n}T", [DH, 2, D + 1]) for n in "qkv"]
    bias_sb = sb("bias_sb", [DH, 3, 2])
    bo_sb = sb("bo_sb", [128, D])
    b2_sb = sb("b2_sb", [128, D])
    wr_sb = sb("wr_sb", [DH, 2, E])
    memT = sb("memT", [128, 2, MEM])
    zero_sb = sb("zero_sb", [128, 2 * DW])
    qk_sb = sb("qk_sb", [128, 3, 2 * DM])
    vo_sb = sb("vo_sb", [128, 3, DV])
    w21 = [sb(f"w21_{p}", [128, D], F32R) for p in ("hi", "lo")]
    qk_main = [sb(f"qk_main_{p}", [128, 2 * DM], F32R) for p in ("hi", "lo")]
    qk_rest = sb("qk_rest", [128, 2 * DM], F32R)
    qk_small = sb("qk_small", [128, 2 * DM], F32R)
    vo_main = [sb(f"vo_main_{p}", [128, DV], F32R) for p in ("hi", "lo")]
    vo_rest = sb("vo_rest", [128, DV], F32R)
    vo_small = sb("vo_small", [128, DV], F32R)
    vmem = sb("vmem", [128, D], F32R)
    mem3 = sb("mem3", [128, 2, 128])
    half = sb("half", [128, 2])
    patches = sb("patches", [128, 2, 2, PATCH])
    patchT = [sb(f"patchT_{p}", [128, 256], F32R) for p in ("hi", "lo")]
    h = sb("h", [128, 4, 2, D])
    c = sb("c", [128, 2, 2 * DM])
    cT_hi = sb("cT_hi", [128, 2, 2, KW], F32R)
    cT_lo = sb("cT_lo", [128, 2, KW], F32R)
    cT_small = sb("cT_small", [128, 2, KW], F32R)
    qT_hi = sb("qT_hi", [128, 2, 2, 256], F32R)
    qT_lo = sb("qT_lo", [128, 2, 256], F32R)
    kbias = sb("kbias", [128, 2])
    fullpeak = sb("fullpeak", [128, 2])
    v = [sb(f"v_{p}", [128, 2, 2, D], F32R) for p in ("hi", "lo")]
    probs = sb("probs", [128, 2, 384])
    probsT = [sb(f"probsT_{p}", [128, n, 256], F32R) for p, n in (("hi", 3), ("lo", 2))]
    h2 = sb("h2", [128, 2, 2, D])
    c2 = sb("c2", [128, 2, D])
    c2T = sb("c2T", [DH, 2, 256])
    stats = sb("stats", [128, 2, 2, 6])
    mv = sb("mv", [128, 2, 2, 2])
    vare = sb("vare", [128, 2, 2])
    nmean = sb("nmean", [128, 2, 2])
    scales = sb("scales", [128, 2, 2, 2])
    peak = sb("peak", [128, 2])
    npeak = sb("npeak", [128, 2])
    total = sb("total", [128, 2, 2])
    rtotal = sb("rtotal", [128, 2])
    ps_h = psum("ps_h", [128, 512])
    ps_q = psum("ps_q", [128, 2, 256])
    ps_c = psum("ps_c", [128, 2, 256])
    ps_v = psum("ps_v", [128, 512])
    ps_s = psum("ps_s", [128, 2, 512])
    ps_p = psum("ps_p", [128, 4, 256])
    ps_x = ps_h[:, 0:256]
    values = ps_v[:, 0:2 * DV].rearrange("p (t d) -> p t d", t=2)[:, :, 0:D]
    ps_kbias = ps_v[:, 0:2 * DV].rearrange("p (t d) -> p t d", t=2)[:, :, D]
    ps_lg = ps_c[:, 0, 0:2 * E]
    ps_o = ps_p[:].rearrange("p k n -> p (k n)")[:, 0:2 * D].rearrange("p (k d) -> p k d", k=2)
    weights_in = sem("weights_to_transpose_in")
    first_loads = sem("w1_and_biases_in")
    loads = sem("setup_loads")
    zeroed = sem("slots_zeroed")
    pool_set = sem("pool_set")
    weights_tr = sem("weights_transposed")
    weights_cp = sem("weights_copied")
    folded = sem("weights_folded")
    split_hi = sem("folded_split_hi")
    qk_staged = sem("qk_staged")
    vo_staged = sem("vo_staged")
    mem_placed = sem("memory_placed")
    mem_set = sem("memory_keys_set")
    vmem_mm = sem("memory_values_made")
    x_loaded = [sem(f"x_loaded_{i}") for i in range(2)]
    patch_tr = sem("patch_transposed")
    patch_hi = sem("patchT_hi_ready")
    patch_lo = sem("patchT_lo_ready")
    h_mm = sem("tokens_made")
    h_ready = sem("tokens_ready")
    st1 = sem("stats1_ready")
    mv1 = sem("mean_var1_ready")
    sc1 = sem("scales1_steps")
    c_ready = sem("c_ready")
    c_doubled = sem("c_doubled")
    c_tr = sem("c_transposed")
    c_hi = sem("cT_hi_ready")
    c_lo = sem("cT_lo_ready")
    q_mm = sem("q_made")
    q_hi = sem("q_hi_ready")
    q_lo = sem("q_lo_ready")
    v_mm = sem("v_made")
    v_hi = sem("v_hi_ready")
    v_lo = sem("v_lo_ready")
    s_mm = sem("scores_made")
    kbias_ready = sem("key_bias_ready")
    peak_ready = sem("peak_ready")
    full_ready = sem("full_peak_ready")
    npeak_ready = sem("npeak_ready")
    exp_done = sem("exp_done")
    mem_twice = sem("memory_probs_copied")
    p_tr = sem("probs_transposed")
    pT_hi = sem("probsT_hi_ready")
    pT_lo = sem("probsT_lo_ready")
    pv_mm = sem("attended_made")
    rt_ready = sem("rtotal_ready")
    h2_ready = sem("h2_ready")
    h2_stored = [sem(f"h2_stored_{i}") for i in range(2)]
    st2 = sem("stats2_ready")
    mv2 = sem("mean_var2_ready")
    sc2 = sem("scales2_steps")
    sc_kept = sem("scales_kept")
    c2_ready = sem("c2_ready")
    c2_tr = sem("c2_transposed")
    c2T_ready = sem("c2T_ready")
    lg_mm = sem("logits_made")
    lg_kept = sem("logits_kept")
    dve_passed = sem("vector_waits_passed")
    sp_passed = sem("sync_waits_passed")
    pool_passed = sem("gpsimd_waits_passed")
    NLOADS = 8
    block = ctx.enter_context(nc.Block())

    def rows(w):
        return w.rearrange("(t p) d -> p t d", t=2)

    def all_iterations(eng, body):
        for j in range(4):
            body(0, j, lambda lag: j >= lag)
        for j in range(4):
            body(1, j, lambda lag: True)
        with eng.Fori(2, B // 4 - 1) as g:
            for j in range(4):
                body(g, j, lambda lag: True)
        for j in range(4):
            body(B // 4 - 1, j, lambda lag: True)
        for j in range(LAGS):
            body(B // 4, j, lambda lag: j < lag)

    def folded_parts(main, rest, small):
        full = slice(0, 128)
        return ((full, 0, main), (full, 1, rest), (slice(0, BIAS[0] + 1), 2, small),
                (slice(BIAS[1], BIAS[1] + 1), 2, small))

    ROUTE = B - 4
    SEND = ROUTE + 3

    def splits(t):
        if not isinstance(t, int) or 8 <= t < ROUTE:
            return None
        n = t if t < 8 else t - ROUTE + 8
        return (n // 2, n % 2) if n < 2 * EARLY else None

    def turns(g, j, lag):
        return g * 2 + ((j - lag) // 2 + 1)

    @block.sync
    def _(sp):
        for w, d in zip([w2_sb] + wqkv_sb, (W2, Wq, Wk, Wv)):
            sp.dma_start(w[:], rows(d)).then_inc(weights_in, 16)
        sp.dma_start(w1_sb[:], rows(W1)).then_inc(first_loads, 16)
        with nc.allow_non_contiguous_dma(reason="small vectors, once"):
            for i, b in enumerate((bq, bk, bv)):
                sp.dma_start(bias_sb[:, i, :], b.rearrange("(t p) -> p t", t=2)).then_inc(first_loads, 16)
            sp.dma_start(wo_sb[:], rows(Wo)).then_inc(loads, 16)
            for part, first in ((slice(0, DM), 0), (slice(0, DR), DM), (slice(DR, 2 * DR), DM)):
                n = part.stop - part.start
                sp.dma_start(memT[part, min(first, 1), :], memory[:, first:first + n].rearrange("m p -> p m")) \
                    .then_inc(loads, 16)
        for row in BIAS:
            sp.dma_start(bo_sb[row:row + 1, :], bo.rearrange("(a d) -> a d", a=1)).then_inc(loads, 16)
        sp.dma_start(wr_sb[:], rows(Wr)).then_inc(loads, 16)
        sp.dma_start(b2_sb[:], b2.rearrange("(a d) -> a d", a=1).to_broadcast([128, D])).then_inc(loads, 16)
        flats = [slots.rearrange("(n p r) d -> n p (r d)", p=128, r=2) for slots in (routing.xs_dram, ys_dram)]
        zeroes = [flat[n] for n in range(2 * ROWS // 256) for flat in flats]
        share = -(-len(zeroes) // 8)

        def body(g, j, live):
            t = g * 4 + j
            if live(0):
                if not (isinstance(t, int) and t < 2):
                    sp.wait_ge(patch_tr, t - 1)
                for k in range(2):
                    n = 127 if k and isinstance(t, int) and t == B - 1 else 128
                    src = windows(x, t, k * 128, n)
                    settle(sp, sp_passed)
                    sp.dma_start(patches[0:n, j % 2, k, :], src).then_inc(x_loaded[j % 2], 16)
            if splits(t):
                e, part = splits(t)
                if part == 0:
                    ffn.load_wi(sp, e)
                else:
                    ffn.load_wo(sp, e)
            if isinstance(t, int) and t == ROUTE:
                for stored in h2_stored:
                    sp.wait_ge(stored, 16 * SPG // 2)
                routing.load_send(sp, 0, sp_passed)
            if isinstance(t, int) and 0 < t <= 8:
                if t == 1:
                    sp.wait_ge(pool_set, 2)
                for part in zeroes[(t - 1) * share:t * share]:
                    sp.dma_start(part, zero_sb[:, 0:part.shape[1]]).then_inc(zeroed, 16)
            if live(3):
                sp.wait_ge(h2_ready, t - 2)
                settle(sp, sp_passed)
                sp.dma_start(routing.h2_dram[t - 3].rearrange("k p d -> p k d"), h2[:, (j + 1) % 2, :, :]) \
                    .then_inc(h2_stored[(j + 1) % 2], 16)

        for j in range(4):
            body(0, j, lambda lag: j >= lag)
        for j in range(4):
            body(1, j, lambda lag: True)
        for j in range(4):
            body(2, j, lambda lag: True)
        with sp.Fori(3, B // 4 - 1) as g:
            for j in range(4):
                body(g, j, lambda lag: True)
        for j in range(4):
            body(B // 4 - 1, j, lambda lag: True)
        for j in range(LAGS):
            body(B // 4, j, lambda lag: j < lag)
        sp.wait_ge(h2_stored[0], 16 * (B // 2))
        sp.wait_ge(h2_stored[1], 16 * (B // 2))
        sp.wait_ge(zeroed, 2 * 16 * (2 * ROWS // 256))

    @block.gpsimd
    def _(pool):
        pool.memset(ident[:], 0.0).then_inc(pool_set, 1)
        pool.memset(zero_sb[:], 0.0).then_inc(pool_set, 1)
        pool.wait_ge(pool_set, 1)
        pool.affine_select(out=ident[:], in_=ident[:], compare_op=ALU.not_equal, fill=1.0, base=0,
                           pattern=[[-1, 128]], channel_multiplier=1).then_inc(pool_set, 1)
        pool.memset(half[:], -0.5).then_inc(pool_set, 1)
        pool.memset(probs[:], 0.0).then_inc(pool_set, 1)
        pool.wait_ge(pool_set, 5)
        routing.constants(pool)

        def norm(n, which, mv_ready, done, applied):
            pool.wait_ge(mv_ready, n + 1)
            wait(pool, applied, n)
            settle(pool, pool_passed)
            pool.tensor_scalar(vare[:, which, :], mv[:, which, :, 1], EPS, None, ALU.add)
            pool.tensor_scalar(nmean[:, which, :], mv[:, which, :, 0], -1.0, None, ALU.mult).then_inc(done, 1)
            pool.wait_ge(done, n * 3 + 1)
            pool.tensor_tensor(scales[:, which, :, 0], vare[:, which, :], half[:], ALU.pow).then_inc(done, 1)
            pool.wait_ge(done, n * 3 + 2)
            pool.tensor_tensor(scales[:, which, :, 1], nmean[:, which, :], scales[:, which, :, 0],
                               ALU.mult).then_inc(done, 1)

        def body(g, j, live):
            t = g * 4 + j
            if live(2):
                pool.wait_ge(exp_done, t - 1)
                settle(pool, pool_passed)
                for k in range(2):
                    copies = probs[:, k, 288:352].rearrange("p (i m) -> p i m", i=2)[:, :, 0:MEM - 1]
                    ins = pool.tensor_copy(copies, probs[:, k, 256:NK].unsqueeze(1).to_broadcast([128, 2, MEM - 1]))
                ins.then_inc(mem_twice, 1)
            if live(0):
                norm(t, 0, mv1, sc1, c_ready)
            if live(3):
                n = t - 3
                norm(n, 1, mv2, sc2, c2_ready)
            if live(0):
                pool.wait_ge(c_ready, t + 1)
                settle(pool, pool_passed)
                pool.tensor_copy(c[:, :, D:2 * DM], c[:, :, DM:D]).then_inc(c_doubled, 1)
            if live(3):
                pool.wait_ge(sc2, n * 3 + 3)
                settle(pool, pool_passed)
                kept = routing.routes[:, bass.ds(n * 20, 20)].rearrange("p (k r) -> p k r", k=2)
                pool.tensor_copy(kept[:, :, E:E + 2], scales[:, 1, :, :]).then_inc(sc_kept, 1)
            if splits(t):
                e, part = splits(t)
                if part == 0:
                    ffn.low_wi(pool, e)
                else:
                    ffn.low_wo(pool, e)
            if isinstance(t, int) and t == SEND - 1:
                routing.double(pool, 0, pool_passed)
                pool.wait_ge(zeroed, 2 * 16 * (2 * ROWS // 256))
                settle(pool, pool_passed)
            if isinstance(t, int) and t >= SEND:
                n = 3 * (t - SEND)
                routing.dispatch(pool, range(n, min(n + 3, TPG)))

        all_iterations(pool, body)

    @block.scalar
    def _(act):
        act.wait_ge(weights_tr, 2)
        act.activation(w2T[:], ps_h[0:DH, 0:2 * D].rearrange("p (t d) -> p t d", t=2), ACT.Copy).then_inc(weights_cp, 1)
        act.activation(wqkvT[0][:, :, 0:D], ps_v[0:DH, 0:2 * D].rearrange("p (t d) -> p t d", t=2),
                       ACT.Copy).then_inc(weights_cp, 1)
        act.wait_ge(folded, 1)
        act.activation(w21[0][:], ps_q[:, 0, 0:D], ACT.Copy).then_inc(split_hi, 1)
        act.wait_ge(folded, 2)
        for rows_, n, bank in folded_parts(ps_s[:, 0], ps_s[:, 1], ps_p[:, 0]):
            act.activation(qk_sb[rows_, n, 0:D], bank[rows_, 0:D], ACT.Copy)
            ins = act.activation(qk_sb[rows_, n, D:2 * DM], bank[rows_, DM:D], ACT.Copy)
        ins.then_inc(qk_staged, 1)
        act.wait_ge(qk_staged, 1)
        for (rows_, n, dst) in folded_parts(qk_main[0], qk_rest, qk_small):
            ins = act.activation(dst[rows_, :], qk_sb[rows_, n, :], ACT.Copy)
        ins.then_inc(split_hi, 1)
        act.wait_ge(vo_staged, 2)
        for (rows_, n, dst) in folded_parts(vo_main[0], vo_rest, vo_small):
            ins = act.activation(dst[rows_, :], vo_sb[rows_, n, :], ACT.Copy)
        ins.then_inc(split_hi, 1)
        act.wait_ge(vmem_mm, 1)
        act.activation(vmem[:], ps_h[:, 0:D], ACT.Copy).then_inc(split_hi, 1)
        act.wait_ge(mem_set, 1)

        def normed(dst, src, which, k):
            return act.activation(dst, src, ACT.Identity, bias=scales[:, which, k, 1:2], scale=scales[:, which, k, 0:1])

        def body(g, j, live):
            t = g * 4 + j
            if live(0):
                n = t
                act.wait_ge(patch_tr, n + 1)
                wait(act, h_mm, n)
                act.activation(patchT[0][:], ps_x, ACT.Copy).then_inc(patch_hi, 1)
            if live(1):
                n = t - 1
                r = (j - 1) % 2
                act.wait_ge(c_tr, n + 1)
                wait(act, s_mm, n - 1)
                act.activation(cT_hi[:, r, :, 0:NP], ps_c[:, :, 0:NP], ACT.Copy).then_inc(c_hi, 1)
            if live(2):
                n = t - 2
                act.wait_ge(npeak_ready, n + 1)
                wait(act, p_tr, n)
                wait(act, rt_ready, n - 1)
                for k in range(2):
                    ins = act.activation(probs[:, k, 0:NK], ps_s[:, k, 0:NK], ACT.Exp, bias=npeak[:, k:k + 1],
                                         scale=SCALE, accum_out=total[:, j % 2, k:k + 1])
                ins.then_inc(exp_done, 1)
            if live(4):
                n = t - 4
                act.wait_ge(c2_tr, n + 1)
                wait(act, lg_mm, n)
                act.activation(c2T[:], ps_c[0:DH, :, :], ACT.Copy).then_inc(c2T_ready, 1)
            if live(1):
                n = t - 1
                act.wait_ge(q_mm, n + 1)
                wait(act, s_mm, n - 1)
                act.activation(qT_hi[:, r, :, :], ps_q[:], ACT.Copy).then_inc(q_hi, 1)
            if live(2):
                n = t - 2
                act.wait_ge(p_tr, n + 1)
                wait(act, pv_mm, n)
                act.activation(probsT[0][:], ps_p[:, 0:3, :], ACT.Copy).then_inc(pT_hi, 1)
            if live(0):
                n = t
                act.wait_ge(sc1, n * 3 + 3)
                wait(act, c_tr, n)
                for k in range(2):
                    ins = normed(c[:, k, 0:D], h[:, j, k, :], 0, k)
                ins.then_inc(c_ready, 1)
            if live(1):
                n = t - 1
                act.wait_ge(v_mm, n + 1)
                wait(act, pv_mm, n - 1)
                act.activation(v[0][:, r, :, :], values, ACT.Copy).then_inc(v_hi, 1)
            if live(3):
                n = t - 3
                act.wait_ge(sc2, n * 3 + 3)
                wait(act, c2_tr, n)
                for k in range(2):
                    ins = normed(c2[:, k, :], h2[:, (j + 1) % 2, k, :], 1, k)
                ins.then_inc(c2_ready, 1)
            if splits(t):
                e, part = splits(t)
                if part == 0:
                    ffn.high_wi(act, e)
                else:
                    ffn.high_wo(act, e)
            if isinstance(t, int) and t == ROUTE:
                routing.exponentials(act, 0)

        all_iterations(act, body)

    @block.vector
    def _(dve):
        for r in range(2):
            for part in (cT_hi[:, r, 0], cT_hi[:, r, 1], cT_lo[:, r]):
                dve.memset(part[:, NP:KW].bitcast(F32), 0.0)
            dve.memset(cT_small[:, r, :].bitcast(F32), 0.0)
        for part in (qk_small, vo_small):
            dve.memset(part[:].bitcast(F32), 0.0)
        dve.memset(vo_sb[:], 0.0)
        dve.memset(mem3[:], 0.0).then_inc(mem_placed, 1)
        dve.wait_ge(mem_placed, 1)
        for row in BIAS:
            ins = dve.memset(cT_small[row:row + 1, :, :].bitcast(F32), 1.0)
        dve.memset(mem3[BIAS[0]:BIAS[0] + 1, 1, 0:128], 1.0)
        dve.wait_ge(weights_tr, 4)
        for i in range(1, 3):
            src = ps_q if i == 1 else ps_c
            for k in range(2):
                ins = dve.tensor_copy(wqkvT[i][:, k, 0:D], src[0:DH, k, 0:D])
        dve.wait_ge(first_loads, 16 * 4)
        for i in range(3):
            ins = dve.tensor_copy(wqkvT[i][:, :, D], bias_sb[:, i, :])
        ins.then_inc(weights_cp, 1)
        dve.wait_ge(loads, 16 * NLOADS)
        for i in range(3):
            cols = slice(32 * i, 32 * i + MEM - 1)
            dve.tensor_copy(mem3[:, 0, cols], memT[:, 0, 1:MEM])
            dve.tensor_copy(mem3[0:DR, 1, cols], memT[0:DR, 1, 1:MEM])
        for r in range(2):
            ins = dve.tensor_copy(cT_hi[:, r, :, NP:NK], memT[:])
        ins.then_inc(mem_placed, 1)
        dve.wait_ge(mem_placed, 2)
        for r in range(2):
            dve.tensor_tensor(cT_lo[:, r, NP:NK], memT[:, 0], cT_hi[:, r, 0, NP:NK].bitcast(F32), ALU.subtract)
            dve.tensor_tensor(cT_small[0:DR, r, NP:NK], memT[0:DR, 1], cT_hi[0:DR, r, 1, NP:NK].bitcast(F32),
                              ALU.subtract)
        dve.wait_ge(folded, 3)
        for rows_, n, bank in folded_parts(ps_h, ps_v, ps_p[:, 2]):
            dve.tensor_copy(vo_sb[rows_, n, 0:D], bank[rows_, 0:D])
        dve.wait_ge(qk_staged, 1)
        for rows_, n, bank in folded_parts(ps_s[:, 0], ps_s[:, 1], ps_p[:, 0]):
            ins = dve.tensor_copy(vo_sb[rows_, n, D:D + 1], bank[rows_, D:D + 1])
        ins.then_inc(vo_staged, 1)
        dve.wait_ge(vo_staged, 1)
        for row in BIAS:
            ins = dve.tensor_tensor(vo_sb[row:row + 1, 2, 0:D], vo_sb[row:row + 1, 2, 0:D], bo_sb[row:row + 1, :], ALU.add)
        ins.then_inc(vo_staged, 1)
        dve.wait_ge(split_hi, 2)
        dve.tensor_tensor(w21[1][:], ps_q[:, 0, 0:D], w21[0][:].bitcast(F32), ALU.subtract)

        def low_weights(staged, main, rest, small):
            dve.tensor_tensor(main[1][:], staged[:, 0, :], main[0][:].bitcast(F32), ALU.subtract)
            dve.tensor_tensor(rest[DR:128, :], staged[DR:128, 1, :], rest[DR:128, :].bitcast(F32), ALU.subtract)
            row = slice(BIAS[1], BIAS[1] + 1)
            dve.tensor_tensor(small[row, :], staged[row, 2, :], small[row, :].bitcast(F32), ALU.subtract)

        low_weights(qk_sb, qk_main, qk_rest, qk_small)
        dve.wait_ge(split_hi, 3)
        low_weights(vo_sb, vo_main, vo_rest, vo_small)
        dve.wait_ge(split_hi, 4)
        ins = dve.tensor_tensor(vmem[64:96, :], ps_h[64:96, 0:D], vmem[64:96, :].bitcast(F32), ALU.subtract)
        ins.then_inc(mem_set, 1)

        def statistics(n, src, which, src_ready, st_ready, mv_ready):
            dve.wait_ge(src_ready, n + 1)
            wait(dve, mv_ready, n)
            for k in range(2):
                ins = dve.bn_stats(stats[:, which, k, :], src[:, k, :])
            ins.then_inc(st_ready, 1)

        def mean_variance(n, which, st_ready, scaled, mv_ready):
            dve.wait_ge(st_ready, n + 1)
            wait(dve, scaled, n * 3)
            settle(dve, dve_passed)
            for k in range(2):
                ins = dve.bn_aggr(mv[:, which, k, :], stats[:, which, k, :])
            ins.then_inc(mv_ready, 1)

        def low(dst, src, hi, hi_ready, lo_ready, n):
            dve.wait_ge(hi_ready, n + 1)
            dve.tensor_tensor(dst, src, hi.bitcast(F32), ALU.subtract).then_inc(lo_ready, 1)

        def body(g, j, live):
            t = g * 4 + j
            if isinstance(t, int) and t == ROUTE + 2:
                routing.counts(dve, 0, ps_q)
                routing.slots(dve, 0)
            if live(0):
                low(patchT[1][:], ps_x, patchT[0][:], patch_hi, patch_lo, t)
            if live(2):
                n = t - 2
                dve.wait_ge(peak_ready, n + 1)
                dve.wait_ge(kbias_ready, n + 1)
                dve.scalar_tensor_tensor(fullpeak[:], peak[:], SCALE, kbias[:], ALU.mult, ALU.add).then_inc(full_ready, 1)
                dve.wait_ge(full_ready, n + 1)
                wait(dve, exp_done, n)
                dve.tensor_tensor(npeak[:], kbias[:], fullpeak[:], ALU.subtract).then_inc(npeak_ready, 1)
            if live(1):
                r = (j - 1) % 2
                dve.wait_ge(c_hi, t)
                dve.tensor_tensor(cT_small[0:DR, r, 0:NP], ps_c[0:DR, 1, 0:NP], cT_hi[0:DR, r, 1, 0:NP].bitcast(F32),
                                  ALU.subtract)
                low(cT_lo[:, r, 0:NP], ps_c[:, 0, 0:NP], cT_hi[:, r, 0, 0:NP], c_hi, c_lo, t - 1)
            if live(3):
                n = t - 3
                dve.wait_ge(rt_ready, n + 1)
                dve.wait_ge(pv_mm, n + 1)
                if not (isinstance(t, int) and n < 2):
                    dve.wait_ge(h2_stored[(j - 3) % 2], (turns(g, j, 3) - 1) * 16)
                    dve.wait_ge(c2_ready, n - 1)
                for k in range(2):
                    ins = dve.scalar_tensor_tensor(h2[:, (j - 3) % 2, k, :], ps_o[:, k, :], rtotal[:, k:k + 1],
                                                   h[:, (j - 3) % 4, k, :], ALU.mult, ALU.add)
                ins.then_inc(h2_ready, 1)
            if live(0):
                dve.wait_ge(h_mm, t + 1)
                dve.tensor_tensor(h[:, j, :, :], ps_h[:, 0:2 * D].rearrange("p (t d) -> p t d", t=2),
                                  b2_sb[:].rearrange("p (a d) -> p a d", a=1).to_broadcast([128, 2, D]),
                                  ALU.add).then_inc(h_ready, 1)
            if live(2):
                n = t - 2
                dve.wait_ge(exp_done, n + 1)
                wait(dve, h2_ready, n)
                dve.reciprocal(rtotal[:], total[:, j % 2, :]).then_inc(rt_ready, 1)
            if live(0):
                statistics(t, h[:, j], 0, h_ready, st1, mv1)
            if live(0):
                mean_variance(t, 0, st1, sc1, mv1)
            if live(3):
                statistics(t - 3, h2[:, (j - 3) % 2], 1, h2_ready, st2, mv2)
            if live(3):
                mean_variance(t - 3, 1, st2, sc2, mv2)
            if live(1):
                dve.wait_ge(q_hi, t)
                rest = qT_hi[DR:128, r, 1, :]
                dve.tensor_tensor(rest, ps_q[DR:128, 1, :], rest.bitcast(F32), ALU.subtract)
                low(qT_lo[:, r, :], ps_q[:, 0, :], qT_hi[:, r, 0, :], q_hi, q_lo, t - 1)
            if live(4):
                n = t - 4
                dve.wait_ge(lg_mm, n + 1)
                kept = routing.routes[:, bass.ds(n * 20, 20)].rearrange("p (k r) -> p k r", k=2)
                dve.tensor_copy(kept[:, :, 0:E], ps_lg.rearrange("p (k e) -> p k e", k=2)).then_inc(lg_kept, 1)
            if live(2):
                dve.wait_ge(pT_hi, t - 1)
                low3 = probsT[0][32:64, 2, :]
                dve.tensor_tensor(low3, ps_p[32:64, 2, :], low3.bitcast(F32), ALU.subtract)
                low(probsT[1][:], ps_p[:, 0:2, :], probsT[0][:, 0:2, :], pT_hi, pT_lo, t - 2)
            if live(1):
                n = t - 1
                dve.wait_ge(v_hi, n + 1)
                wait(dve, npeak_ready, n)
                dve.tensor_scalar(kbias[:], ps_kbias, SCALE, None, ALU.mult).then_inc(kbias_ready, 1)
                low(v[1][:, r, :, :], values, v[0][:, r, :, :], v_hi, v_lo, n)
                dve.wait_ge(s_mm, n + 1)
                dve.tensor_reduce(peak[:], ps_s[:, :, 0:NK], AX.X, ALU.max).then_inc(peak_ready, 1)
            if splits(t) and splits(t)[1] == 0:
                ffn.low_rest(dve, splits(t)[0])
            if isinstance(t, int) and t == ROUTE:
                dve.wait_ge(routing.consts, NCONSTS)
                dve.wait_ge(sc_kept, SPG)
                routing.logits(dve, 0)
                routing.normed(dve, 0, range(0, TPG // 2))
            if isinstance(t, int) and t == ROUTE + 1:
                routing.choice(dve, 0, dve_passed)
                routing.normed(dve, 0, range(TPG // 2, TPG)).then_inc(routing.send_ready, 1)

        all_iterations(dve, body)

    @block.tensor
    def _(pe):
        pe.wait_ge(weights_in, 16 * 4)
        pe.wait_ge(pool_set, 5)
        for w, bank in ((w2_sb, ps_h), (wqkv_sb[0], ps_v), (wqkv_sb[1], ps_q), (wqkv_sb[2], ps_c)):
            for k in range(2):
                for i in range(2):
                    dst = bank[0:DH, k * D + i * DH:k * D + (i + 1) * DH] if bank in (ps_h, ps_v) \
                        else bank[0:DH, k, i * DH:(i + 1) * DH]
                    ins = pe.transpose(dst, w[:, i, k * DH:(k + 1) * DH], ident[0:DH, 0:DH])
            ins.then_inc(weights_tr, 1)
        pe.wait_ge(weights_cp, 3)
        pe.wait_ge(first_loads, 16 * 4)
        for k in range(2):
            ins = pe.matmul(ps_q[:, 0, 0:D], w1_sb[:, k, :], w2T[:, k, :], start=(k == 0), stop=(k == 1))
        ins.then_inc(folded, 1)
        rest, bias = slice(DM, D), slice(D, D + 1)
        for left, right, n, banks in ((wqkvT[0], wqkvT[1], D + 1, (ps_s[:, 0], ps_s[:, 1], ps_p[:, 0])),
                                      (wqkvT[2], wo_sb, D, (ps_h, ps_v, ps_p[:, 2]))):
            if right is wo_sb:
                pe.wait_ge(loads, 16 * NLOADS)
            for bank, first, cols in ((0, 0, slice(0, DM)), (1, 0, rest), (1, DR, rest), (2, 0, rest),
                                      (2, BIAS[0], bias), (2, BIAS[1], bias)):
                m = cols.stop - cols.start
                for k in range(2):
                    ins = pe.matmul(banks[bank][first:first + m, 0:n], left[:, k, cols], right[:, k, 0:n],
                                    start=(k == 0), stop=(k == 1))
            ins.then_inc(folded, 1)
        pe.wait_ge(vo_staged, 2)
        pe.wait_ge(mem_placed, 2)
        pe.matmul(ps_h[:, 0:D], mem3[:, 0, :], vo_sb[:, 0, 0:D], start=True, stop=False)
        pe.matmul(ps_h[:, 0:D], mem3[0:DS, 1, :], vo_sb[0:DS, 2, 0:D], start=False, stop=True).then_inc(vmem_mm, 1)
        pe.wait_ge(mem_set, 1)
        pe.wait_ge(split_hi, 4)

        PASSES = ((0, 0), (0, 1), (1, 0))

        def product(dst, terms, first=True):
            n = 0
            for stationary, moving in terms:
                for a, b in PASSES:
                    ins = pe.matmul(dst, stationary[a], moving[b], start=(first and n == 0),
                                    stop=(n == 3 * len(terms) - 1))
                    n += 1
            return ins

        def passes(dst, terms):
            for n, (stationary, moving) in enumerate(terms):
                ins = pe.matmul(dst, stationary, moving, start=(n == 0), stop=(n == len(terms) - 1))
            return ins

        def pair(two, *index):
            return [part[index] for part in two]

        def body(g, j, live):
            t = g * 4 + j
            if live(0):
                n = t
                pe.wait_ge(x_loaded[j % 2], turns(g, j, 0) * 32)
                wait(pe, h_ready, n)
                for k in range(2):
                    ins = pe.transpose(ps_x[:, k * 128:(k + 1) * 128], patches[:, j % 2, k, :], ident[:])
                ins.then_inc(patch_tr, 1)
            if live(1):
                n = t - 1
                pe.wait_ge(c_doubled, n + 1)
                wait(pe, lg_kept, n - 3)
                for i in range(2):
                    for k in range(2):
                        ins = pe.transpose(ps_c[:, i, k * 128:(k + 1) * 128], c[:, k, i * DM:(i + 1) * DM], ident[:])
                ins.then_inc(c_tr, 1)
            if live(3):
                n = t - 3
                r = (j - 3) % 2
                pe.wait_ge(pT_lo, n + 1)
                pe.wait_ge(v_lo, n + 1)
                for k in range(2):
                    q = slice(k * 128, (k + 1) * 128)
                    pe.matmul(ps_o[:, k, :], probsT[0][:, 2, q], vmem[:], start=True, stop=False)
                    ins = product(ps_o[:, k, :],
                                  [(pair(probsT, slice(0, 128), i, q), pair(v, slice(0, 128), r, i, slice(0, D)))
                                   for i in range(2)], first=False)
                ins.then_inc(pv_mm, 1)
            if live(0):
                n = t
                pe.wait_ge(patch_lo, n + 1)
                for k in range(2):
                    ins = product(ps_h[:, k * D:(k + 1) * D],
                                  [(pair(patchT, slice(0, 128), slice(k * 128, (k + 1) * 128)),
                                    pair(w21, slice(0, 128), slice(0, D)))])
                ins.then_inc(h_mm, 1)
            if live(4):
                n = t - 4
                pe.wait_ge(c2_ready, n + 1)
                if live(1):
                    pe.wait_ge(c_lo, t)
                else:
                    pe.wait_ge(lg_kept, n)
                for i in range(2):
                    for k in range(2):
                        ins = pe.transpose(ps_c[0:DH, i, k * 128:(k + 1) * 128], c2[:, k, i * DH:(i + 1) * DH], ident[:])
                ins.then_inc(c2_tr, 1)
            if live(1):
                n = t - 1
                r = (j - 1) % 2
                pe.wait_ge(c_lo, n + 1)
                wait(pe, q_lo, n)
                if isinstance(t, int) and t == ROUTE + 2:
                    pe.wait_ge(routing.route, 9)
                for o in range(2):
                    m = slice(o * DM, (o + 1) * DM)
                    tokens = cT_hi[:, r, 0, 0:256]
                    ins = passes(ps_q[:, o, :], (
                        (qk_main[0][:, m], tokens), (qk_main[0][:, m], cT_lo[:, r, 0:256]), (qk_main[1][:, m], tokens),
                        (qk_rest[:, m], cT_hi[:, r, 1, 0:256]), (qk_small[0:DS, m], cT_small[0:DS, r, 0:256])))
                ins.then_inc(q_mm, 1)
            if live(2):
                n = t - 2
                pe.wait_ge(mem_twice, n + 1)
                wait(pe, h2_ready, n)
                for i in range(3):
                    for k in range(2):
                        ins = pe.transpose(ps_p[:, i, k * 128:(k + 1) * 128], probs[:, k, i * 128:(i + 1) * 128], ident[:])
                ins.then_inc(p_tr, 1)
            if live(1):
                n = t - 1
                r = (j - 1) % 2
                wait(pe, v_lo, n)
                for k in range(2):
                    tok = slice(k * 128, (k + 1) * 128)
                    tokens = cT_hi[:, r, 0, tok]
                    ins = passes(ps_v[:, k * DV:(k + 1) * DV], (
                        (tokens, vo_main[0][:]), (tokens, vo_main[1][:]), (cT_lo[:, r, tok], vo_main[0][:]),
                        (cT_hi[:, r, 1, tok], vo_rest[:]), (cT_small[0:DS, r, tok], vo_small[0:DS, :])))
                ins.then_inc(v_mm, 1)
            if live(4):
                n = t - 4
                pe.wait_ge(c2T_ready, n + 1)
                for k in range(2):
                    for i in range(2):
                        ins = pe.matmul(ps_lg[:, k * E:(k + 1) * E], c2T[:, i, k * 128:(k + 1) * 128], wr_sb[:, i, :],
                                        start=(i == 0), stop=(i == 1))
                ins.then_inc(lg_mm, 1)
            if live(1):
                n = t - 1
                r = (j - 1) % 2
                pe.wait_ge(q_lo, n + 1)
                wait(pe, exp_done, n)
                for k in range(2):
                    q = slice(k * 128, (k + 1) * 128)
                    q_main, keys = qT_hi[:, r, 0, q], cT_hi[:, r, 0, :]
                    ins = passes(ps_s[:, k, 0:KW], (
                        (q_main, keys), (q_main, cT_lo[:, r, :]), (qT_lo[:, r, q], keys),
                        (qT_hi[:, r, 1, q], cT_hi[:, r, 1, :]), (qT_hi[0:DR, r, 1, q], cT_small[0:DR, r, :])))
                ins.then_inc(s_mm, 1)
            if isinstance(t, int) and t == ROUTE + 1:
                pe.wait_ge(routing.consts, NCONSTS)
                routing.count(pe, 0, ps_q)

        all_iterations(pe, body)


def windows(x, s, first, count):
    return bass.AP(x.tensor, s * L + first * HOP, [[HOP, count], [1, PATCH]])


class ExpertWeights:

    def __init__(self, nc, ctx, wi, wo):
        self.nc, self.wi_dram, self.wo_dram = nc, wi, wo
        self.area = ctx.enter_context(nc.sbuf_tensor("area", [128, 16 * D], F32))
        self.raw_main = self.area[:, 0:F]
        self.raw_rest = self.area[:, F:2 * F]
        self.raw_wo = self.area[:, 2 * F:2 * F + FT * D].rearrange("p (f d) -> p f d", f=FT)
        self.wi_main, self.wi_rest, self.wo = [], [], []
        self.room(ctx, range(EARLY))

        def sem(name):
            return ctx.enter_context(nc.semaphore(name))

        self.wi_in = sem("raw_wi_in")
        self.wo_in = sem("raw_wo_in")
        self.hi = sem("weights_hi_ready")
        self.lo = sem("weights_lo_ready")
        self.rest_lo = sem("wi_rest_lo_ready")

    def room(self, ctx, experts_):
        def sb(name, shape):
            return ctx.enter_context(self.nc.sbuf_tensor(name, shape, F32R))

        for e in experts_:
            self.wi_main.append([sb(f"wi_main_{p}_{e}", [128, F]) for p in ("hi", "lo")])
            self.wi_rest.append(sb(f"wi_rest_{e}", [128, F]))
            self.wo.append(sb(f"wo_{e}", [128, FT, 2, D]))

    def load_wi(self, sp, e):
        if e:
            sp.wait_ge(self.lo, 2 * e - 1)
            sp.wait_ge(self.rest_lo, e)
        sp.dma_start(self.raw_main, self.wi_dram[e, 0:128, :]).then_inc(self.wi_in, 16)
        for half in range(2):
            sp.dma_start(self.raw_rest[64 * half:64 * half + 64, :], self.wi_dram[e, 128:192, :]) \
                .then_inc(self.wi_in, 16)

    def load_wo(self, sp, e):
        if e:
            sp.wait_ge(self.lo, 2 * e)
        sp.dma_start(self.raw_wo, self.wo_dram[e].rearrange("(f p) d -> p f d", p=128)).then_inc(self.wo_in, 16)

    def high_wi(self, act, e):
        act.wait_ge(self.wi_in, 48 * (e + 1))
        act.activation(self.wi_main[e][0][:], self.raw_main, ACT.Copy)
        act.activation(self.wi_rest[e][:], self.raw_rest, ACT.Copy).then_inc(self.hi, 1)

    def high_wo(self, act, e):
        act.wait_ge(self.wo_in, 16 * (e + 1))
        act.activation(self.wo[e][:, :, 0, :], self.raw_wo, ACT.Copy).then_inc(self.hi, 1)

    def low_wi(self, pool, e):
        pool.wait_ge(self.hi, 2 * e + 1)
        pool.tensor_tensor(self.wi_main[e][1][:], self.raw_main, self.wi_main[e][0][:].bitcast(F32),
                           ALU.subtract).then_inc(self.lo, 1)

    def low_wo(self, pool, e):
        pool.wait_ge(self.hi, 2 * e + 2)
        pool.tensor_tensor(self.wo[e][:, :, 1, :], self.raw_wo, self.wo[e][:, :, 0, :].bitcast(F32),
                           ALU.subtract).then_inc(self.lo, 1)

    def low_rest(self, dve, e):
        dve.wait_ge(self.hi, 2 * e + 1)
        lower = self.wi_rest[e][64:128, :]
        dve.tensor_tensor(lower, self.raw_rest[64:128, :], lower.bitcast(F32), ALU.subtract).then_inc(self.rest_lo, 1)


class Router:

    def __init__(self, nc, ctx, routes, h2_dram, xs_dram):
        def sb(name, shape, dt=F32):
            return ctx.enter_context(nc.sbuf_tensor(name, shape, dt))

        def sem(name):
            return ctx.enter_context(nc.semaphore(name))

        self.routes, self.h2_dram, self.xs_dram = routes, h2_dram, xs_dram
        self.send = sb("send", [128, TPG, DW])
        self.rt = sb("rt", [128, TPG, E + 2])
        self.expo = sb("expo", [128, TPG, E])
        self.tokmax = sb("tokmax", [128, TPG])
        self.toksum = sb("toksum", [128, TPG])
        self.top = sb("top", [128, TPG, 8])
        self.topi = sb("topi", [128, TPG, 8], U32)
        self.chosen = sb("chosen", [128, 2, TPG])
        self.gate = sb("gate", [128, 2, TPG])
        self.mask = sb("mask", [128, 2, TPG, E], BF16)
        self.scan = [sb(f"scan_{i}", [128, 24, E]) for i in range(2)]
        self.pos = sb("pos", [128, 16, E])
        self.sel = sb("sel", [128, 16])
        self.ok = sb("ok", [128, 16])
        self.slot = sb("slot", [128, 16])
        self.miss = sb("miss", [128, 16])
        self.send_idx = sb("send_idx", [128, 16], I32)
        self.ret_new = sb("ret_new", [128, 2, 16], I32)
        self.ring = sb("ring", [128, 1])
        self.before = sb("before", [128, 128], BF16)
        self.ones = sb("ones", [128, 128], BF16)
        self.which = sb("which", [128, TPG, E])
        self.whichi = sb("whichi", [128, TPG * E], I32)
        self.far = sb("far", [128, 2, TPG])
        self.consts = sem("route_consts_set")
        self.send_in = sem("send_in")
        self.route = sem("route_steps")
        self.exp_done = sem("route_exp_done")
        self.mask_ready = sem("mask_ready")
        self.count_mm = sem("counts_made")
        self.send_ready = sem("send_ready")
        self.idx_ready = sem("indices_ready")
        self.twice = sem("last_features_doubled")
        self.sent = sem("sent")

    def constants(self, pool):
        n = [0]

        def mark(ins):
            n[0] += 1
            ins.then_inc(self.consts, 1)

        mark(pool.memset(self.before[:], 1.0))
        mark(pool.memset(self.ones[:], 1.0))
        mark(pool.memset(self.far[:], FAR))
        mark(pool.iota(self.whichi[:], pattern=[[0, TPG], [1, E]], base=0, channel_multiplier=0))
        pool.wait_ge(self.consts, n[0])
        mark(pool.memset(self.ring[:], float(ROWS)))
        for s in self.scan:
            mark(pool.memset(s[:, 0:9, :], 0.0))
        pool.wait_ge(self.consts, n[0])
        mark(pool.affine_select(out=self.before[:], in_=self.before[:], compare_op=ALU.is_gt, fill=0.0, base=0,
                                pattern=[[1, 128]], channel_multiplier=-1))
        oddfar = self.far[:].rearrange("p k (s o) -> p k s o", o=2)[:, :, :, 1]
        mark(pool.affine_select(out=oddfar, in_=oddfar, compare_op=ALU.is_gt, fill=2 * FAR, base=127,
                                pattern=[[0, 2], [0, SPG]], channel_multiplier=-1))
        mark(pool.tensor_copy(self.which[:].rearrange("p t e -> p (t e)"), self.whichi[:]))
        pool.wait_ge(self.consts, n[0])
        oddwhich = self.which[:].rearrange("p (s o) e -> p s o e", o=2)[:, :, 1, :]
        mark(pool.affine_select(out=oddwhich, in_=oddwhich, compare_op=ALU.is_gt, fill=100.0, base=127,
                                pattern=[[0, SPG], [0, E]], channel_multiplier=-1))
        assert n[0] == NCONSTS

    def load_send(self, sp, g, passed):
        if not (isinstance(g, int) and g == 0):
            sp.wait_ge(self.sent, g * 256)
        settle(sp, passed)
        sp.dma_start(self.send[:, :, 0:D], self.h2_dram[bass.ds(g * SPG, SPG)].rearrange("s k p d -> p (s k) d")) \
            .then_inc(self.send_in, 16)

    def exponentials(self, act, g):
        act.wait_ge(self.route, g * STEPS + 3)
        act.activation(self.expo[:], self.expo[:], ACT.Exp).then_inc(self.exp_done, 1)

    def count(self, pe, g, bank):
        pe.wait_ge(self.mask_ready, g + 1)
        m = self.mask[:].rearrange("p k t e -> p (k t e)")
        pe.matmul(bank[:, 0, 0:128], self.before[:], m, start=True, stop=True)
        pe.matmul(bank[:, 1, 0:128], self.ones[:], m, start=True, stop=True).then_inc(self.count_mm, 1)

    def double(self, pool, g, passed):
        pool.wait_ge(self.send_ready, g + 1)
        settle(pool, passed)
        pool.tensor_copy(self.send[:, :, D:DW], self.send[:, :, 128:D]).then_inc(self.twice, 1)
        pool.wait_ge(self.twice, g + 1)
        pool.wait_ge(self.idx_ready, g + 1)

    def dispatch(self, pool, tiles):
        for t in tiles:
            for k in range(2):
                i = k * TPG + t
                pool.indirect_dma_start(self.xs_dram, bass.IndirectOffsetOnAxis(ap=self.send_idx[:, i:i + 1], axis=0),
                                        self.send[:, t, :], None, bounds_check=2 * ROWS - 1, oob_is_err=False) \
                    .then_inc(self.sent, 16)

    @staticmethod
    def spread(ap, n):
        return ap.unsqueeze(len(ap.shape)).to_broadcast(list(ap.shape) + [n])

    def step(self, dve, g, i, ins, go_on=False):
        ins.then_inc(self.route, 1)
        if not go_on:
            dve.wait_ge(self.route, g * STEPS + i)

    def logits(self, dve, g):
        self.step(dve, g, 1, dve.tensor_copy(self.rt[:].rearrange("p t r -> p (t r)"), self.routes[:, bass.ds(g * 80, 80)]))
        self.step(dve, g, 2, dve.tensor_reduce(self.tokmax[:], self.rt[:, :, 0:E], AX.X, ALU.max))
        self.step(dve, g, 3, dve.tensor_tensor(self.expo[:], self.rt[:, :, 0:E], self.spread(self.tokmax[:], E), ALU.subtract), True)

    def normed(self, dve, g, tiles):
        dve.wait_ge(self.route, g * STEPS + 1)
        dve.wait_ge(self.send_in, (g + 1) * 16)
        for t in tiles:
            ins = dve.tensor_scalar(self.send[:, t, 0:D], self.send[:, t, 0:D], self.rt[:, t, E:E + 1], self.rt[:, t, E + 1:E + 2],
                                    ALU.mult, ALU.add)
        return ins

    def choice(self, dve, g, passed):
        dve.wait_ge(self.exp_done, g + 1)
        self.step(dve, g, 4, dve.tensor_reduce(self.toksum[:], self.expo[:], AX.X, ALU.add))
        self.step(dve, g, 5, dve.reciprocal(self.toksum[:], self.toksum[:]), True)
        for t in range(TPG):
            ins = dve.max(self.top[:, t, :], self.expo[:, t, :])
        self.step(dve, g, 6, ins)
        settle(dve, passed)
        for t in range(TPG):
            ins = dve.max_index(self.topi[:, t, :], self.top[:, t, :], self.expo[:, t, :])
        self.step(dve, g, 7, ins)
        for k in range(2):
            dve.tensor_tensor(self.gate[:, k, :], self.top[:, :, k], self.toksum[:], ALU.mult)
        self.step(dve, g, 8, dve.tensor_copy(self.chosen[:].rearrange("p k t -> p t k"), self.topi[:, :, 0:2]))
        for k in range(2):
            ins = dve.tensor_tensor(self.mask[:, k, :, :], self.which[:], self.spread(self.chosen[:, k, :], E), ALU.is_equal)
        ins.then_inc(self.mask_ready, 1)

    def counts(self, dve, g, bank):
        dve.wait_ge(self.count_mm, g + 1)
        before, tot = (bank[:, i, 0:128].rearrange("p (b e) -> p b e", e=E) for i in range(2))
        dve.tensor_copy(self.pos[:], before)
        self.step(dve, g, 9, dve.tensor_copy(self.scan[0][:, 9:24, :], tot[:, 0:15, :]))

    def slots(self, dve, g):
        for i, d in enumerate((1, 2, 4, 8)):
            src, dst = self.scan[i % 2], self.scan[1 - i % 2]
            self.step(dve, g, 10 + i, dve.tensor_tensor(dst[:, 8:24, :], src[:, 8:24, :], src[:, 8 - d:24 - d, :], ALU.add))
        self.step(dve, g, 14, dve.tensor_tensor(self.pos[:], self.pos[:], self.scan[0][:, 8:24, :], ALU.add))
        m = self.mask[:].rearrange("p k t e -> p (k t) e")
        self.step(dve, g, 15, dve.tensor_tensor(self.pos[:], self.pos[:], m, ALU.mult))
        self.step(dve, g, 16, dve.tensor_reduce(self.sel[:], self.pos[:], AX.X, ALU.add))
        self.step(dve, g, 17, dve.tensor_scalar(self.ok[:], self.sel[:], float(C), None, ALU.is_lt), True)
        self.step(dve, g, 18, dve.scalar_tensor_tensor(self.slot[:], self.chosen[:].rearrange("p k t -> p (k t)"), float(SLOTS),
                                             self.sel[:], ALU.mult, ALU.add), True)
        self.step(dve, g, 19, dve.tensor_scalar(self.ring[:], self.ring[:], -1.0, float(ROWS), ALU.mult, ALU.add))
        self.step(dve, g, 20, dve.tensor_tensor(self.slot[:], self.slot[:], self.ok[:], ALU.mult), True)
        self.step(dve, g, 21, dve.scalar_tensor_tensor(self.miss[:], self.ok[:], -FAR, self.far[:].rearrange("p k t -> p (k t)"),
                                             ALU.mult, ALU.add))
        if not (isinstance(g, int) and g == 0):
            dve.wait_ge(self.sent, g * 256)
        dve.tensor_scalar(self.ret_new[:, 0, :], self.slot[:], self.ring[:, 0:1], None, ALU.add)
        dve.tensor_tensor(self.ret_new[:, 1, :].bitcast(F32), self.gate[:].rearrange("p k t -> p (k t)"), self.ok[:],
                          ALU.mult).then_inc(self.route, 1)
        dve.scalar_tensor_tensor(self.send_idx[:], self.slot[:], self.ring[:, 0:1], self.miss[:], ALU.add, ALU.add) \
            .then_inc(self.idx_ready, 1)


def experts(nc, ctx, ident, r, w, ys_dram, out):
    def sb(name, shape, dt=F32):
        return ctx.enter_context(nc.sbuf_tensor(name, shape, dt))

    def psum(name, shape):
        return ctx.enter_context(nc.psum_tensor(name, shape, F32))

    def sem(name):
        return ctx.enter_context(nc.semaphore(name))

    xrow = sb("xrow", [CPP, 2, J, DW])
    xmain = [sb(f"xmain_{p}", [128, C], F32R) for p in ("hi", "lo")]
    xrest = [sb(f"xrest_{p}", [128, C], F32R) for p in ("hi", "lo")]
    hid = [sb(f"hid_{p}", [128, FT, C], F32R) for p in ("hi", "lo")]
    yrow = sb("yrow", [CPP, 2, J, D])
    ret_mid = sb("ret_mid", [128, 2, 16], I32)
    ret_use = sb("ret_use", [128, 2, 16], I32)
    back = w.area[:, 0:TPG * D].rearrange("p (t d) -> p t d", t=TPG)
    got = w.area[:, TPG * D:16 * D].rearrange("p (r k d) -> p r k d", r=4, k=2)
    ps_x = psum("ps_xT", [128, 2, 512])
    ps_h = psum("ps_hid", [128, 3, 512])
    ps_y = psum("ps_y", [128, J, 512])
    ps_r = ps_x[:, :, C:C + 128]
    yrow_set = sem("yrow_set")
    x_in = [sem(f"xrow_in_{i}") for i in range(2)]
    x_tr = sem("x_transposed")
    x_hi = sem("xT_hi_ready")
    x_lo = sem("xT_lo_ready")
    h_mm = sem("hidden_made")
    h_hi = sem("hidden_hi_ready")
    h_lo = sem("hidden_lo_ready")
    y_mm = sem("y_made")
    y_half = sem("y_first_half_copied")
    y_ready = sem("y_ready")
    y_out = [sem(f"y_stored_{i}") for i in range(2)]
    use_ready = sem("return_indices_ready")
    fetched = [sem(f"fetched_{i}") for i in range(4)]
    back_in = sem("back_in")
    comb_half = sem("first_expert_added")
    comb = sem("second_expert_added")
    out_done = sem("out_stored")
    ret_moved = sem("return_indices_moved")
    dve_passed = sem("vector_passed")
    sp_passed = sem("sync_passed")
    pool_passed = sem("gpsimd_passed")
    block = ctx.enter_context(nc.Block())

    def all_groups(eng, body):
        body(0, False, True, True)
        body(1, True, True, True)
        with eng.Fori(2, G - 1) as g:
            body(g, True, True, True)
        body(G - 1, True, True, False)
        body(G, True, False, False)

    @block.sync
    def _(sp):
        def load_x(g, e):
            if e < 2:
                sp.wait_ge(r.sent, (g + 1) * 256)
            if not (isinstance(g, int) and g == 0 and e < 2):
                sp.wait_ge(x_tr, g * E + (e - 1))
            first = (g % 2) * ROWS + e * SLOTS
            settle(sp, sp_passed)
            sp.dma_start(xrow[:, e % 2, :, :].rearrange("p j d -> p (j d)"),
                         r.xs_dram[bass.ds(first, SLOTS), :].rearrange("(p j) d -> p (j d)", j=J)) \
                .then_inc(x_in[e % 2], 16)

        load_x(0, 0)
        load_x(0, 1)

        def body(g, prev, cur, nxt):
            if cur:
                load_x(g, 2)
            if nxt:
                r.load_send(sp, g + 1, sp_passed)
            if prev:
                sp.wait_ge(w.lo, 2 * E)
                sp.wait_ge(w.rest_lo, E)
                wait(sp, out_done, (g - 1) * (16 * 3 * SPG))
                settle(sp, sp_passed)
                sp.dma_start(back, r.h2_dram[bass.ds((g - 1) * SPG, SPG)].rearrange("s k p d -> p (s k) d")) \
                    .then_inc(back_in, 16)
            for e in range(E):
                if cur:
                    if isinstance(g, int) and g == 0 and e + EARLY < E:
                        w.load_wi(sp, e + EARLY)
                        w.load_wo(sp, e + EARLY)
                    if 0 < e < E - 2:
                        load_x(g, e + 2)
                    elif e and nxt:
                        load_x(g + 1, e + 2 - E)
                    sp.wait_ge(y_ready, g * E + (e + 1))
                    settle(sp, sp_passed)
                    if not (isinstance(g, int) and g < 2):
                        sp.wait_ge(comb, (g - 1) * TPG)
                    first = (g % 2) * ROWS + e * SLOTS
                    settle(sp, sp_passed)
                    sp.dma_start(ys_dram[bass.ds(first, SLOTS), :].rearrange("(p j) d -> p (j d)", j=J),
                                 yrow[:, e % 2, :, :].rearrange("p j d -> p (j d)")).then_inc(y_out[e % 2], 16)
                if prev and e in STORES:
                    for s in STORES[e]:
                        sp.wait_ge(comb, (g - 1) * TPG + (2 * s + 2))
                        settle(sp, sp_passed)
                        b = (g - 1) * SPG + s
                        sp.dma_start(out[bass.ds(b, 1), 0:128, :].rearrange("b p d -> p (b d)"), back[:, 2 * s, :]) \
                            .then_inc(out_done, 16)
                        for lo, hi in ((0, 112), (112, 127)):
                            sp.dma_start(out[bass.ds(b, 1), 128 + lo:128 + hi, :].rearrange("b p d -> p (b d)"),
                                         back[lo:hi, 2 * s + 1, :]).then_inc(out_done, 16)

        all_groups(sp, body)
        sp.wait_ge(out_done, G * 16 * 3 * SPG)

    @block.gpsimd
    def _(pool):
        def fetch(g, t):
            if t == 0:
                pool.wait_ge(use_ready, g + 1)
                for i in range(2):
                    pool.wait_ge(y_out[i], (g + 1) * (16 * E // 2))
                pool.wait_ge(w.lo, 2 * E)
                pool.wait_ge(w.rest_lo, E)
            if t >= 4 or not (isinstance(g, int) and g == 0):
                pool.wait_ge(comb, g * TPG + (t - 3))
            settle(pool, pool_passed)
            for k in range(2):
                i = k * TPG + t
                pool.indirect_dma_start(got[:, t % 4, k, :], None, ys_dram,
                                        bass.IndirectOffsetOnAxis(ap=ret_use[:, 0, i:i + 1], axis=0),
                                        bounds_check=2 * ROWS - 1, oob_is_err=False).then_inc(fetched[t % 4], 16)

        pool.memset(yrow[:], 0.0).then_inc(yrow_set, 1)

        def body(g, prev, cur, nxt):
            if prev:
                for t in range(4):
                    fetch(g - 1, t)
            if isinstance(g, int) and g == 0:
                for e in range(EARLY, E):
                    w.low_wi(pool, e)
                    w.low_wo(pool, e)
            if nxt:
                r.double(pool, g + 1, pool_passed)
                if not (isinstance(g, int) and g == 0):
                    for i in range(2):
                        pool.wait_ge(x_in[i], g * (16 * E // 2))
                settle(pool, pool_passed)
                r.dispatch(pool, range(TPG))
            if prev:
                for t in range(4, 8):
                    fetch(g - 1, t)

        all_groups(pool, body)

    @block.scalar
    def _(act):
        def high_x(g, e):
            act.wait_ge(x_tr, g * E + (e + 1))
            act.activation(xmain[0][:], ps_x[:, 0, 0:C], ACT.Copy)
            act.activation(xrest[0][:], ps_x[:, 1, 0:C], ACT.Copy).then_inc(x_hi, 1)

        act.wait_ge(yrow_set, 1)
        high_x(0, 0)

        def body(g, prev, cur, nxt):
            for e in range(E):
                if cur:
                    wait(act, y_mm, g * (2 * E) + 2 * e)
                    for f in range(FT):
                        act.wait_ge(h_mm, g * (FT * E) + (FT * e + f + 1))
                        act.activation(hid[0][:, f, :], ps_h[:, f % 3, 0:C], ACT.Relu).then_inc(h_hi, 1)
                    if e + 1 < E:
                        high_x(g, e + 1)
                    elif nxt:
                        high_x(g + 1, 0)
                    if isinstance(g, int) and g == 0 and e + EARLY < E:
                        w.high_wi(act, e + EARLY)
                        w.high_wo(act, e + EARLY)
                if cur:
                    if not (isinstance(g, int) and g == 0 and e < 2):
                        act.wait_ge(y_out[e % 2], g * (16 * E // 2) + 16 * (e // 2))
                    for n, tiles in enumerate((slice(0, 2), slice(2, 3))):
                        act.wait_ge(y_mm, g * (2 * E) + (2 * e + 1 + n))
                        act.activation(yrow[0:CP, e % 2, tiles, :], ps_y[0:CP, tiles, 0:D], ACT.Copy).then_inc(y_half, 1)
                if nxt and e == 0:
                    r.exponentials(act, g + 1)

        all_groups(act, body)

    @block.vector
    def _(dve):
        def low_x(g, e):
            dve.wait_ge(x_hi, g * E + (e + 1))
            dve.tensor_tensor(xmain[1][:], ps_x[:, 0, 0:C], xmain[0][:].bitcast(F32), ALU.subtract)
            dve.tensor_tensor(xrest[1][:], ps_x[:, 1, 0:C], xrest[0][:].bitcast(F32), ALU.subtract).then_inc(x_lo, 1)

        def add_expert(g, t):
            if t == 0:
                dve.wait_ge(back_in, (g + 1) * 16)
                dve.wait_ge(use_ready, g + 1)
            dve.wait_ge(fetched[t % 4], g * 64 + (32 * (t // 4) + 32))
            for k, done in ((0, comb_half), (1, comb)):
                i = k * TPG + t
                dve.scalar_tensor_tensor(back[:, t, :], got[:, t % 4, k, :], ret_use[:, 1, i:i + 1].bitcast(F32),
                                         back[:, t, :], ALU.mult, ALU.add).then_inc(done, 1)
                dve.wait_ge(done, g * TPG + (t + 1))

        def keep_return(g):
            dve.wait_ge(r.route, (g + 1) * STEPS)
            dve.tensor_copy(ret_mid[:], r.ret_new[:]).then_inc(ret_moved, 1)
            dve.wait_ge(ret_moved, g + 1)

        keep_return(0)
        dve.wait_ge(yrow_set, 1)
        low_x(0, 0)

        def body(g, prev, cur, nxt):
            for e in range(E):
                if cur:
                    for f in range(FT):
                        dve.wait_ge(h_hi, g * (FT * E) + (FT * e + f + 1))
                        dve.scalar_tensor_tensor(hid[1][:, f, :], ps_h[:, f % 3, 0:C], 0.0,
                                                 hid[0][:, f, :].bitcast(F32), ALU.max, ALU.subtract).then_inc(h_lo, 1)
                    if e + 1 < E:
                        low_x(g, e + 1)
                    elif nxt:
                        low_x(g + 1, 0)
                if nxt:
                    if e == 0:
                        r.logits(dve, g + 1)
                    if e == 1:
                        r.choice(dve, g + 1, dve_passed)
                    if e == 2:
                        r.counts(dve, g + 1, ps_r)
                        r.normed(dve, g + 1, range(TPG)).then_inc(r.send_ready, 1)
                    if e == 3:
                        r.slots(dve, g + 1)
                if prev:
                    for t in ADDS[e]:
                        add_expert(g - 1, t)
                if e == E - 1:
                    if cur:
                        dve.tensor_copy(ret_use[:], ret_mid[:]).then_inc(use_ready, 1)
                        dve.wait_ge(use_ready, g + 1)
                    if nxt:
                        keep_return(g + 1)
                if cur:
                    for n, tiles in enumerate((slice(0, 2), slice(2, 3))):
                        dve.wait_ge(y_half, g * (2 * E) + (2 * e + 1 + n))
                        half = yrow[0:CP, e % 2, tiles, :]
                        ins = dve.tensor_tensor(half, ps_y[0:CP, tiles, D:2 * D], half, ALU.add)
                    ins.then_inc(y_ready, 1)
                    if isinstance(g, int) and g == 0 and e + EARLY < E:
                        w.low_rest(dve, e + EARLY)

        all_groups(dve, body)

    @block.tensor
    def _(pe):
        PASSES = ((0, 0), (0, 1), (1, 0))

        def transpose_x(g, e, group_counted=None):
            pe.wait_ge(x_in[e % 2], g * (16 * E // 2) + 16 * (e // 2 + 1))
            if not (isinstance(g, int) and g == 0 and e == 0):
                pe.wait_ge(x_lo, g * E + e)
            if group_counted is not None:
                r.count(pe, group_counted, ps_r)
            for j in range(J):
                for part in range(2):
                    ins = pe.transpose(ps_x[:, part, j * CP:(j + 1) * CP],
                                       xrow[0:CP, e % 2, j, part * 128:(part + 1) * 128], ident[0:CP, 0:CP])
            ins.then_inc(x_tr, 1)

        transpose_x(0, 0)

        def body(g, prev, cur, nxt):
            if not cur:
                return
            for e in range(E):
                first = isinstance(g, int) and g == 0
                pe.wait_ge(x_lo, g * E + (e + 1))
                if first:
                    pe.wait_ge(w.lo, 2 * e + 2)
                    pe.wait_ge(w.rest_lo, e + 1)
                for f in range(FT):
                    if not (first and e == 0 and f < 3):
                        pe.wait_ge(h_lo, g * (FT * E) + (FT * e + f - 2))
                    cols = slice(f * 128, (f + 1) * 128)
                    rest = w.wi_rest[e][:, cols]
                    terms = [(w.wi_main[e][a][:, cols], xmain[b]) for a, b in PASSES] + [(rest, part) for part in xrest]
                    for n, (ww, xx) in enumerate(terms):
                        ins = pe.matmul(ps_h[:, f % 3, 0:C], ww, xx[:], start=(n == 0), stop=(n == len(terms) - 1))
                    ins.then_inc(h_mm, 1)
                if nxt and e == 3:
                    pe.wait_ge(r.route, (g + 1) * STEPS + 9)
                if e + 1 < E:
                    transpose_x(g, e + 1, g + 1 if nxt and e == 2 else None)
                elif nxt:
                    transpose_x(g + 1, 0)
                if not (first and e == 0):
                    pe.wait_ge(y_ready, g * E + e)
                for j in range(J):
                    for f in range(FT):
                        if j == 0:
                            pe.wait_ge(h_lo, g * (FT * E) + (FT * e + f + 1))
                        slots_f = [part[:, f, j * CP:(j + 1) * CP] for part in hid]
                        pe.matmul(ps_y[0:CP, j, 0:2 * D], slots_f[0], w.wo[e][:, f, :, :].rearrange("p h d -> p (h d)"),
                                  start=(f == 0), stop=False)
                        ins = pe.matmul(ps_y[0:CP, j, D:2 * D], slots_f[1], w.wo[e][:, f, 0, :],
                                        start=False, stop=(f == FT - 1))
                    if j:
                        ins.then_inc(y_mm, 1)

        all_groups(pe, body)


ADDS = ((), (), (), (), (0, 1), (2, 3), (4, 5), (6, 7))
STORES = {5: (0,), 6: (1,), 7: (2, 3)}


_INS = ['x', 'L0_tok_W1', 'L0_tok_W2', 'L0_tok_b2', 'L0_attn_memory', 'L0_attn_Wq', 'L0_attn_bq', 'L0_attn_Wk',
        'L0_attn_bk', 'L0_attn_Wv', 'L0_attn_bv', 'L0_attn_Wo', 'L0_attn_bo', 'L0_ffn_w_router', 'L0_ffn_wi',
        'L0_ffn_wo']


def kernel(**inputs):
    import numpy as np
    import concourse.bacc as bacc
    from concourse.bass_utils import run_bass_kernel_spmd

    nc = bacc.Bacc("TRN2", target_bir_lowering=False, num_devices=1)
    arrays, args = {}, []
    for name in _INS:
        a = np.ascontiguousarray(inputs[name])
        arrays["in_" + name] = a
        args.append(nc.dram_tensor("in_" + name, a.shape, F32, kind="ExternalInput").ap())
    out = nc.dram_tensor("out", (B, NP, D), F32, kind="ExternalOutput").ap()
    audio_tower(nc, *args, out)
    r = run_bass_kernel_spmd(nc, [arrays], core_ids=[0])
    return r.results[0]["out"]
```
